# Optimizing a Trainium2 kernel written in Bass

```python
import numpy as np
import jax
import jax.numpy as jnp

def _softmax(x, axis=-1):
    return jax.nn.softmax(x, axis=axis)

def _gelu(x):
    return jax.nn.gelu(x, approximate=True)

def _silu(x):
    return jax.nn.silu(x)

def _sigmoid(x):
    return jax.nn.sigmoid(x)

def _layernorm(x, axis=-1, eps=1e-05):
    m = jnp.mean(x, axis=axis, keepdims=True)
    v = jnp.var(x, axis=axis, keepdims=True)
    return (x - m) / jnp.sqrt(v + eps)

def _scatter_add(tgt, idx, src, axis=0):
    return tgt.at[idx].add(src)

def _segment_sum(src, seg, n):
    return jax.ops.segment_sum(src, seg, n)
kernel_name = 'mk_macaron_d2_jaxref_r4_875d7e'

def setup_inputs(seed: int=0):
    np.random.seed(seed)
    _w = jnp.asarray

    def _L0_attn_setup():
        import jax, jax.numpy as jnp
        import numpy as np
        B, S, E, H, M = (4, 512, 256, 16, 64)
        D = E // H
        LN_EPS = 1e-06

        def softmax_kernel(x, proj):
            x = x * (1.0 / jnp.sqrt(jnp.asarray(x.shape[-1], x.dtype)))
            mapping = jnp.einsum('bhsd,md->bhsm', x, proj)
            correction = jnp.sum(x * x, axis=-1, keepdims=True) * 0.5
            scaling = 1.0 / jnp.sqrt(jnp.asarray(proj.shape[0], x.dtype))
            return scaling * jnp.exp(mapping - correction)

        def favor_forward(x, q_w, q_b, k_w, k_b, v_w, v_b, out_w, out_b, proj, gamma, beta):
            b, s, e = x.shape
            split = lambda y: y.reshape(b, s, H, D).transpose(0, 2, 1, 3)
            Q = split(x @ q_w + q_b)
            K = split(x @ k_w + k_b)
            V = split(x @ v_w + v_b)
            qp = softmax_kernel(Q, proj).transpose(2, 0, 1, 3)
            kp = softmax_kernel(K, proj).transpose(2, 0, 1, 3)
            vs = V.transpose(2, 0, 1, 3)

            def step(carry, inp):
                ksum, kv = carry
                q, k, v = inp
                ksum = ksum + k
                kv = kv + k[..., :, None] * v[..., None, :]
                num = jnp.einsum('bhmd,bhm->bhd', kv, q)
                den = jnp.einsum('bhm,bhm->bh', q, ksum)
                return ((ksum, kv), (num, den))
            init = (jnp.zeros((b, H, M), x.dtype), jnp.zeros((b, H, M, D), x.dtype))
            _, (num, den) = jax.lax.scan(step, init, (qp, kp, vs))
            attn = num / den[..., None]
            attn = attn.transpose(1, 0, 2, 3).reshape(b, s, e)
            main = attn @ out_w + out_b
            res = main + x
            mu = jnp.mean(res, axis=-1, keepdims=True)
            var = jnp.mean(jnp.square(res - mu), axis=-1, keepdims=True)
            return gamma * (res - mu) * jax.lax.rsqrt(var + LN_EPS) + beta
        key = jax.random.key(seed)
        ks = jax.random.split(key, 7)
        glorot = lambda k, sh: jax.random.uniform(k, sh, jnp.float32, -1.0, 1.0) * np.sqrt(6.0 / (sh[0] + sh[1]))
        return {'x': jax.random.normal(ks[0], (B, S, E), jnp.float32), 'q_w': glorot(ks[1], (E, E)), 'q_b': jnp.zeros((E,), jnp.float32), 'k_w': glorot(ks[2], (E, E)), 'k_b': jnp.zeros((E,), jnp.float32), 'v_w': glorot(ks[3], (E, E)), 'v_b': jnp.zeros((E,), jnp.float32), 'out_w': glorot(ks[4], (E, E)), 'out_b': jnp.zeros((E,), jnp.float32), 'proj': jax.random.normal(ks[5], (M, D), jnp.float32), 'gamma': jnp.ones((E,), jnp.float32), 'beta': jnp.zeros((E,), jnp.float32)}
    _L0_attn_in = _L0_attn_setup()

    def _L0_ffn_setup():
        import jax, jax.numpy as jnp
        import numpy as np
        D_MODEL = 256
        EXPERT_DIM = 1024
        N_EXPERTS = 8
        CAP_FACTOR = 0.5
        key = jax.random.key(seed)
        ks = jax.random.split(key, 7)
        inp = {'input': jax.random.normal(ks[0], (4, 1024, D_MODEL), dtype=jnp.float32), 'w_switch': jax.random.normal(ks[1], (D_MODEL, N_EXPERTS), dtype=jnp.float32) * 0.02, 'b_switch': jnp.zeros((N_EXPERTS,), jnp.float32), 'w1': jax.random.normal(ks[2], (N_EXPERTS, D_MODEL, EXPERT_DIM), dtype=jnp.float32) * 0.02, 'b1': jnp.zeros((N_EXPERTS, EXPERT_DIM), jnp.float32), 'w2': jax.random.normal(ks[3], (N_EXPERTS, EXPERT_DIM, D_MODEL), dtype=jnp.float32) * 0.02, 'b2': jnp.zeros((N_EXPERTS, D_MODEL), jnp.float32)}
        return inp
    _L0_ffn_in = _L0_ffn_setup()

    def _L1_attn_setup():
        import jax, jax.numpy as jnp
        import numpy as np
        NUM_HEADS = 16
        NEG = -1000000000.0

        def _split_heads(t, h):
            *lead, s, hd = t.shape
            return jnp.swapaxes(t.reshape(*lead, s, h, hd // h), -3, -2)
        key = jax.random.key(seed)
        ks = jax.random.split(key, 5)
        B, S, D = (4, 512, 256)
        scale = 1.0 / np.sqrt(D)
        return {'x': jax.random.normal(ks[0], (B, S, D), dtype=jnp.float32), 'WQ': jax.random.normal(ks[1], (D, D), dtype=jnp.float32) * scale, 'WK': jax.random.normal(ks[2], (D, D), dtype=jnp.float32) * scale, 'WV': jax.random.normal(ks[3], (D, D), dtype=jnp.float32) * scale, 'WO': jax.random.normal(ks[4], (D, D), dtype=jnp.float32) * scale}
    _L1_attn_in = _L1_attn_setup()

    def _L1_ffn_setup():
        import jax, jax.numpy as jnp
        import numpy as np
        E = 8
        K = 2
        CF = 1.25
        key = jax.random.key(seed)
        kx, kr, kg, ku, kd = jax.random.split(key, 5)
        D, F = (256, 1024)
        x = jax.random.normal(kx, (4, 512, D), dtype=jnp.float32)
        router_w = 0.02 * jax.random.normal(kr, (E, D), dtype=jnp.float32)
        wg = jax.random.normal(kg, (E, D, F), dtype=jnp.float32) / np.sqrt(D)
        wu = jax.random.normal(ku, (E, D, F), dtype=jnp.float32) / np.sqrt(D)
        wd = jax.random.normal(kd, (E, F, D), dtype=jnp.float32) / np.sqrt(F)
        return {'x': x, 'router_w': router_w, 'wg': wg, 'wu': wu, 'wd': wd}
    _L1_ffn_in = _L1_ffn_setup()
    _d = {'L0_attn_x': _L0_attn_in['x'], 'L0_attn_q_w': _L0_attn_in['q_w'], 'L0_attn_q_b': _L0_attn_in['q_b'], 'L0_attn_k_w': _L0_attn_in['k_w'], 'L0_attn_k_b': _L0_attn_in['k_b'], 'L0_attn_v_w': _L0_attn_in['v_w'], 'L0_attn_v_b': _L0_attn_in['v_b'], 'L0_attn_out_w': _L0_attn_in['out_w'], 'L0_attn_out_b': _L0_attn_in['out_b'], 'L0_attn_proj': _L0_attn_in['proj'], 'L0_attn_gamma': _L0_attn_in['gamma'], 'L0_attn_beta': _L0_attn_in['beta'], 'L0_ffn_w_switch': _L0_ffn_in['w_switch'], 'L0_ffn_b_switch': _L0_ffn_in['b_switch'], 'L0_ffn_w1': _L0_ffn_in['w1'], 'L0_ffn_b1': _L0_ffn_in['b1'], 'L0_ffn_w2': _L0_ffn_in['w2'], 'L0_ffn_b2': _L0_ffn_in['b2'], 'L1_attn_WQ': _L1_attn_in['WQ'], 'L1_attn_WK': _L1_attn_in['WK'], 'L1_attn_WV': _L1_attn_in['WV'], 'L1_attn_WO': _L1_attn_in['WO'], 'L1_ffn_router_w': _L1_ffn_in['router_w'], 'L1_ffn_wg': _L1_ffn_in['wg'], 'L1_ffn_wu': _L1_ffn_in['wu'], 'L1_ffn_wd': _L1_ffn_in['wd']}
    _x0 = _d['L0_attn_x']
    _d['L0_attn_x'] = jax.random.normal(jax.random.fold_in(jax.random.key(seed), 1), (1, 4096, 256), dtype=_x0.dtype)
    del _x0
    return _d

def reference(L0_attn_x, L0_attn_q_w, L0_attn_q_b, L0_attn_k_w, L0_attn_k_b, L0_attn_v_w, L0_attn_v_b, L0_attn_out_w, L0_attn_out_b, L0_attn_proj, L0_attn_gamma, L0_attn_beta, L0_ffn_w_switch, L0_ffn_b_switch, L0_ffn_w1, L0_ffn_b1, L0_ffn_w2, L0_ffn_b2, L1_attn_WQ, L1_attn_WK, L1_attn_WV, L1_attn_WO, L1_ffn_router_w, L1_ffn_wg, L1_ffn_wu, L1_ffn_wd):

    def _L0_attn_ref(x, q_w, q_b, k_w, k_b, v_w, v_b, out_w, out_b, proj, gamma, beta):
        import jax, jax.numpy as jnp
        import numpy as np
        B, S, E, H, M = (4, 512, 256, 16, 64)
        D = E // H
        LN_EPS = 1e-06

        def softmax_kernel(x, proj):
            x = x * (1.0 / jnp.sqrt(jnp.asarray(x.shape[-1], x.dtype)))
            mapping = jnp.einsum('bhsd,md->bhsm', x, proj)
            correction = jnp.sum(x * x, axis=-1, keepdims=True) * 0.5
            scaling = 1.0 / jnp.sqrt(jnp.asarray(proj.shape[0], x.dtype))
            return scaling * jnp.exp(mapping - correction)

        def favor_forward(x, q_w, q_b, k_w, k_b, v_w, v_b, out_w, out_b, proj, gamma, beta):
            b, s, e = x.shape
            split = lambda y: y.reshape(b, s, H, D).transpose(0, 2, 1, 3)
            Q = split(x @ q_w + q_b)
            K = split(x @ k_w + k_b)
            V = split(x @ v_w + v_b)
            qp = softmax_kernel(Q, proj).transpose(2, 0, 1, 3)
            kp = softmax_kernel(K, proj).transpose(2, 0, 1, 3)
            vs = V.transpose(2, 0, 1, 3)

            def step(carry, inp):
                ksum, kv = carry
                q, k, v = inp
                ksum = ksum + k
                kv = kv + k[..., :, None] * v[..., None, :]
                num = jnp.einsum('bhmd,bhm->bhd', kv, q)
                den = jnp.einsum('bhm,bhm->bh', q, ksum)
                return ((ksum, kv), (num, den))
            init = (jnp.zeros((b, H, M), x.dtype), jnp.zeros((b, H, M, D), x.dtype))
            _, (num, den) = jax.lax.scan(step, init, (qp, kp, vs))
            attn = num / den[..., None]
            attn = attn.transpose(1, 0, 2, 3).reshape(b, s, e)
            main = attn @ out_w + out_b
            res = main + x
            mu = jnp.mean(res, axis=-1, keepdims=True)
            var = jnp.mean(jnp.square(res - mu), axis=-1, keepdims=True)
            return gamma * (res - mu) * jax.lax.rsqrt(var + LN_EPS) + beta
        return favor_forward(x, q_w, q_b, k_w, k_b, v_w, v_b, out_w, out_b, proj, gamma, beta)

    def _L0_ffn_ref(input, w_switch, b_switch, w1, b1, w2, b2):
        import jax, jax.numpy as jnp
        import numpy as np
        D_MODEL = 256
        EXPERT_DIM = 1024
        N_EXPERTS = 8
        CAP_FACTOR = 0.5
        B, S, D = input.shape
        T = B * S
        E = b_switch.shape[0]
        capacity = int(CAP_FACTOR * T / E)
        x = input.reshape(T, D)
        logits = x @ w_switch + b_switch
        probs = jax.nn.softmax(logits, axis=-1)
        pmax = probs.max(axis=-1)
        routes = probs.argmax(axis=-1)
        oh = (routes[:, None] == jnp.arange(E)[None, :]).astype(jnp.int32)
        pos = (jnp.cumsum(oh, axis=0) * oh).sum(-1) - 1
        keep = pos < capacity
        slot = jnp.where(keep, routes * capacity + pos, E * capacity)
        buf = jnp.zeros((E * capacity + 1, D), x.dtype).at[slot].set(x)
        buf_e = buf[:E * capacity].reshape(E, capacity, D)
        h = jax.nn.relu(jnp.einsum('ecd,edh->ech', buf_e, w1) + b1[:, None, :])
        y = jnp.einsum('ech,ehd->ecd', h, w2) + b2[:, None, :]
        y_flat = jnp.concatenate([y.reshape(E * capacity, D), jnp.zeros((1, D), x.dtype)], axis=0)
        out = jnp.where(keep[:, None], y_flat[slot], x)
        scale = pmax / jax.lax.stop_gradient(pmax)
        out = out * scale[:, None]
        return out.reshape(B, S, D)

    def _L1_attn_ref(x, WQ, WK, WV, WO):
        import jax, jax.numpy as jnp
        import numpy as np
        NUM_HEADS = 16
        NEG = -1000000000.0

        def _split_heads(t, h):
            *lead, s, hd = t.shape
            return jnp.swapaxes(t.reshape(*lead, s, h, hd // h), -3, -2)
        h = NUM_HEADS
        S = x.shape[-2]
        Q = _split_heads(x @ WQ.T, h)
        K = _split_heads(x @ WK.T, h)
        V = _split_heads(x @ WV.T, h)
        dk = Q.shape[-1]
        scores = jnp.einsum('bhqd,bhkd->bhqk', Q, K) / jnp.sqrt(jnp.float32(dk))
        causal = jnp.tril(jnp.ones((S, S), dtype=bool))
        scores = jnp.where(causal, scores, NEG)
        m = jnp.max(scores, axis=-1, keepdims=True)
        e = jnp.exp(scores - m)
        attn = e / jnp.sum(e, axis=-1, keepdims=True)
        out = jnp.einsum('bhqk,bhkd->bhqd', attn, V)
        out = jnp.swapaxes(out, -3, -2).reshape(*x.shape[:-1], -1)
        return out @ WO.T

    def _L1_ffn_ref(x, router_w, wg, wu, wd):
        import jax, jax.numpy as jnp
        import numpy as np
        E = 8
        K = 2
        CF = 1.25
        B, L, D = x.shape
        xf = x.reshape(-1, D)
        N = xf.shape[0]
        capacity = max(1, int(CF * N / E))
        logits = xf @ router_w.T
        probs = jax.nn.softmax(logits, axis=-1)
        topw, topi = jax.lax.top_k(probs, K)
        topw = topw / (topw.sum(-1, keepdims=True) + 1e-06)
        fe = topi.reshape(-1)
        fw = topw.reshape(-1)
        ft = jnp.repeat(jnp.arange(N), K)
        order = jnp.lexsort((-fw, fe))
        se, sw, st = (fe[order], fw[order], ft[order])
        counts = jax.ops.segment_sum(jnp.ones_like(se), se, num_segments=E)
        starts = jnp.cumsum(counts) - counts
        rank = jnp.arange(N * K) - starts[se]
        keep = rank < capacity
        pos = jnp.where(keep, rank, capacity)
        disp = jnp.zeros((E, capacity + 1, D), x.dtype).at[se, pos].set(xf[st])
        disp = disp[:, :capacity]
        g = jnp.einsum('ecd,edf->ecf', disp, wg)
        u = jnp.einsum('ecd,edf->ecf', disp, wu)
        eo = jnp.einsum('ecf,efd->ecd', jax.nn.silu(g) * u, wd)
        gathered = eo[se, jnp.minimum(pos, capacity - 1)]
        contrib = gathered * (sw * keep.astype(x.dtype))[:, None]
        out = jnp.zeros_like(xf).at[st].add(contrib)
        return out.reshape(B, L, D)
    x = L0_attn_x
    x = x + 0.5 * _L0_ffn_ref(_layernorm(x, axis=-1), L0_ffn_w_switch, L0_ffn_b_switch, L0_ffn_w1, L0_ffn_b1, L0_ffn_w2, L0_ffn_b2)
    x = x + _L0_attn_ref(_layernorm(x, axis=-1), L0_attn_q_w, L0_attn_q_b, L0_attn_k_w, L0_attn_k_b, L0_attn_v_w, L0_attn_v_b, L0_attn_out_w, L0_attn_out_b, L0_attn_proj, L0_attn_gamma, L0_attn_beta)
    x = x + 0.5 * _L0_ffn_ref(_layernorm(x, axis=-1), L0_ffn_w_switch, L0_ffn_b_switch, L0_ffn_w1, L0_ffn_b1, L0_ffn_w2, L0_ffn_b2)
    x = x + 0.5 * _L1_ffn_ref(_layernorm(x, axis=-1), L1_ffn_router_w, L1_ffn_wg, L1_ffn_wu, L1_ffn_wd)
    x = x + _L1_attn_ref(_layernorm(x, axis=-1), L1_attn_WQ, L1_attn_WK, L1_attn_WV, L1_attn_WO)
    x = x + 0.5 * _L1_ffn_ref(_layernorm(x, axis=-1), L1_ffn_router_w, L1_ffn_wg, L1_ffn_wu, L1_ffn_wd)
    return x

_drawn_inputs = setup_inputs


def setup_inputs(seed=0):
    import zlib

    import numpy as np

    out = dict(_drawn_inputs(seed))
    spreads = {'L0_attn_q_b': (0.0, 0.664),
     'L0_attn_k_b': (0.0, 0.8),
     'L0_attn_v_b': (0.0, 0.1),
     'L0_attn_out_b': (0.0, 0.1),
     'L0_attn_gamma': (1.0, 0.2),
     'L0_attn_beta': (0.0, 0.1),
     'L0_ffn_b_switch': (0.0, 0.1),
     'L0_ffn_b1': (0.0, 0.1),
     'L0_ffn_b2': (0.0, 0.1)}
    factors = {'L0_attn_q_w': 2.722, 'L0_attn_proj': 2.993}
    for name, (base, spread) in spreads.items():
        noise = np.random.default_rng([zlib.crc32(name.encode()), seed]).standard_normal(out[name].shape)
        drawn = base * np.exp(spread * noise) if base else spread * noise
        out[name] = jnp.asarray(drawn.astype(out[name].dtype))
    for name, factor in factors.items():
        out[name] = (out[name] * factor).astype(out[name].dtype)
    return out
```

```python
from collections import namedtuple
from contextlib import ExitStack, contextmanager

import concourse.bass as bass
from concourse import mybir

ALU = mybir.AluOpType
ACT = mybir.ActivationFunctionType
AX = mybir.AxisListType
F32 = mybir.dt.float32
BF16 = mybir.dt.bfloat16
U32 = mybir.dt.uint32
I32 = mybir.dt.int32

P = 128
T = 4096
D = 256
NT = T // P
KC = D // P
F = 1024
FC = F // P
E = 8
FETCH = 8
FAR = 65536
SWITCH_CAP = int(0.5 * T / E)
TOP2_CAP = int(1.25 * T / E)


@contextmanager
def stage(nc, name, sems):
    with ExitStack() as ctx:
        s = namedtuple("Semaphores", sems)(*(ctx.enter_context(nc.semaphore(f"{name}_{n}")) for n in sems.split()))
        with nc.Block() as block:
            yield block, s
        for one in s:
            nc.sync.sem_clear(one)
        nc.all_engine_barrier()


def pool_semaphore(m, n, increments):
    past = m.pool_past[n]
    m.pool_past[n] += 16 * increments
    return m.pool_dma[n], past


def bc(ap, shape):
    return ap.to_broadcast(shape)



class Memory:
    pass


def make_constants(nc, ctx):
    def sb(name, shape, dt):
        return ctx.enter_context(nc.sbuf_tensor(name, shape, dt))

    m = Memory()
    m.x = sb("x_stream", [P, NT, D], F32)
    m.xn = sb("x_normed", [P, NT, D], F32)
    m.ident = sb("ident", [P, P], F32)
    m.ones = sb("ones_bf", [P, P], BF16)
    m.upto = sb("upto_bf", [P, P], BF16)
    m.eidx8 = sb("eidx8", [P, E], F32)
    m.bits = sb("bit30", [P, 1], U32)
    m.pool_dma = [ctx.enter_context(nc.semaphore(f"pool_dma{n}")) for n in range(2 * NT // FETCH)]
    m.pool_past = [0] * len(m.pool_dma)
    return m


def constants_stage(nc, m, x_in):
    with stage(nc, "const", "filled made x_in") as (block, s):
        @block.gpsimd
        def _(pool):
            pool.memset(m.ident[:], 0.0).then_inc(s.filled, 1)
            pool.memset(m.ones[:], 1.0).then_inc(s.filled, 1)
            pool.memset(m.upto[:], 1.0).then_inc(s.filled, 1)
            pool.wait_ge(s.filled, 3)
            pool.affine_select(out=m.ident[:], in_=m.ident[:], compare_op=ALU.not_equal, fill=1.0, base=0,
                               pattern=[[-1, P]], channel_multiplier=1).then_inc(s.made, 1)
            pool.affine_select(out=m.upto[:], in_=m.upto[:], compare_op=ALU.is_ge, fill=0.0, base=0,
                               pattern=[[1, P]], channel_multiplier=-1).then_inc(s.made, 1)
            pool.iota(m.eidx8[:], pattern=[[1, E]], base=-E, channel_multiplier=0,
                      allow_small_or_imprecise_dtypes=True).then_inc(s.made, 1)
            pool.wait_ge(s.made, 3)

        @block.sync
        def _(sp):
            sp.dma_start(m.x[:], x_in.rearrange("b (t p) d -> (b p) t d", p=P)).then_inc(s.x_in, 16)
            sp.wait_ge(s.x_in, 16)


def store_stage(nc, m, out):
    with stage(nc, "store", "stored") as (block, s):
        @block.sync
        def _(sp):
            sp.dma_start(out.rearrange("b (t p) d -> (b p) t d", p=P), m.x[:]).then_inc(s.stored, 16)
            sp.wait_ge(s.stored, 16)



def norm_statistics(nc, dve, s, m, b, src=None, eps=1e-5):
    n = 0

    def link(ins):
        nonlocal n
        n += 1
        ins.then_inc(s.stat_step, 1)
        dve.wait_ge(s.stat_step, n)

    with dve.Fori(0, NT) as t:
        nc.vector.bn_stats(b.stats[:, t, :], (src or m.x)[:, t, :]).then_inc(s.stats, 1)
    dve.wait_ge(s.stats, NT)
    mean_e, m2_e, mean_o, m2_o = (b.stats[:, :, i] for i in (1, 2, 4, 5))
    link(nc.vector.tensor_tensor(b.mean[:], mean_e, mean_o, ALU.add))
    link(nc.vector.tensor_scalar(b.mean[:], b.mean[:], 0.5, None, ALU.mult))
    link(nc.vector.tensor_tensor(b.t0[:], mean_e, mean_o, ALU.subtract))
    link(nc.vector.tensor_tensor(b.t0[:], b.t0[:], b.t0[:], ALU.mult))
    link(nc.vector.tensor_tensor(b.t1[:], m2_e, m2_o, ALU.add))
    link(nc.vector.tensor_scalar(b.t1[:], b.t1[:], 1.0 / D, eps, ALU.mult, ALU.add))
    link(nc.vector.scalar_tensor_tensor(out=b.var[:], in0=b.t0[:], scalar=0.25, in1=b.t1[:],
                                        op0=ALU.mult, op1=ALU.add))
    link(nc.vector.reciprocal(b.t1[:], b.var[:]))
    nc.vector.nop().then_inc(s.var_ready, 1)
    dve.wait_ge(s.root_ready, 1)
    link(nc.vector.tensor_tensor(b.t0[:], b.rstd[:], b.rstd[:], ALU.mult))
    link(nc.vector.tensor_tensor(b.t0[:], b.t0[:], b.var[:], ALU.mult))
    link(nc.vector.tensor_scalar(b.t0[:], b.t0[:], -0.5, 1.5, ALU.mult, ALU.add))
    link(nc.vector.tensor_tensor(b.rstd[:], b.rstd[:], b.t0[:], ALU.mult))


RING = 8

NORM_SEMS = "stats stat_step var_ready root_ready normed transposed kept xT_ready projected"


NormBuffers = namedtuple("NormBuffers", "stats mean var rstd t0 t1 tile xT")


def norm_buffers(nc, ctx, name):
    def sb(n, shape, dt=F32):
        return ctx.enter_context(nc.sbuf_tensor(f"{name}_{n}", shape, dt))

    return NormBuffers(
        stats=sb("stats", [P, NT, 6]), mean=sb("mean", [P, NT]), var=sb("var", [P, NT]),
        rstd=sb("rstd", [P, NT]), t0=sb("t0", [P, NT]), t1=sb("t1", [P, NT]),
        tile=sb("tile", [P, RING, D]), xT=sb("xT", [P, 2, D]))


def norm_loop_dve(nc, dve, s, m, b, keeps_turned=False):
    with dve.Fori(0, NT // RING) as g:
        for j in range(RING):
            t = g * RING + j
            dve.wait_ge(s.transposed, t + 1)
            if not keeps_turned:
                dve.wait_ge(s.kept, t + 1)
            nc.vector.tensor_scalar(b.tile[:, j, :], m.x[:, t, :], b.mean[:, bass.ds(t, 1)],
                                    b.rstd[:, bass.ds(t, 1)],
                                    ALU.subtract, ALU.mult).then_inc(s.normed, 1)


def norm_loop_act(nc, act, s, b, psT, keeps_turned=False):
    act.wait_ge(s.var_ready, 1)
    nc.scalar.activation(b.rstd[:], b.t1[:], ACT.Sqrt).then_inc(s.root_ready, 1)
    with act.Fori(0, NT // RING) as g:
        for j in range(RING):
            t = g * RING + j
            act.wait_ge(s.transposed, t + 1 + RING)
            act.wait_ge(s.projected, t + 1)
            if keeps_turned:
                act.wait_ge(s.kept, t + RING - 1)
            nc.scalar.copy(b.xT[:, j % 2], psT[:, j % 2, 0:D]).then_inc(s.xT_ready, 1)


def norm_loop_pe(nc, pe, s, m, b, psT, project):
    pe.sem_inc(s.transposed, RING)
    pe.sem_inc(s.projected, 2)

    def transposes(t, j):
        pe.wait_ge(s.normed, t + 1)
        for k in range(KC):
            last = nc.tensor.transpose(psT[:, j % 2, k * P:(k + 1) * P], b.tile[:, j, k * P:(k + 1) * P],
                                       m.ident[:])
        last.then_inc(s.transposed, 1)

    def projection(t, j):
        pe.wait_ge(s.xT_ready, t + 1)
        project(t, j).then_inc(s.projected, 1)

    with pe.Fori(0, NT // RING) as g:
        for j in range(RING):
            transposes(g * RING + j, j)
            if j:
                projection(g * RING + j - 1, j - 1)
        projection(g * RING + RING - 1, RING - 1)



class Steps:

    def __init__(self, eng, sem):
        self.eng, self.sem, self.n = eng, sem, 0

    def __call__(self, ins):
        self.n += 1
        ins.then_inc(self.sem, 1)
        self.eng.wait_ge(self.sem, self.n)


def first_hot(nc, link, hot, values, top, t3, t1, eidx8):
    full = [P, NT, E]
    link(nc.vector.tensor_tensor(t3, values, bc(top.unsqueeze(2), full), ALU.is_equal))
    link(nc.vector.tensor_tensor(t3, t3, bc(eidx8.unsqueeze(1), full), ALU.mult))
    link(nc.vector.tensor_reduce(t1, t3, AX.X, ALU.min))
    link(nc.vector.tensor_tensor(hot, bc(eidx8.unsqueeze(1), full), bc(t1.unsqueeze(2), full), ALU.is_equal))


def route_stage(nc, m, w, top2):
    K = 2 if top2 else 1
    cap = TOP2_CAP if top2 else SWITCH_CAP
    name = w.name
    with ExitStack() as ctx:
        def sb(n, shape, dt=F32):
            return ctx.enter_context(nc.sbuf_tensor(f"{name}_{n}", shape, dt))

        b = norm_buffers(nc, ctx, name)
        wr = sb("wr", [P, KC, E])
        br = sb("br", [P, E])
        lg = sb("lg", [P, NT, E])
        ex = sb("ex", [P, NT, E])
        t3 = sb("t3", [P, NT, E])
        hots = [sb(f"hot{k}", [P, NT, E], BF16) for k in range(K)]
        top = [sb(f"top{k}", [P, NT]) for k in range(K)]
        r0, r1 = sb("r0", [P, NT]), sb("r1", [P, NT])
        count_in = sb("count_in", [P, NT, E], BF16)
        scanned = sb("scanned", [P, E, NT])
        restart = sb("restart", [P, E, NT])
        keep = sb("keep", [P, NT, E])
        wt = sb("wt", [P, NT, E])
        ebase = sb("ebase", [P, E])
        cur, cand, cnt = (sb(n, [P, E]) for n in ("cur", "cand", "cnt"))
        psT = ctx.enter_context(nc.psum_tensor(f"{name}_psT", [P, 2, 512], F32))
        psL = ctx.enter_context(nc.psum_tensor(f"{name}_psL", [P, NT, E], F32))
        psP = ctx.enter_context(nc.psum_tensor(f"{name}_psP", [P, NT, E], F32))
        psS = ctx.enter_context(nc.psum_tensor(f"{name}_psS", [P, NT, E], F32))
        full = [P, NT, E]
        turn = 5

        with stage(nc, name, NORM_SEMS + " w_in made step to_exp exped asked counted asked_bit "
                                         "counted_bit bit_step") as (block, s):
            def prefix(dve, link, asked):
                dve.wait_ge(s.counted, asked)
                sums = psS[:].rearrange("p t e -> p e t")
                link(nc.vector.tensor_copy(scanned[:], sums))
                link(nc.vector.tensor_tensor_scan(lg[:].rearrange("p t e -> p (t e)"),
                                                  restart[:].rearrange("p e t -> p (e t)"),
                                                  scanned[:].rearrange("p e t -> p (e t)"), 0.0,
                                                  ALU.mult, ALU.add))
                tiles = lg[:].rearrange("p t e -> p (t e)").rearrange("p (e t) -> p t e", e=E)
                link(nc.vector.tensor_tensor(t3[:], tiles, psS[:], ALU.subtract))
                link(nc.vector.tensor_tensor(t3[:], t3[:], psP[:], ALU.add))

            @block.sync
            def _(sp):
                sp.dma_start(wr[:], w.router.rearrange("(k p) e -> p k e", p=P)).then_inc(s.w_in, 16)
                if not top2:
                    sp.dma_start(br[:], w.router_b.partition_broadcast(P)).then_inc(s.w_in, 16)

            @block.gpsimd
            def _(pool):
                pool.iota(ebase[:], pattern=[[cap, E]], base=-1, channel_multiplier=0,
                          allow_small_or_imprecise_dtypes=True).then_inc(s.made, 1)
                pool.memset(restart[:], 1.0).then_inc(s.made, 1)
                pool.wait_ge(s.made, 2)
                pool.memset(restart[:, :, 0], 0.0).then_inc(s.made, 1)
                pool.sem_inc(s.kept, RING)
                with pool.Fori(0, NT // RING) as g:
                    for j in range(RING):
                        t = g * RING + j
                        pool.wait_ge(s.normed, t + 1)
                        nc.gpsimd.tensor_copy(m.xn[:, t, :], b.tile[:, j, :]).then_inc(s.kept, 1)

            @block.scalar
            def _(act):
                norm_loop_act(nc, act, s, b, psT)
                act.wait_ge(s.to_exp, 1)
                nc.scalar.activation(ex[:], ex[:], ACT.Exp).then_inc(s.exped, 1)

            @block.tensor
            def _(pe):
                pe.wait_ge(s.w_in, 16 if top2 else 32)

                def logits(t, j):
                    for k in range(KC):
                        last = nc.tensor.matmul(psL[:, t, :], b.xT[:, j % 2, k * P:(k + 1) * P], wr[:, k, :],
                                                start=(k == 0), stop=(k == KC - 1))
                    return last

                norm_loop_pe(nc, pe, s, m, b, psT, logits)

                def counts(asked):
                    pe.wait_ge(s.asked, asked)
                    nc.tensor.matmul(psP[:], m.upto[:], count_in[:], start=True, stop=True)
                    nc.tensor.matmul(psS[:], m.ones[:], count_in[:], start=True, stop=True).then_inc(s.counted, 1)

                if top2:
                    with pe.Fori(0, 31) as i:
                        pe.wait_ge(s.asked_bit, i + 1)
                        nc.tensor.matmul(psS[:], m.ones[:], count_in[:], start=True, stop=True)\
                            .then_inc(s.counted_bit, 1)
                    counts(1)
                    counts(2)
                else:
                    counts(1)

            @block.vector
            def _(dve):
                norm_statistics(nc, dve, s, m, b)
                norm_loop_dve(nc, dve, s, m, b)
                link = Steps(dve, s.step)
                dve.wait_ge(s.made, 3)
                dve.wait_ge(s.projected, 2 + NT)
                if top2:
                    link(nc.vector.tensor_copy(lg[:], psL[:]))
                else:
                    link(nc.vector.tensor_tensor(lg[:], psL[:], bc(br[:].unsqueeze(1), full), ALU.add))
                link(nc.vector.tensor_reduce(top[0][:], lg[:], AX.X, ALU.max))
                nc.vector.tensor_tensor(ex[:], lg[:], bc(top[0][:].unsqueeze(2), full), ALU.subtract)\
                    .then_inc(s.to_exp, 1)
                if not top2:
                    first_hot(nc, link, hots[0][:], lg[:], top[0][:], t3[:], r0[:], m.eidx8[:])
                    dve.wait_ge(s.exped, 1)
                    link(nc.vector.tensor_reduce(r0[:], ex[:], AX.X, ALU.add))
                    link(nc.vector.reciprocal(r0[:], r0[:]))
                    link(nc.vector.reciprocal(r1[:], r0[:]))
                    link(nc.vector.scalar_tensor_tensor(out=m.gate[0][:], in0=r0[:], scalar=0.5, in1=r1[:],
                                                        op0=ALU.mult, op1=ALU.mult))
                else:
                    dve.wait_ge(s.exped, 1)
                    link(nc.vector.tensor_reduce(r0[:], ex[:], AX.X, ALU.add))
                    link(nc.vector.reciprocal(r0[:], r0[:]))
                    link(nc.vector.tensor_tensor(ex[:], ex[:], bc(r0[:].unsqueeze(2), full), ALU.mult))
                    link(nc.vector.tensor_reduce(top[0][:], ex[:], AX.X, ALU.max))
                    first_hot(nc, link, hots[0][:], ex[:], top[0][:], t3[:], r0[:], m.eidx8[:])
                    link(nc.vector.scalar_tensor_tensor(out=ex[:], in0=hots[0][:], scalar=-2.0, in1=ex[:],
                                                        op0=ALU.mult, op1=ALU.add))
                    link(nc.vector.tensor_reduce(top[1][:], ex[:], AX.X, ALU.max))
                    first_hot(nc, link, hots[1][:], ex[:], top[1][:], t3[:], r0[:], m.eidx8[:])
                    link(nc.vector.tensor_tensor(r0[:], top[0][:], top[1][:], ALU.add))
                    link(nc.vector.tensor_scalar(r0[:], r0[:], 1e-6, None, ALU.add))
                    link(nc.vector.reciprocal(r0[:], r0[:]))
                    for k in range(2):
                        link(nc.vector.tensor_tensor(top[k][:], top[k][:], r0[:], ALU.mult))
                    link(nc.vector.tensor_tensor(wt[:], hots[0][:], bc(top[0][:].unsqueeze(2), full), ALU.mult))
                    link(nc.vector.tensor_tensor(t3[:], hots[1][:], bc(top[1][:].unsqueeze(2), full), ALU.mult))
                    link(nc.vector.tensor_tensor(wt[:], wt[:], t3[:], ALU.add))
                    link(nc.vector.tensor_tensor(t3[:], hots[0][:], hots[1][:], ALU.add))
                    link(nc.vector.scalar_tensor_tensor(out=wt[:], in0=t3[:], scalar=-1.0, in1=wt[:],
                                                        op0=ALU.add, op1=ALU.add))
                    link(nc.vector.memset(cur[:], 0.0))
                    link(nc.vector.memset(m.bits[:], float(1 << 29)))
                    with dve.Fori(0, 30) as i:
                        nc.vector.tensor_tensor(cand[:].bitcast(U32), cur[:].bitcast(U32),
                                                bc(m.bits[:], [P, E]), ALU.bitwise_or).then_inc(s.bit_step, 1)
                        dve.wait_ge(s.bit_step, i * turn + 1)
                        nc.vector.tensor_tensor(count_in[:], wt[:], bc(cand[:].unsqueeze(1), full), ALU.is_ge)\
                            .then_inc(s.asked_bit, 1)
                        nc.vector.tensor_scalar(m.bits[:], m.bits[:], 1, None, ALU.logical_shift_right)\
                            .then_inc(s.bit_step, 1)
                        dve.wait_ge(s.counted_bit, i + 1)
                        nc.vector.tensor_reduce(cnt[:], psS[:].rearrange("p t e -> p e t"), AX.X, ALU.add)\
                            .then_inc(s.bit_step, 1)
                        dve.wait_ge(s.bit_step, i * turn + 3)
                        nc.vector.scalar_tensor_tensor(out=cand[:], in0=cnt[:], scalar=float(cap), in1=cand[:],
                                                       op0=ALU.is_ge, op1=ALU.mult).then_inc(s.bit_step, 1)
                        dve.wait_ge(s.bit_step, i * turn + 4)
                        nc.vector.tensor_tensor(cur[:], cur[:], cand[:], ALU.max).then_inc(s.bit_step, 1)
                        dve.wait_ge(s.bit_step, i * turn + 5)
                    thr = bc(cur[:].unsqueeze(1), full)
                    link(nc.vector.tensor_tensor(keep[:], wt[:], thr, ALU.is_gt))
                    nc.vector.tensor_copy(count_in[:], keep[:]).then_inc(s.asked_bit, 1)
                    dve.wait_ge(s.counted_bit, 31)
                    link(nc.vector.tensor_reduce(cnt[:], psS[:].rearrange("p t e -> p e t"), AX.X, ALU.add))
                    link(nc.vector.tensor_scalar(cnt[:], cnt[:], -1.0, float(cap), ALU.mult, ALU.add))
                    link(nc.vector.tensor_tensor(wt[:], wt[:], thr, ALU.is_equal))
                    nc.vector.tensor_copy(count_in[:], wt[:]).then_inc(s.asked, 1)
                    prefix(dve, link, 1)
                    link(nc.vector.tensor_tensor(t3[:], t3[:], bc(cnt[:].unsqueeze(1), full), ALU.is_le))
                    link(nc.vector.tensor_tensor(t3[:], t3[:], wt[:], ALU.mult))
                    link(nc.vector.tensor_tensor(keep[:], keep[:], t3[:], ALU.add))
                link(nc.vector.tensor_copy(count_in[:], (keep if top2 else hots[0])[:]))
                nc.vector.nop().then_inc(s.asked, 1)
                prefix(dve, link, K)
                if not top2:
                    link(nc.vector.tensor_scalar(keep[:], t3[:], float(cap), None, ALU.is_le))
                link(nc.vector.tensor_tensor(t3[:], t3[:], bc(ebase[:].unsqueeze(1), full), ALU.add))
                for k in range(K):
                    link(nc.vector.tensor_tensor(ex[:], t3[:], hots[k][:], ALU.mult))
                    link(nc.vector.tensor_reduce(r0[:], ex[:], AX.X, ALU.add))
                    link(nc.vector.tensor_tensor(ex[:], keep[:], hots[k][:], ALU.mult))
                    link(nc.vector.tensor_reduce(r1[:], ex[:], AX.X, ALU.add))
                    if top2:
                        link(nc.vector.tensor_tensor(m.fetch[k][:], r0[:], r1[:], ALU.mult))
                        link(nc.vector.scalar_tensor_tensor(out=m.gate[k][:], in0=top[k][:], scalar=0.5,
                                                            in1=r1[:], op0=ALU.mult, op1=ALU.mult))
                    link(nc.vector.tensor_scalar(r1[:], r1[:], -float(FAR), float(FAR), ALU.mult, ALU.add))
                    link(nc.vector.tensor_tensor(m.place[k][:], r0[:], r1[:], ALU.add))



def zero_slots_stage(nc, m):
    with ExitStack() as ctx:
        zeros = ctx.enter_context(nc.sbuf_tensor("zeros", [P, 8, D], F32))
        with stage(nc, "zero", "zeroed written") as (block, s):
            @block.vector
            def _(dve):
                nc.vector.memset(zeros[:], 0.0).then_inc(s.zeroed, 1)

            @block.sync
            def _(sp):
                sp.wait_ge(s.zeroed, 1)
                rows = P * 8
                for r in range(E * TOP2_CAP // rows):
                    sp.dma_start(m.slots[r * rows:(r + 1) * rows, :].rearrange("(p a) d -> p a d", p=P),
                                 zeros[:]).then_inc(s.written, 16)
                sp.wait_ge(s.written, 16 * (E * TOP2_CAP // rows))


def dispatch_stage(nc, m, name, top2):
    K, cap = (2, TOP2_CAP) if top2 else (1, SWITCH_CAP)
    scattered, past = pool_semaphore(m, 0, NT * K)
    with stage(nc, name, "") as (block, s):
        @block.gpsimd
        def _(pool):
            for t in range(NT):
                for k in range(K):
                    pool.indirect_dma_start(
                        out=m.slots[0:E * cap, :], out_offset=bass.IndirectOffsetOnAxis(ap=m.place[k][:, t:t + 1], axis=0),
                        in_=m.xn[:, t, :], in_offset=None, bounds_check=E * cap - 1,
                        oob_is_err=False).then_inc(scattered, 16)
            pool.wait_ge(scattered, past + 16 * NT * K)


def experts_stage(nc, m, w, top2):
    cap = TOP2_CAP if top2 else SWITCH_CAP
    S = cap // P
    NP = 2 if top2 else 1
    W = cap // NP
    UP = 2 if top2 else 1
    name = w.name + "_x"
    with ExitStack() as ctx:
        def sb(n, shape, dt=F32):
            return ctx.enter_context(nc.sbuf_tensor(f"{name}_{n}", shape, dt))

        def ps(n):
            return ctx.enter_context(nc.psum_tensor(f"{name}_{n}", [P, 2, 512], F32))

        w1 = [sb(f"w1_{h}", [P, UP, KC, F]) for h in range(2)]
        w2 = [sb(f"w2_{h}", [P, FC, D]) for h in range(2)]
        a = [sb(f"a_{h}", [P, S, D]) for h in range(2)]
        aT = [sb(f"aT_{h}", [P, KC, cap]) for h in range(2)]
        hid = sb("hid", [P, FC, cap])
        yo = [sb(f"yo_{h}", [P, S, D]) for h in range(2)]
        if top2:
            sg = sb("sg", [P, 2, W])
        else:
            b1 = sb("b1", [P, E * FC])
            b1r = sb("b1r", [E * FC, P])
            b2 = sb("b2", [P, E, D])
        psT, psG, psU, psY = ps("psT"), ps("psG"), ps("psU"), ps("psY")
        slots = m.slots[0:E * cap, :].rearrange("(e s p) d -> e p s d", e=E, p=P)
        outs = m.outs[0:E * cap, :].rearrange("(e s p) d -> e p s d", e=E, p=P)
        w1_dram = [v.rearrange("e (k p) f -> e p k f", p=P) for v in w.up]
        w2_dram = w.down.rearrange("e (c p) d -> e p c d", p=P)

        def over_experts(eng, body):
            with eng.Fori(0, E // 2 - 1) as pair:
                for h in range(2):
                    body(pair * 2 + h, h, pair, False)
            for h in range(2):
                body(E - 2 + h, h, E // 2 - 1, h == 1)

        with stage(nc, name, "a_in0 a_in1 w1_in0 w1_in1 w2_in0 w2_in1 bias_in b1_turned b1_ready "
                                   "turned turned_out hidden gated done y_ready y_out yo_free") as (block, s):
            a_in, w1_in, w2_in = (s.a_in0, s.a_in1), (s.w1_in0, s.w1_in1), (s.w2_in0, s.w2_in1)
            stored = [pool_semaphore(m, h, E // 2) for h in range(2)]
            hid_done = s.done if top2 else s.gated

            @block.sync
            def _(sp):
                def loads(e, h):
                    sp.dma_start(a[h][:], slots[e]).then_inc(a_in[h], 16)
                    for u in range(UP):
                        sp.dma_start(w1[h][:, u], w1_dram[u][e]).then_inc(w1_in[h], 16)
                    sp.dma_start(w2[h][:], w2_dram[e]).then_inc(w2_in[h], 16)

                loads(0, 0)
                if not top2:
                    sp.dma_start(b1r[:], w.up_b.rearrange("e (c p) -> (e c) p", p=P)).then_inc(s.bias_in, 16)
                    sp.dma_start(b2[:], w.down_b.partition_broadcast(P)).then_inc(s.bias_in, 16)
                loads(1, 1)
                with sp.Fori(1, E // 2) as pair:
                    for h in range(2):
                        sp.wait_ge(s.y_ready, (pair * 2 + h - 1) * S)
                        loads(pair * 2 + h, h)

            @block.tensor
            def _(pe):
                def turn(e, h, pair):
                    pe.wait_ge(a_in[h], pair * 16 + 16)
                    for i in range(S):
                        n = e * S + i
                        pe.wait_ge(s.turned_out, n + 1)
                        for k in range(KC):
                            last = nc.tensor.transpose(psT[:, (h * S + i) % 2, k * P:(k + 1) * P],
                                                       a[h][:, i, k * P:(k + 1) * P], m.ident[:])
                        last.then_inc(s.turned, 1)

                def hidden(e, h, pair):
                    pe.wait_ge(s.turned_out, e * S + S + 2)
                    pe.wait_ge(w1_in[h], pair * (16 * UP) + 16 * UP)
                    for c in range(FC):
                        for q in range(NP):
                            n = (e * FC + c) * NP + q
                            slot = (c * NP + q) % 2
                            pe.wait_ge(s.gated, n + 1)
                            if top2:
                                pe.wait_ge(s.done, n + 1)
                            for u, ps_u in enumerate((psG, psU)[:UP]):
                                for k in range(KC):
                                    last = nc.tensor.matmul(ps_u[:, slot, 0:W], w1[h][:, u, k, c * P:(c + 1) * P],
                                                            aT[h][:, k, q * W:(q + 1) * W],
                                                            start=(k == 0), stop=(k == KC - 1))
                            last.then_inc(s.hidden, 1)

                def down(e, h, pair):
                    pe.wait_ge(w2_in[h], pair * 16 + 16)
                    pe.wait_ge(hid_done, e * (FC * NP) + (FC * NP + 2))
                    for i in range(S):
                        pe.wait_ge(s.y_out, e * S + i + 1)
                        for c in range(FC):
                            last = nc.tensor.matmul(psY[:, (h * S + i) % 2, 0:D], hid[:, c, i * P:(i + 1) * P],
                                                    w2[h][:, c, :], start=(c == 0), stop=(c == FC - 1))
                        last.then_inc(s.y_ready, 1)

                pe.sem_inc(s.turned_out, 2)
                pe.sem_inc(s.gated, 2)
                pe.sem_inc(s.y_out, 2)
                if top2:
                    pe.sem_inc(s.done, 2)
                else:
                    pe.wait_ge(s.bias_in, 32)
                    nc.tensor.transpose(psU[:, 0, 0:E * FC], b1r[:], m.ident[0:E * FC, 0:E * FC])\
                        .then_inc(s.b1_turned, 1)
                turn(0, 0, 0)

                def body(e, h, pair, last):
                    hidden(e, h, pair)
                    if not last:
                        turn(e + 1, 1 - h, pair + h)
                    down(e, h, pair)

                over_experts(pe, body)

            @block.scalar
            def _(act):
                def turned(e, h):
                    for i in range(S):
                        act.wait_ge(s.turned, e * S + i + 1)
                        nc.scalar.copy(aT[h][:, :, i * P:(i + 1) * P],
                                       psT[:, (h * S + i) % 2, 0:D].rearrange("p (k n) -> p k n", k=KC))\
                            .then_inc(s.turned_out, 1)

                turned(0, 0)
                if not top2:
                    act.wait_ge(s.b1_ready, 1)

                def body(e, h, pair, last):
                    for c in range(FC):
                        for q in range(NP):
                            n = (e * FC + c) * NP + q
                            slot = (c * NP + q) % 2
                            act.wait_ge(s.hidden, n + 1)
                            if top2:
                                act.wait_ge(s.done, n + 1)
                                nc.scalar.activation(sg[:, slot, :], psG[:, slot, 0:W], ACT.Silu)\
                                    .then_inc(s.gated, 1)
                            else:
                                nc.scalar.activation(hid[:, c, :], psG[:, slot, 0:W], ACT.Relu,
                                                     bias=b1[:, bass.ds(e * FC + c, 1)]).then_inc(s.gated, 1)
                    if not last:
                        turned(e + 1, 1 - h)

                over_experts(act, body)

            @block.vector
            def _(dve):
                if not top2:
                    dve.wait_ge(s.b1_turned, 1)
                    nc.vector.tensor_copy(b1[:], psU[:, 0, 0:E * FC]).then_inc(s.b1_ready, 1)

                def body(e, h, pair, last):
                    if top2:
                        for c in range(FC):
                            for q in range(NP):
                                n = (e * FC + c) * NP + q
                                slot = (c * NP + q) % 2
                                dve.wait_ge(s.gated, n + 3)
                                nc.vector.tensor_tensor(hid[:, c, q * W:(q + 1) * W], sg[:, slot, :],
                                                        psU[:, slot, 0:W], ALU.mult).then_inc(s.done, 1)
                    dve.wait_ge(s.yo_free, e + 1)
                    for i in range(S):
                        dve.wait_ge(s.y_ready, e * S + i + 1)
                        src = psY[:, (h * S + i) % 2, 0:D]
                        if top2:
                            nc.vector.tensor_copy(yo[h][:, i, :], src).then_inc(s.y_out, 1)
                        else:
                            nc.vector.tensor_tensor(yo[h][:, i, :], src, b2[:, e, :], ALU.add).then_inc(s.y_out, 1)

                over_experts(dve, body)

            @block.gpsimd
            def _(pool):
                pool.sem_inc(s.yo_free, 2)

                def body(e, h, pair, last):
                    pool.wait_ge(s.y_out, e * S + S + 2)
                    in_dram, past = stored[h]
                    pool.dma_start(outs[e], yo[h][:]).then_inc(in_dram, 16)
                    pool.wait_ge(in_dram, pair * 16 + (past + 16))
                    pool.sem_inc(s.yo_free, 1)

                over_experts(pool, body)


def combine_stage(nc, m, name, top2):
    K, cap = (2, TOP2_CAP) if top2 else (1, SWITCH_CAP)
    with ExitStack() as ctx:
        got = [m.xn, ctx.enter_context(nc.sbuf_tensor(name + "_got1", [P, NT, D], F32)) if top2 else None]
        groups = NT // FETCH
        fetched = [pool_semaphore(m, n, FETCH) for n in range(K * groups)]
        with stage(nc, name, "added") as (block, s):

            @block.gpsimd
            def _(pool):
                for t in range(NT):
                    for k in range(K):
                        where = (m.fetch if top2 else m.place)[k]
                        pool.indirect_dma_start(
                            out=got[k][:, t, :], out_offset=None, in_=m.outs[0:E * cap, :],
                            in_offset=bass.IndirectOffsetOnAxis(ap=where[:, t:t + 1], axis=0),
                            bounds_check=E * cap - 1, oob_is_err=False)\
                            .then_inc(fetched[k * groups + t // FETCH][0], 16)

            @block.vector
            def _(dve):
                for g in range(NT // FETCH):
                    for k in range(K):
                        got_in, past = fetched[k * groups + g]
                        dve.wait_ge(got_in, past + 16 * FETCH)
                        if k:
                            dve.wait_ge(s.added, (g * K + k) * FETCH)
                        with dve.Fori(g * FETCH, g * FETCH + FETCH) as t:
                            nc.vector.scalar_tensor_tensor(
                                out=m.x[:, t, :], in0=got[k][:, t, :], scalar=m.gate[k][:, bass.ds(t, 1)],
                                in1=m.x[:, t, :], op0=ALU.mult, op1=ALU.add).then_inc(s.added, 1)


def ffn(nc, m, w, top2):
    K = 2 if top2 else 1
    with ExitStack() as ctx:
        m.place = [ctx.enter_context(nc.sbuf_tensor(f"{w.name}_place{k}", [P, NT], U32)) for k in range(K)]
        m.fetch = [ctx.enter_context(nc.sbuf_tensor(f"{w.name}_fetch{k}", [P, NT], U32)) for k in range(K)]
        m.gate = [ctx.enter_context(nc.sbuf_tensor(f"{w.name}_gate{k}", [P, NT], F32)) for k in range(K)]
        route_stage(nc, m, w, top2)
        dispatch_stage(nc, m, w.name + "_dispatch", top2)
        experts_stage(nc, m, w, top2)
        combine_stage(nc, m, w.name + "_combine", top2)



QB = 512
NB = T // QB
TB = QB // P
H = 16
DH = D // H
EVEN = 8


def norm_and_values_stage(nc, m, name, wv_dram, values, bias_dram=None, stats=None):
    xnT = turned_view(m)
    with ExitStack() as ctx:
        def sb(n, shape, dt=F32):
            return ctx.enter_context(nc.sbuf_tensor(f"{name}_{n}", shape, dt))

        b = norm_buffers(nc, ctx, name)
        if stats is not None:
            b = b._replace(mean=stats[0], rstd=stats[1])
        wv = sb("wv", [P, KC, D])
        bv = sb("bv", [P, D])
        psT = ctx.enter_context(nc.psum_tensor(f"{name}_psT", [P, 2, 512], F32))
        psV = ctx.enter_context(nc.psum_tensor(f"{name}_psV", [P, 2, 512], F32))
        with stage(nc, name, NORM_SEMS + " w_in v_done ones_made") as (block, s):
            @block.sync
            def _(sp):
                sp.dma_start(wv[:], wv_dram.rearrange("(k p) n -> p k n", p=P)).then_inc(s.w_in, 16)
                if bias_dram is not None:
                    sp.dma_start(bv[:], bias_dram.partition_broadcast(P)).then_inc(s.w_in, 16)

            @block.gpsimd
            def _(pool):
                if values.shape[3] > DH:
                    pool.memset(values[:, :, :, DH:], 1.0).then_inc(s.ones_made, 1)
                pool.sem_inc(s.kept, RING)
                with pool.Fori(0, NT // RING) as g:
                    for j in range(RING):
                        t = g * RING + j
                        pool.wait_ge(s.xT_ready, t + 1)
                        nc.gpsimd.tensor_copy(xnT[:, :, bass.ds(t * P, P)],
                                              b.xT[:, j % 2].rearrange("p (k n) -> p k n", k=KC))\
                            .then_inc(s.kept, 1)

            @block.scalar
            def _(act):
                norm_loop_act(nc, act, s, b, psT, keeps_turned=True)

            @block.tensor
            def _(pe):
                pe.wait_ge(s.w_in, 16 if bias_dram is None else 32)
                pe.sem_inc(s.v_done, 2)

                def v(t, j):
                    pe.wait_ge(s.v_done, t + 1)
                    for k in range(KC):
                        last = nc.tensor.matmul(psV[:, j % 2, 0:D], b.xT[:, j % 2, k * P:(k + 1) * P], wv[:, k, :],
                                                start=(k == 0), stop=(k == KC - 1))
                    return last

                norm_loop_pe(nc, pe, s, m, b, psT, v)

            @block.vector
            def _(dve):
                norm_statistics(nc, dve, s, m, b)
                norm_loop_dve_values(nc, dve, s, m, b, psV, values, bv if bias_dram is not None else None)


def norm_loop_dve_values(nc, dve, s, m, b, psV, values, bv):
    def normed(t, j):
        dve.wait_ge(s.transposed, t + 1)
        nc.vector.tensor_scalar(b.tile[:, j, :], m.x[:, t, :], b.mean[:, bass.ds(t, 1)],
                                b.rstd[:, bass.ds(t, 1)], ALU.subtract, ALU.mult).then_inc(s.normed, 1)

    def value(t, j):
        dve.wait_ge(s.projected, t + 3)
        out = values[:, t, :, 0:DH]
        src = psV[:, j % 2, 0:D].rearrange("p (h d) -> p h d", h=H)
        if bv is None:
            nc.vector.tensor_copy(out, src).then_inc(s.v_done, 1)
        else:
            nc.vector.tensor_tensor(out, src, bv[:].rearrange("p (h d) -> p h d", h=H), ALU.add)\
                .then_inc(s.v_done, 1)

    with dve.Fori(0, NT // RING) as g:
        for j in range(RING):
            normed(g * RING + j, j)
        for j in range(RING):
            value(g * RING + j, j)


def turned_view(m):
    return m.xn[:].rearrange("p t d -> p (t d)").rearrange("p (k n) -> p k n", k=KC)



Q_PART = (0, 0, 0, 1, 1, 2)
K_PART = (0, 1, 2, 0, 1, 0)
STACK = len(Q_PART) * DH
G = 4
NG = H // G
LN8 = 2.0794415416798357
FAR_BELOW = -1e30


def runs(parts):
    found, r = [], 0
    while r < len(parts):
        n = 1
        while r + n < len(parts) and parts[r + n] == parts[r] + n:
            n += 1
        found.append((r, parts[r], n))
        r += n
    return found


def load_stack(sp, m, which, heads, parts, cols, out, sem):
    for r, part, n in runs(parts):
        sp.dma_start(out[r * DH:(r + n) * DH],
                     m.stacks[which, heads, part * DH:(part + n) * DH, cols]
                     .rearrange("h r n -> r h n")).then_inc(sem, 16)


def stack_loads(parts):
    return 16 * len(runs(parts))


def split_stage(nc, m, name, w, bias=None):
    xnT = turned_view(m)
    favor_kind = bias is not None
    with ExitStack() as ctx:
        def sb(n, shape, dt=F32):
            return ctx.enter_context(nc.sbuf_tensor(f"{name}_{n}", shape, dt))

        wqk = [sb(f"w{i}", [P, KC, D]) for i in range(2)]
        PR = 4
        parts = sb("parts", [P, PR, 3, QB], BF16)
        rest = sb("rest", [P, 2, QB])
        ps = ctx.enter_context(nc.psum_tensor(f"{name}_ps", [P, 2, QB], F32))
        tasks = [(i, c) for i in range(2) for c in range(KC)]
        n_tasks = len(tasks)
        if favor_kind:
            b = sb("b", [P, 2, KC])
            val, sq = sb("val", [P, 2, QB]), sb("sq", [P, 2, QB])
            halves = sb("halves", [P, 32])
            norm, norm_rest = sb("norm", [P, QB]), sb("norm_rest", [P, QB])
            norm_parts = sb("norm_parts", [P, 3, QB], BF16)
            psC = ctx.enter_context(nc.psum_tensor(f"{name}_psC", [P, QB], F32))
        with stage(nc, name, "w_in ready taken high rest1 mid low put0 put1 put2 put3 part_free filled made squared summed "
                             "sum_taken sum_step sums_ready sums_put") as (block, s):
            put = (s.put0, s.put1, s.put2, s.put3)

            @block.sync
            def _(sp):
                for i in range(2):
                    sp.dma_start(wqk[i][:], w[i].rearrange("(k p) n -> p k n", p=P)).then_inc(s.w_in, 16)
                    if favor_kind:
                        sp.dma_start(b[:, i, :], bias[i].rearrange("(k p) -> p k", p=P),
                                     allow_slow_non_contiguous=True).then_inc(s.w_in, 16)
                with sp.Fori(0, NB) as blk:
                    cols = bass.ds(blk * QB, QB)
                    for j, (i, c) in enumerate(tasks):
                        sp.wait_ge(s.low, blk * n_tasks + (j + 1))
                        rows = m.stacks[i, c * EVEN:(c + 1) * EVEN]
                        for part in range(3):
                            sp.dma_start(rows[:, part * DH:(part + 1) * DH, cols],
                                         parts[:, j, part, :]).then_inc(put[j], 16)
                    if favor_kind:
                        sp.wait_ge(s.sums_ready, blk + 1)
                        for j, (i, c) in enumerate(tasks):
                            for part in range(3):
                                sp.dma_start(m.stacks[i, c * EVEN:(c + 1) * EVEN, 3 * DH + part, cols],
                                             norm_parts[32 * j:32 * j + EVEN, part, :]).then_inc(s.sums_put, 16)
                for one in put:
                    sp.wait_ge(one, 48 * NB)
                if favor_kind:
                    sp.wait_ge(s.sums_put, 48 * n_tasks * NB)

            if favor_kind:
                @block.gpsimd
                def _(pool):
                    pool.memset(halves[:], 0.5).then_inc(s.filled, 1)
                    pool.wait_ge(s.filled, 1)
                    pool.affine_select(out=halves[:], in_=halves[:], compare_op=ALU.is_ge, fill=0.0, base=0,
                                       pattern=[[-DH, 32]], channel_multiplier=1).then_inc(s.filled, 1)
                    pool.wait_ge(s.filled, 2)
                    pool.affine_select(out=halves[:], in_=halves[:], compare_op=ALU.is_ge, fill=0.0, base=DH - 1,
                                       pattern=[[DH, 32]], channel_multiplier=-1).then_inc(s.made, 1)

            @block.tensor
            def _(pe):
                pe.wait_ge(s.w_in, 64 if favor_kind else 32)
                pe.sem_inc(s.taken, 2)
                if favor_kind:
                    pe.wait_ge(s.made, 1)
                    pe.sem_inc(s.summed, 2)
                    pe.sem_inc(s.sum_taken, 1)

                def square_sums(blk, j):
                    pe.wait_ge(s.squared, blk * n_tasks + (j + 1))
                    if j == 0:
                        pe.wait_ge(s.sum_taken, blk + 1)
                    nc.tensor.matmul(psC[32 * j:32 * j + 32, :], halves[:], sq[:, j % 2, :],
                                     start=True, stop=True).then_inc(s.summed, 1)

                with pe.Fori(0, NB) as blk:
                    for j, (i, c) in enumerate(tasks):
                        pe.wait_ge(s.taken, blk * n_tasks + (j + 1))
                        for k in range(KC):
                            last = nc.tensor.matmul(ps[:, j % 2, :], wqk[i][:, k, c * P:(c + 1) * P],
                                                    xnT[:, k, bass.ds(blk * QB, QB)],
                                                    start=(k == 0), stop=(k == KC - 1))
                        last.then_inc(s.ready, 1)
                        if favor_kind and j:
                            square_sums(blk, j - 1)
                    if favor_kind:
                        square_sums(blk, n_tasks - 1)

            @block.scalar
            def _(act):
                def block_parts(blk, first):
                    for j in range(n_tasks):
                        n = blk * n_tasks + j
                        if not first:
                            act.wait_ge(put[j], blk * 48)
                        if favor_kind:
                            act.wait_ge(s.taken, n + 3)
                            nc.scalar.copy(parts[:, j, 0, :], val[:, j % 2, :]).then_inc(s.high, 1)
                            act.wait_ge(s.summed, n + 1)
                            nc.scalar.activation(sq[:, j % 2, :], val[:, j % 2, :], ACT.Square,
                                                 scale=DH ** -0.5).then_inc(s.squared, 1)
                        else:
                            act.wait_ge(s.ready, n + 1)
                            nc.scalar.copy(parts[:, j, 0, :], ps[:, j % 2, :]).then_inc(s.high, 1)
                        act.wait_ge(s.rest1, n + 1)
                        nc.scalar.copy(parts[:, j, 1, :], rest[:, j % 2, :]).then_inc(s.mid, 1)

                block_parts(0, True)
                with act.Fori(1, NB) as blk:
                    block_parts(blk, False)

            @block.vector
            def _(dve):
                if favor_kind:
                    dve.wait_ge(s.w_in, 64)

                def block_parts(blk, first):
                    for j, (i, c) in enumerate(tasks):
                        n = blk * n_tasks + j
                        if favor_kind:
                            dve.wait_ge(s.ready, n + 1)
                            nc.vector.tensor_scalar(val[:, j % 2, :], ps[:, j % 2, :], b[:, i, c:c + 1], None,
                                                    ALU.add).then_inc(s.taken, 1)
                            dve.wait_ge(s.high, n + 1)
                            nc.vector.tensor_tensor(rest[:, j % 2, :], val[:, j % 2, :], parts[:, j, 0, :],
                                                    ALU.subtract).then_inc(s.rest1, 1)
                        else:
                            dve.wait_ge(s.high, n + 1)
                            nc.vector.tensor_tensor(rest[:, j % 2, :], ps[:, j % 2, :], parts[:, j, 0, :],
                                                    ALU.subtract).then_inc(s.rest1, 1)
                        dve.wait_ge(s.mid, n + 1)
                        nc.vector.tensor_tensor(parts[:, j, 2, :], rest[:, j % 2, :], parts[:, j, 1, :],
                                                ALU.subtract).then_inc(s.low, 1)
                        if not favor_kind:
                            dve.sem_inc(s.taken, 1)
                    if favor_kind:
                        step = blk * 3
                        dve.wait_ge(s.summed, blk * n_tasks + (n_tasks + 2))
                        nc.vector.tensor_scalar(norm[:], psC[:], LN8, None, ALU.add).then_inc(s.sum_taken, 1)
                        dve.wait_ge(s.sum_taken, blk + 2)
                        if not first:
                            dve.wait_ge(s.sums_put, blk * (48 * n_tasks))
                        nc.vector.tensor_copy(norm_parts[:, 0, :], norm[:]).then_inc(s.sum_step, 1)
                        dve.wait_ge(s.sum_step, step + 1)
                        nc.vector.tensor_tensor(norm_rest[:], norm[:], norm_parts[:, 0, :], ALU.subtract)\
                            .then_inc(s.sum_step, 1)
                        dve.wait_ge(s.sum_step, step + 2)
                        nc.vector.tensor_copy(norm_parts[:, 1, :], norm_rest[:]).then_inc(s.sum_step, 1)
                        dve.wait_ge(s.sum_step, step + 3)
                        nc.vector.tensor_tensor(norm_parts[:, 2, :], norm_rest[:], norm_parts[:, 1, :],
                                                ALU.subtract).then_inc(s.sums_ready, 1)

                block_parts(0, True)
                with dve.Fori(1, NB) as blk:
                    block_parts(blk, False)


def attention_plan():
    def maxima(i):
        return [("max", i, qt, h, c) for qt in range(TB) for h in range(G) for c in range(i + 1)]

    def turns(i):
        return [("turn", i, h) for h in range(G)]

    plan = maxima(0) + [("rows", 0)] + turns(0)
    waiting = []
    for i in range(NB):
        ahead = maxima(i + 1) if i + 1 < NB else []
        kts = TB * (i + 1)
        slots = G * (kts - 1)
        done = 0
        for kt in range(kts):
            for h in range(G):
                plan.append(("score", i, kt, h))
                upto = len(ahead) * min(G * kt + h + 1, slots) // slots
                plan += ahead[done:upto]
                done = upto
                if h == 0 and len(waiting) >= 2:
                    plan += waiting.pop(0)
                if kt == kts - 1 and i + 1 < NB and h in (1, 2):
                    plan += turns(i + 1)[2 * h - 2:2 * h]
            waiting.append([("pv", i, kt)] + ([("out", i)] if kt == kts - 1 else []))
            if kt == kts - 2 and i + 1 < NB:
                plan.append(("rows", i + 1))
            if i and kt == 2:
                plan.append(("den", i - 1))
            if i and kt == 4:
                plan += [("proj", i - 1, half) for half in range(2)]
    for left in waiting:
        plan += left
    last = NB - 1
    return plan + [("den", last), ("proj", last, 0), ("proj", last, 1)]


def attention_stage(nc, m, w_out, values):
    name = "attn"
    plan = attention_plan()
    max_unit = {ev: n for n, ev in enumerate(e for e in plan if e[0] == "max")}
    act_unit = {ev: n for n, ev in enumerate(e for e in plan if e[0] in ("score", "turn"))}
    ps_unit = {ev: n for n, ev in enumerate(e for e in plan if e in max_unit or e in act_unit)}
    ps_user = list(ps_unit)
    ktg = {(i, kt): n for n, (i, kt) in enumerate((i, kt) for i in range(NB) for kt in range(TB * (i + 1)))}
    PR = 3
    SR = 6
    with ExitStack() as ctx:
        def sb(n, shape, dt=F32):
            return ctx.enter_context(nc.sbuf_tensor(f"{name}_{n}", shape, dt))

        def ps(n, shape):
            return ctx.enter_context(nc.psum_tensor(f"{name}_{n}", shape, F32))

        K = sb("K", [STACK + 2, G, T], BF16)
        Q = [sb(f"Q{i}", [STACK + 2, G, QB], BF16) for i in range(2)]
        V = sb("V", [P, NT, G, 32])
        prob = sb("prob", [P, PR, G, QB])
        pmax = sb("pmax", [P, 2, TB * G, NB])
        mx, low = sb("mx", [P, TB * G]), sb("low", [P, TB * G])
        rows = sb("rows", [P, 2, TB * G, 2], BF16)
        oT = sb("oT", [P, 2, QB])
        rden, aT = sb("rden", [P, QB]), sb("aT", [P, QB])
        wo = sb("wo", [P, NG, D])
        spread = sb("spread", [P, P])
        identb = sb("identb", [P, P], BF16)
        mask_q = sb("mask_q", [P, P], BF16)
        mask_k = sb("mask_k", [P, P], BF16)
        psS = ps("psS", [P, SR, QB])
        psO = ps("psO", [P, QB])
        psM = ps("psM", [P, QB])

        with stage(nc, name + "_prep", "filled made wo_in") as (block, s):
            @block.gpsimd
            def _(pool):
                for ap, v in ((wo[:], 0.0), (V[:], 0.0), (spread[:], 0.0),
                              (mask_q[:], 0.0), (mask_k[:], 0.0)):
                    pool.memset(ap, v).then_inc(s.filled, 1)
                pool.wait_ge(s.filled, 5)
                pool.memset(V[:, :, :, DH:DH + 1], 1.0).then_inc(s.made, 1)
                pool.affine_select(out=mask_q[:], in_=mask_q[:], compare_op=ALU.is_ge, fill=FAR_BELOW, base=0,
                                   pattern=[[-1, P]], channel_multiplier=1).then_inc(s.made, 1)
                pool.affine_select(out=mask_k[:], in_=mask_k[:], compare_op=ALU.is_ge, fill=FAR_BELOW, base=0,
                                   pattern=[[1, P]], channel_multiplier=-1).then_inc(s.made, 1)
                pool.affine_select(out=spread[:].rearrange("p (h r) -> p h r", h=G),
                                   in_=spread[:].rearrange("p (h r) -> p h r", h=G),
                                   compare_op=ALU.not_equal, fill=1.0, base=-DH,
                                   pattern=[[-32, G], [0, 32]], channel_multiplier=1).then_inc(s.made, 1)

            @block.vector
            def _(dve):
                nc.vector.tensor_copy(identb[:], m.ident[:]).then_inc(s.made, 1)
                nc.vector.memset(K[STACK:STACK + 2], 1.0).then_inc(s.made, 1)

            @block.sync
            def _(sp):
                sp.wait_ge(s.filled, 1)
                for h in range(G):
                    sp.dma_start(wo[32 * h:32 * h + DH],
                                 w_out.rearrange("(g h d) n -> h d g n", g=NG, h=G)[h]).then_inc(s.wo_in, 16)
                sp.wait_ge(s.wo_in, 16 * G)

        with nc.Fori(0, NG) as g:
            names = " ".join(f"k_in{i}" for i in range(NB))
            with stage(nc, name, names + " q_in0 q_in1 v_in s_ready s_used rows_step rows_ready st_ready st_done "
                                         "pv_done out_done den_ready recip_done mul_done proj_ready added")                    as (block, s):
                k_in = s[0:NB]
                q_in = (s.q_in0, s.q_in1)

                def key_cols(i, kt):
                    return max(0, kt - TB * i) * P

                @block.sync
                def _(sp):
                    for i in range(NB):
                        cols = slice(i * QB, (i + 1) * QB)
                        load_stack(sp, m, 1, bass.ds(g * G, G), K_PART, cols, K[0:STACK, :, cols], k_in[i])
                        if i >= 2:
                            sp.wait_ge(s.st_ready, act_unit["score", i - 2, TB * (i - 1) - 1, G - 1] + 1)
                        load_stack(sp, m, 0, bass.ds(g * G, G), Q_PART, cols, Q[i % 2][0:STACK], q_in[i % 2])

                @block.gpsimd
                def _(pool):
                    for i in range(NB):
                        tiles = slice(i * TB, (i + 1) * TB)
                        for h in range(G):
                            nc.gpsimd.tensor_copy(V[:, tiles, h, 0:DH],
                                                  values[:, tiles, bass.ds(g * G + h, 1), :]
                                                  .rearrange("p t a d -> p t (a d)")).then_inc(s.v_in, 1)
                    for i in range(NB):
                        pool.wait_ge(s.recip_done, i + 1)
                        if i:
                            pool.wait_ge(s.proj_ready, 2 * i)
                        nc.gpsimd.tensor_tensor(aT[:], oT[:, i % 2, :], rden[:], ALU.mult).then_inc(s.mul_done, 1)

                @block.tensor
                def _(pe):
                    for ev in plan:
                        kind, i = ev[0:2]
                        if ev in ps_unit:
                            u = ps_unit[ev]
                            before = ps_user[u - SR] if u >= SR else None
                            if before in max_unit:
                                pe.wait_ge(s.s_used, max_unit[before] + 1)
                            elif before in act_unit:
                                pe.wait_ge(s.st_done, act_unit[before] + 1)
                        if kind == "max":
                            _, i, qt, h, c = ev
                            if (qt, h, c) == (0, 0, 0):
                                pe.wait_ge(q_in[i % 2], stack_loads(Q_PART) * (i // 2 + 1))
                                pe.wait_ge(k_in[i], stack_loads(K_PART))
                            n = QB if c < i else (qt + 1) * P
                            diagonal = c == i
                            mm = nc.tensor.matmul(psS[:, u % SR, 0:n], Q[i % 2][0:STACK, h, qt * P:(qt + 1) * P],
                                                  K[0:STACK, h, c * QB:c * QB + n], start=True, stop=not diagonal,
                                                  skip_group_check=True)
                            if diagonal:
                                mm = nc.tensor.matmul(psS[:, u % SR, n - P:n], identb[:], mask_q[:],
                                                      start=False, stop=True, skip_group_check=True)
                            mm.then_inc(s.s_ready, 1)
                        elif kind == "turn":
                            h = ev[2]
                            pe.wait_ge(s.rows_ready, i + 1)
                            for qt in range(TB):
                                mm = nc.tensor.matmul(psS[STACK:STACK + 2, u % SR, qt * P:(qt + 1) * P],
                                                      rows[:, i % 2, qt * G + h, :], identb[:],
                                                      start=True, stop=True)
                            mm.then_inc(s.st_ready, 1)
                        elif kind == "score":
                            _, i, kt, h = ev
                            if kt == 0 and h == 0:
                                pe.wait_ge(s.st_done, act_unit["turn", i, G - 1] + 1)
                            q0 = key_cols(i, kt)
                            diagonal = kt >= TB * i
                            mm = nc.tensor.matmul(psS[:, u % SR, q0:QB], K[:, h, kt * P:(kt + 1) * P],
                                                  Q[i % 2][:, h, q0:QB], start=True, stop=not diagonal,
                                                  skip_group_check=True)
                            if diagonal:
                                mm = nc.tensor.matmul(psS[:, u % SR, q0:q0 + P], identb[:], mask_k[:],
                                                      start=False, stop=True, skip_group_check=True)
                            mm.then_inc(s.st_ready, 1)
                        elif kind == "pv":
                            _, i, kt = ev
                            n = ktg[i, kt]
                            pe.wait_ge(s.st_done, act_unit["score", i, kt, G - 1] + 1)
                            if kt == 0 and i:
                                pe.wait_ge(s.out_done, i)
                            if kt >= TB * i:
                                pe.wait_ge(s.v_in, G * (i + 1))
                            q0 = key_cols(i, kt)
                            for h in range(G):
                                mm = nc.tensor.matmul(psO[32 * h:32 * h + 32, q0:QB], V[:, kt, h, :],
                                                      prob[:, n % PR, h, q0:QB], start=(kt == 0),
                                                      stop=(kt == TB * (i + 1) - 1), skip_group_check=True)
                            mm.then_inc(s.pv_done, 1)
                        elif kind == "den":
                            pe.wait_ge(s.out_done, i + 1)
                            if i:
                                pe.wait_ge(s.added, 2 * i)
                            nc.tensor.matmul(psM[:], spread[:], oT[:, i % 2, :], start=True, stop=True)\
                                .then_inc(s.den_ready, 1)
                        elif kind == "proj":
                            half = ev[2]
                            pe.wait_ge(s.mul_done, i + 1)
                            if half:
                                pe.wait_ge(s.added, 2 * i + 1)
                            for j in range(2):
                                t = half * 2 + j
                                mm = nc.tensor.matmul(psM[:, j * D:(j + 1) * D], aT[:, t * P:(t + 1) * P],
                                                      wo[:, g, :], start=True, stop=True)
                            mm.then_inc(s.proj_ready, 1)

                @block.scalar
                def _(act):
                    for ev in plan:
                        kind, i = ev[0:2]
                        if kind == "score":
                            _, i, kt, h = ev
                            k = ktg[i, kt]
                            n = act_unit[ev]
                            act.wait_ge(s.st_ready, n + 1)
                            if k >= PR and h == 0:
                                act.wait_ge(s.pv_done, k - PR + 1)
                            q0 = key_cols(i, kt)
                            nc.scalar.activation(prob[:, k % PR, h, q0:QB], psS[:, ps_unit[ev] % SR, q0:QB], ACT.Exp,
                                                 scale=DH ** -0.5).then_inc(s.st_done, 1)
                        elif kind == "turn":
                            n = act_unit[ev]
                            act.wait_ge(s.st_ready, n + 1)
                            nc.scalar.copy(Q[i % 2][STACK:STACK + 2, ev[2], :], psS[STACK:STACK + 2, ps_unit[ev] % SR, :])\
                                .then_inc(s.st_done, 1)
                        elif kind == "out":
                            act.wait_ge(s.pv_done, ktg[i, TB * (i + 1) - 1] + 1)
                            if i >= 2:
                                act.wait_ge(s.mul_done, i - 1)
                            nc.scalar.copy(oT[:, i % 2, :], psO[:]).then_inc(s.out_done, 1)

                @block.vector
                def _(dve):
                    for ev in plan:
                        kind, i = ev[0:2]
                        if kind == "max":
                            _, i, qt, h, c = ev
                            u = ps_unit[ev]
                            n = QB if c < i else (qt + 1) * P
                            dve.wait_ge(s.s_ready, max_unit[ev] + 1)
                            nc.vector.tensor_reduce(pmax[:, i % 2, qt * G + h, c:c + 1], psS[:, u % SR, 0:n],
                                                    AX.X, ALU.max).then_inc(s.s_used, 1)
                        elif kind == "rows":
                            dve.wait_ge(s.s_used, max_unit["max", i, TB - 1, G - 1, i] + 1)
                            nc.vector.tensor_reduce(mx[:], pmax[:, i % 2, :, 0:i + 1], AX.X, ALU.max)\
                                .then_inc(s.rows_step, 1)
                            dve.wait_ge(s.rows_step, 3 * i + 1)
                            nc.vector.tensor_scalar(rows[:, i % 2, :, 0], mx[:], -1.0, None, ALU.mult)\
                                .then_inc(s.rows_step, 1)
                            dve.wait_ge(s.rows_step, 3 * i + 2)
                            nc.vector.tensor_tensor(low[:], mx[:], rows[:, i % 2, :, 0], ALU.add)\
                                .then_inc(s.rows_step, 1)
                            dve.wait_ge(s.rows_step, 3 * i + 3)
                            nc.vector.tensor_scalar(rows[:, i % 2, :, 1], low[:], -1.0, None, ALU.mult)\
                                .then_inc(s.rows_ready, 1)
                        elif kind == "den":
                            dve.wait_ge(s.den_ready, i + 1)
                            if i:
                                dve.wait_ge(s.mul_done, i)
                            nc.vector.reciprocal(rden[:], psM[:]).then_inc(s.recip_done, 1)
                        elif kind == "proj":
                            half = ev[2]
                            dve.wait_ge(s.proj_ready, 2 * i + half + 1)
                            t = i * TB + half * 2
                            nc.vector.tensor_tensor(m.x[:, t:t + 2, :], psM[:].rearrange("p (t d) -> p t d", t=2),
                                                    m.x[:, t:t + 2, :], ALU.add).then_inc(s.added, 1)


def causal(nc, m, i):
    with ExitStack() as ctx:
        values = ctx.enter_context(nc.sbuf_tensor("causal_values", [P, NT, H, DH], F32))
        norm_and_values_stage(nc, m, "causal_norm", i["L1_attn_WV"], values)
        split_stage(nc, m, "causal_split", (i["L1_attn_WQ"], i["L1_attn_WK"]))
        attention_stage(nc, m, i["L1_attn_WO"], values)



MF = 64
PAIRS = H // 2
VW = DH + 1


def favor_stage(nc, m, projT, values):
    name = "favor"
    LB = 2 * P
    BODY = 4
    with ExitStack() as ctx:
        def sb(n, shape, dt=F32):
            return ctx.enter_context(nc.sbuf_tensor(f"{name}_{n}", shape, dt))

        def ps(n, shape):
            return ctx.enter_context(nc.psum_tensor(f"{name}_{n}", shape, F32))

        R = STACK + 3
        qs = [sb(f"qs{i}", [R, H, LB], BF16) for i in range(2)]
        ks = [sb(f"ks{i}", [R, H, LB], BF16) for i in range(2)]
        fw = sb("fw", [R, MF], BF16)
        pt, pr = sb("pt", [DH, MF]), sb("pr", [DH, MF])
        pp = sb("pp", [DH, 3, MF], BF16)
        qfT = sb("qfT", [P, 2, PAIRS, P])
        kfT = sb("kfT", [P, 2, PAIRS, P])
        kf = sb("kf", [P, 2, H, MF])
        a = sb("a", [P, 2, PAIRS, 2, P])
        mask = sb("mask", [P, P])
        state = sb("state", [P, 2, PAIRS, 2 * VW])
        rec = sb("rec", [P, H])
        psF = ps("psF", [P, 3, 512])
        psA = ps("psA", [P, 2, 4, P])
        psN = ps("psN", [P, H, VW])
        psD = ps("psD", [P, 512])

        with stage(nc, name + "_prep", "p_in step moved filled made") as (block, s):
            @block.sync
            def _(sp):
                sp.dma_start(pt[:], projT).then_inc(s.p_in, 16)
                sp.wait_ge(s.step, 5)
                for r, part in enumerate(K_PART):
                    sp.dma_start(fw[r * DH:(r + 1) * DH, :], pp[:, part, :]).then_inc(s.moved, 16)
                sp.wait_ge(s.moved, 16 * len(K_PART))

            @block.gpsimd
            def _(pool):
                pool.memset(mask[:], 1.0).then_inc(s.filled, 1)
                pool.memset(state[:], 0.0).then_inc(s.filled, 1)
                pool.wait_ge(s.filled, 2)
                pool.affine_select(out=mask[:], in_=mask[:], compare_op=ALU.is_ge, fill=0.0, base=0,
                                   pattern=[[1, P]], channel_multiplier=-1).then_inc(s.made, 1)

            @block.vector
            def _(dve):
                link = Steps(dve, s.step)
                dve.wait_ge(s.p_in, 16)
                link(nc.vector.tensor_scalar(pt[:], pt[:], DH ** -0.5, None, ALU.mult))
                link(nc.vector.tensor_copy(pp[:, 0, :], pt[:]))
                link(nc.vector.tensor_tensor(pr[:], pt[:], pp[:, 0, :], ALU.subtract))
                link(nc.vector.tensor_copy(pp[:, 1, :], pr[:]))
                link(nc.vector.tensor_tensor(pp[:, 2, :], pr[:], pp[:, 1, :], ALU.subtract))
                nc.vector.memset(fw[STACK:STACK + 3, :], -1.0).then_inc(s.made, 1)

        with stage(nc, name, "in0 in1 f_ready f_exp a_ready a_masked d_ready d_added num_ready num_read rec_ready")\
                as (block, s):
            stacks_in = (s.in0, s.in1)
            per_load = 2 * (stack_loads(Q_PART) + 16)

            @block.sync
            def _(sp):
                def loads(blk, i):
                    cols = bass.ds(blk * LB, LB)
                    for which, dst in ((0, qs), (1, ks)):
                        load_stack(sp, m, which, slice(0, H), Q_PART, cols, dst[i], stacks_in[i])
                        sp.dma_start(dst[i][STACK:], m.stacks[which, :, 3 * DH:, cols]
                                     .rearrange("h r n -> r h n")).then_inc(stacks_in[i], 16)

                loads(0, 0)
                loads(1, 1)
                with sp.Fori(1, NT // BODY) as turn:
                    for i in range(2):
                        sp.wait_ge(s.f_ready, turn * (6 * BODY) - (6 * BODY - 12 * (i + 1)))
                        loads(turn * 2 + i, i)

            @block.tensor
            def _(pe):
                pe.sem_inc(s.f_exp, 3)
                pe.sem_inc(s.a_masked, 2)
                pe.sem_inc(s.num_ready, 2)
                pe.sem_inc(s.d_added, 2)
                pe.sem_inc(s.num_read, 1)

                def features(t, j, u):
                    pe.wait_ge(s.f_exp, t * 6 + (u + 1))
                    half, kind = u // 3, u % 3
                    cols = slice((j % 2) * P, (j % 2 + 1) * P)
                    for n in range(4 if kind < 2 else 8):
                        if kind < 2:
                            src = (qs, ks)[kind][j // 2]
                            for b in range(2):
                                last = nc.tensor.matmul(psF[64 * b:64 * b + 64, u % 3, n * P:(n + 1) * P], fw[:],
                                                        src[:, 2 * (4 * half + n) + b, cols], start=True, stop=True)
                        else:
                            last = nc.tensor.matmul(psF[:, u % 3, n * MF:(n + 1) * MF],
                                                    ks[j // 2][:, 8 * half + n, cols], fw[:], start=True, stop=True)
                    last.then_inc(s.f_ready, 1)

                def products(t, j, half):
                    pe.wait_ge(s.f_exp, t * 6 + (3 * half + 2 + 3))
                    pe.wait_ge(s.a_masked, t * 4 + (2 * half + 2))
                    for n in range(4):
                        for b in range(2):
                            rows = slice(64 * b, 64 * b + 64)
                            last = nc.tensor.matmul(psA[:, b, n, :], kfT[rows, j % 2, 4 * half + n, :],
                                                    qfT[rows, j % 2, 4 * half + n, :], start=True, stop=True)
                            if n == 3:
                                last.then_inc(s.a_ready, 1)

                def tile_sums(t, j):
                    pe.wait_ge(s.f_exp, t * 6 + (6 + 3))
                    pe.wait_ge(s.d_added, t * 2 + 2)
                    for p in range(PAIRS):
                        last = nc.tensor.matmul(psD[:, p * 2 * VW:(p + 1) * 2 * VW], kf[:, j % 2, 2 * p:2 * p + 2, :],
                                                values[:, t, 2 * p:2 * p + 2, :], start=True, stop=True)
                    last.then_inc(s.d_ready, 1)

                def outputs(t, j):
                    pe.wait_ge(s.a_masked, t * 4 + 6)
                    pe.wait_ge(s.num_read, t + 1)
                    for h in range(H):
                        nc.tensor.matmul(psN[:, h, :], a[:, j % 2, h // 2, h % 2, :], values[:, t, h, :],
                                         start=(h == 0), stop=False, skip_group_check=True)
                    for p in range(PAIRS):
                        last = nc.tensor.matmul(psN[:, 2 * p:2 * p + 2, :], qfT[:, j % 2, p, :], state[:, j % 2, p, :],
                                                start=False, stop=True, skip_group_check=True)
                    last.then_inc(s.num_ready, 1)

                def tile(turn, j, last):
                    t = turn * BODY + j
                    following = (j + 1) % BODY

                    def next_features(u):
                        if not last:
                            features(t + 1, following, u)

                    if not last and following % 2 == 0:
                        pe.wait_ge(stacks_in[following // 2], (turn + (j + 1) // BODY) * per_load + per_load)
                    next_features(0)
                    products(t, j, 0)
                    next_features(1)
                    next_features(2)
                    products(t, j, 1)
                    next_features(3)
                    tile_sums(t, j)
                    next_features(4)
                    next_features(5)
                    outputs(t, j)

                pe.wait_ge(stacks_in[0], per_load)
                for u in range(6):
                    features(0, 0, u)
                with pe.Fori(0, NT // BODY - 1) as turn:
                    for j in range(BODY):
                        tile(turn, j, False)
                for j in range(BODY):
                    tile(NT // BODY - 1, j, j == BODY - 1)

            @block.scalar
            def _(act):
                with act.Fori(0, NT // BODY) as turn:
                    for j in range(BODY):
                        t = turn * BODY + j
                        for u in range(6):
                            half, kind = u // 3, u % 3
                            act.wait_ge(s.f_ready, t * 6 + (u + 1))
                            if u == 0:
                                act.wait_ge(s.num_ready, t + 1)
                            dst = (qfT, kfT)[kind][:, j % 2, 4 * half:4 * half + 4, :] if kind < 2 else \
                                kf[:, j % 2, 8 * half:8 * half + 8, :]
                            nc.scalar.activation(dst, psF[:, u % 3, :].rearrange(
                                "p (a b) -> p a b", a=4 if kind < 2 else 8), ACT.Exp).then_inc(s.f_exp, 1)

            @block.vector
            def _(dve):
                def divided(t):
                    dve.wait_ge(s.num_ready, t + 3)
                    nc.vector.reciprocal(rec[:], psN[:, :, DH]).then_inc(s.rec_ready, 1)
                    dve.wait_ge(s.rec_ready, t + 1)
                    nc.vector.tensor_tensor(m.xn[:, t, :].rearrange("p (h d) -> p h d", h=H), psN[:, :, 0:DH],
                                            bc(rec[:].unsqueeze(2), [P, H, DH]), ALU.mult)\
                        .then_inc(s.num_read, 1)

                def turns(turn, first):
                    for j in range(BODY):
                        t = turn * BODY + j
                        dve.wait_ge(s.num_ready, t + 1)
                        for half in range(2):
                            for b in range(2):
                                dve.wait_ge(s.a_ready, t * 4 + (2 * half + b + 1))
                                nc.vector.tensor_tensor(a[:, j % 2, 4 * half:4 * half + 4, b, :], psA[:, b],
                                                        bc(mask[:].unsqueeze(1), [P, 4, P]), ALU.mult)\
                                    .then_inc(s.a_masked, 1)
                            if half == 0 and (j or not first):
                                divided(t - 1)
                        dve.wait_ge(s.d_ready, t + 1)
                        for b in range(2):
                            rows, cols = slice(64 * b, 64 * b + 64), slice(VW * b, VW * b + VW)
                            nc.vector.tensor_tensor(state[rows, (j + 1) % 2, :, cols], state[rows, j % 2, :, cols],
                                                    psD[rows, 0:PAIRS * 2 * VW].rearrange(
                                                        "p (a b) -> p a b", a=PAIRS)[:, :, cols],
                                                    ALU.add).then_inc(s.d_added, 1)

                turns(0, True)
                with dve.Fori(1, NT // BODY) as turn:
                    turns(turn, False)
                divided(NT - 1)


def favor_output_stage(nc, m, w, stats):
    name = "favor_out"
    RB = 4
    with ExitStack() as ctx:
        def sb(n, shape, dt=F32):
            return ctx.enter_context(nc.sbuf_tensor(f"{name}_{n}", shape, dt))

        wo, ob = sb("wo", [P, KC, D]), sb("ob", [P, D])
        mean, rstd = stats
        tile, xT, xb = sb("tile", [P, RB, D]), sb("xT", [P, 2, D]), sb("xb", [P, RB, D])
        psT = ctx.enter_context(nc.psum_tensor(f"{name}_psT", [P, 2, 512], F32))
        psY = ctx.enter_context(nc.psum_tensor(f"{name}_psY", [P, 2, 512], F32))
        with stage(nc, name, "w_in fetched based normed turned turned_out ready done") as (block, s):
            @block.sync
            def _(sp):
                sp.dma_start(wo[:], w[0].rearrange("(k p) n -> p k n", p=P)).then_inc(s.w_in, 16)
                sp.dma_start(ob[:], w[1].partition_broadcast(P)).then_inc(s.w_in, 16)


            @block.scalar
            def _(act):
                def fetch(t, j):
                    act.wait_ge(s.turned, t + 1)
                    nc.scalar.copy(tile[:, j, :], m.xn[:, t, :]).then_inc(s.fetched, 1)

                def turned(t, j):
                    act.wait_ge(s.turned, t + (1 + RB))
                    act.wait_ge(s.ready, t + 1)
                    nc.scalar.copy(xT[:, j % 2], psT[:, j % 2, 0:D]).then_inc(s.turned_out, 1)

                with act.Fori(0, NT // RB) as g:
                    for j in range(RB):
                        fetch(g * RB + j, j)
                    for j in range(RB):
                        turned(g * RB + j, j)

            @block.gpsimd
            def _(pool):
                pool.wait_ge(s.w_in, 32)
                with pool.Fori(0, NT // RB) as g:
                    for j in range(RB):
                        t = g * RB + j
                        pool.wait_ge(s.normed, t + 1)
                        nc.gpsimd.tensor_tensor(xb[:, j, :], xb[:, j, :], ob[:], ALU.add).then_inc(s.based, 1)

            @block.tensor
            def _(pe):
                pe.wait_ge(s.w_in, 32)
                pe.sem_inc(s.turned, RB)
                pe.sem_inc(s.ready, 2)
                pe.sem_inc(s.done, 2)

                def turn(t, j):
                    pe.wait_ge(s.fetched, t + 1)
                    for k in range(KC):
                        last = nc.tensor.transpose(psT[:, j % 2, k * P:(k + 1) * P], tile[:, j, k * P:(k + 1) * P],
                                                   m.ident[:])
                    last.then_inc(s.turned, 1)

                def product(t, j):
                    pe.wait_ge(s.turned_out, t + 1)
                    pe.wait_ge(s.done, t + 1)
                    for k in range(KC):
                        last = nc.tensor.matmul(psY[:, j % 2, 0:D], xT[:, j % 2, k * P:(k + 1) * P], wo[:, k, :],
                                                start=(k == 0), stop=(k == KC - 1))
                    last.then_inc(s.ready, 1)

                with pe.Fori(0, NT // RB) as g:
                    for j in range(RB):
                        turn(g * RB + j, j)
                        if j:
                            product(g * RB + j - 1, j - 1)
                    product(g * RB + RB - 1, RB - 1)

            @block.vector
            def _(dve):
                with dve.Fori(0, NT // RB) as g:
                    dve.wait_ge(s.done, g * RB + 2)
                    for j in range(RB):
                        t = g * RB + j
                        nc.vector.tensor_scalar(xb[:, j, :], m.x[:, t, :], mean[:, bass.ds(t, 1)],
                                                rstd[:, bass.ds(t, 1)], ALU.subtract, ALU.mult).then_inc(s.normed, 1)
                    for j in range(RB):
                        t = g * RB + j
                        dve.wait_ge(s.ready, t + 3)
                        dve.wait_ge(s.based, t + 1)
                        nc.vector.tensor_tensor(m.xn[:, t, :], psY[:, j % 2, 0:D], xb[:, j, :], ALU.add)\
                            .then_inc(s.done, 1)


def favor_norm_stage(nc, m, gamma_dram, beta_dram):
    name = "favor_norm"
    with ExitStack() as ctx:
        def sb(n, shape, dt=F32):
            return ctx.enter_context(nc.sbuf_tensor(f"{name}_{n}", shape, dt))

        b = norm_buffers(nc, ctx, name)
        gamma, beta, y = sb("gamma", [P, D]), sb("beta", [P, D]), sb("y", [P, 2, D])
        with stage(nc, name, "w_in stats stat_step var_ready root_ready normed scaled based added") as (block, s):
            @block.sync
            def _(sp):
                sp.dma_start(gamma[:], gamma_dram.partition_broadcast(P)).then_inc(s.w_in, 16)
                sp.dma_start(beta[:], beta_dram.partition_broadcast(P)).then_inc(s.w_in, 16)

            @block.scalar
            def _(act):
                act.wait_ge(s.var_ready, 1)
                nc.scalar.activation(b.rstd[:], b.t1[:], ACT.Sqrt).then_inc(s.root_ready, 1)

            @block.gpsimd
            def _(pool):
                pool.wait_ge(s.w_in, 32)
                with pool.Fori(0, NT) as t:
                    nc.gpsimd.tensor_tensor(m.x[:, t, :], m.x[:, t, :], beta[:], ALU.add).then_inc(s.based, 1)

            @block.vector
            def _(dve):
                norm_statistics(nc, dve, s, m, b, src=m.xn, eps=1e-6)
                dve.wait_ge(s.w_in, 32)
                with dve.Fori(0, NT // 2) as g:
                    for j in range(2):
                        t = g * 2 + j
                        nc.vector.tensor_scalar(y[:, j, :], m.xn[:, t, :], b.mean[:, bass.ds(t, 1)],
                                                b.rstd[:, bass.ds(t, 1)], ALU.subtract, ALU.mult)\
                            .then_inc(s.normed, 1)
                    for j in range(2):
                        dve.wait_ge(s.normed, g * 2 + (j + 1))
                        nc.vector.tensor_tensor(y[:, j, :], y[:, j, :], gamma[:], ALU.mult).then_inc(s.scaled, 1)
                    for j in range(2):
                        t = g * 2 + j
                        dve.wait_ge(s.scaled, t + 1)
                        dve.wait_ge(s.based, t + 1)
                        nc.vector.tensor_tensor(m.x[:, t, :], m.x[:, t, :], y[:, j, :], ALU.add).then_inc(s.added, 1)
                    dve.wait_ge(s.added, g * 2 + 2)


def favor(nc, m, i):
    with ExitStack() as ctx:
        mean = ctx.enter_context(nc.sbuf_tensor("favor_mean", [P, NT], F32))
        rstd = ctx.enter_context(nc.sbuf_tensor("favor_rstd", [P, NT], F32))
        with nc.sbuf_tensor("favor_values", [P, NT, H, VW], F32) as values:
            norm_and_values_stage(nc, m, "favor_in", i["L0_attn_v_w"], values, i["L0_attn_v_b"], (mean, rstd))
            split_stage(nc, m, "favor_split", (i["L0_attn_q_w"], i["L0_attn_k_w"]),
                        (i["L0_attn_q_b"], i["L0_attn_k_b"]))
            favor_stage(nc, m, i["L0_attn_proj"], values)
        favor_output_stage(nc, m, (i["L0_attn_out_w"], i["L0_attn_out_b"]), (mean, rstd))
        favor_norm_stage(nc, m, i["L0_attn_gamma"], i["L0_attn_beta"])



Ffn = namedtuple("Ffn", "name router router_b up up_b down down_b")
STAGES = (0, 1, 2, 3, 4, 5)


def build(nc, i, out):
    with ExitStack() as ctx:
        m = make_constants(nc, ctx)
        m.slots = nc.dram_tensor("slots", [E * TOP2_CAP, D], F32).ap()
        m.outs = nc.dram_tensor("expert_outs", [E * TOP2_CAP, D], F32).ap()
        m.stacks = nc.dram_tensor("qk_stacks", [2, H, 3 * DH + 3, T], BF16).ap()
        constants_stage(nc, m, i["L0_attn_x"])
        zero_slots_stage(nc, m)

        def switch(name):
            ffn(nc, m, Ffn(name=name, router=i["L0_ffn_w_switch"], router_b=i["L0_ffn_b_switch"],
                                       up=[i["L0_ffn_w1"]], up_b=i["L0_ffn_b1"], down=i["L0_ffn_w2"],
                                       down_b=i["L0_ffn_b2"]), False)

        def top2(name):
            ffn(nc, m, Ffn(name=name, router=i["L1_ffn_router_w"], router_b=None,
                             up=[i["L1_ffn_wg"], i["L1_ffn_wu"]], up_b=None, down=i["L1_ffn_wd"],
                             down_b=None), True)

        parts = [lambda: switch("switch_a"), lambda: favor(nc, m, i), lambda: switch("switch_b"),
                 lambda: top2("top2_a"), lambda: causal(nc, m, i), lambda: top2("top2_b")]
        for n in STAGES:
            parts[n]()
        store_stage(nc, m, out)


_TURNED = ("L1_ffn_router_w", "L1_attn_WQ", "L1_attn_WK", "L1_attn_WV", "L1_attn_WO", "L0_attn_proj")


def kernel(**inputs):
    import numpy as _np
    import concourse.bacc as _bacc
    from concourse import mybir as _mybir
    from concourse.bass_utils import run_bass_kernel_spmd as _run

    nc = _bacc.Bacc("TRN2", target_bir_lowering=False, num_devices=1)
    arrays, aps = {}, {}
    for name, value in inputs.items():
        a = _np.asarray(value)
        a = _np.ascontiguousarray(a.T if name in _TURNED else a)
        arrays[f"in_{name}"] = a
        aps[name] = nc.dram_tensor(f"in_{name}", a.shape, _mybir.dt.from_np(a.dtype), kind="ExternalInput").ap()
    out = nc.dram_tensor("out", (1, T, D), _mybir.dt.float32, kind="ExternalOutput").ap()
    build(nc, aps, out)
    return _run(nc, [arrays], core_ids=[0]).results[0]["out"]
```

```python
from collections import namedtuple
from contextlib import ExitStack, contextmanager

import concourse.bass as bass
from concourse import mybir

ALU = mybir.AluOpType
ACT = mybir.ActivationFunctionType
AX = mybir.AxisListType
F32 = mybir.dt.float32
BF16 = mybir.dt.bfloat16
U32 = mybir.dt.uint32
I32 = mybir.dt.int32

P = 128
T = 4096
D = 256
NT = T // P
KC = D // P
F = 1024
FC = F // P
E = 8
FETCH = 8
FAR = 65536
SWITCH_CAP = int(0.5 * T / E)
TOP2_CAP = int(1.25 * T / E)


@contextmanager
def stage(nc, name, sems):
    with ExitStack() as ctx:
        s = namedtuple("Semaphores", sems)(*(ctx.enter_context(nc.semaphore(f"{name}_{n}")) for n in sems.split()))
        with nc.Block() as block:
            yield block, s
        for one in s:
            nc.sync.sem_clear(one)
        nc.all_engine_barrier()


def pool_semaphore(m, n, increments):
    past = m.pool_past[n]
    m.pool_past[n] += 16 * increments
    return m.pool_dma[n], past


def bc(ap, shape):
    return ap.to_broadcast(shape)



class Memory:
    pass


def make_constants(nc, ctx):
    def sb(name, shape, dt):
        return ctx.enter_context(nc.sbuf_tensor(name, shape, dt))

    m = Memory()
    m.x = sb("x_stream", [P, NT, D], F32)
    m.xn = sb("x_normed", [P, NT, D], F32)
    m.ident = sb("ident", [P, P], F32)
    m.ones = sb("ones_bf", [P, P], BF16)
    m.upto = sb("upto_bf", [P, P], BF16)
    m.eidx8 = sb("eidx8", [P, E], F32)
    m.bits = sb("bit30", [P, 1], U32)
    m.pool_dma = [ctx.enter_context(nc.semaphore(f"pool_dma{n}")) for n in range(2 * NT // FETCH)]
    m.pool_past = [0] * len(m.pool_dma)
    return m


def constants_stage(nc, m, x_in):
    with stage(nc, "const", "filled made x_in") as (block, s):
        @block.gpsimd
        def _(pool):
            pool.memset(m.ident[:], 0.0).then_inc(s.filled, 1)
            pool.memset(m.ones[:], 1.0).then_inc(s.filled, 1)
            pool.memset(m.upto[:], 1.0).then_inc(s.filled, 1)
            pool.wait_ge(s.filled, 3)
            pool.affine_select(out=m.ident[:], in_=m.ident[:], compare_op=ALU.not_equal, fill=1.0, base=0,
                               pattern=[[-1, P]], channel_multiplier=1).then_inc(s.made, 1)
            pool.affine_select(out=m.upto[:], in_=m.upto[:], compare_op=ALU.is_ge, fill=0.0, base=0,
                               pattern=[[1, P]], channel_multiplier=-1).then_inc(s.made, 1)
            pool.iota(m.eidx8[:], pattern=[[1, E]], base=-E, channel_multiplier=0,
                      allow_small_or_imprecise_dtypes=True).then_inc(s.made, 1)
            pool.wait_ge(s.made, 3)

        @block.sync
        def _(sp):
            sp.dma_start(m.x[:], x_in.rearrange("b (t p) d -> (b p) t d", p=P)).then_inc(s.x_in, 16)
            sp.wait_ge(s.x_in, 16)


def store_stage(nc, m, out):
    with stage(nc, "store", "stored") as (block, s):
        @block.sync
        def _(sp):
            sp.dma_start(out.rearrange("b (t p) d -> (b p) t d", p=P), m.x[:]).then_inc(s.stored, 16)
            sp.wait_ge(s.stored, 16)



def norm_statistics(nc, dve, s, m, b, src=None, eps=1e-5):
    n = 0

    def link(ins):
        nonlocal n
        n += 1
        ins.then_inc(s.stat_step, 1)
        dve.wait_ge(s.stat_step, n)

    with dve.Fori(0, NT // RING) as g:
        for j in range(RING):
            t = g * RING + j
            nc.vector.bn_stats(b.stats[:, t, :], (src or m.x)[:, t, :]).then_inc(s.stats, 1)
    dve.wait_ge(s.stats, NT)
    mean_e, m2_e, mean_o, m2_o = (b.stats[:, :, i] for i in (1, 2, 4, 5))
    link(nc.vector.tensor_tensor(b.mean[:], mean_e, mean_o, ALU.add))
    link(nc.vector.tensor_scalar(b.mean[:], b.mean[:], 0.5, None, ALU.mult))
    link(nc.vector.tensor_tensor(b.t0[:], mean_e, mean_o, ALU.subtract))
    link(nc.vector.tensor_tensor(b.t0[:], b.t0[:], b.t0[:], ALU.mult))
    link(nc.vector.tensor_tensor(b.t1[:], m2_e, m2_o, ALU.add))
    link(nc.vector.tensor_scalar(b.t1[:], b.t1[:], 1.0 / D, eps, ALU.mult, ALU.add))
    link(nc.vector.scalar_tensor_tensor(out=b.var[:], in0=b.t0[:], scalar=0.25, in1=b.t1[:],
                                        op0=ALU.mult, op1=ALU.add))
    link(nc.vector.reciprocal(b.t1[:], b.var[:]))
    nc.vector.nop().then_inc(s.var_ready, 1)
    dve.wait_ge(s.root_ready, 1)
    link(nc.vector.tensor_tensor(b.t0[:], b.rstd[:], b.rstd[:], ALU.mult))
    link(nc.vector.tensor_tensor(b.t0[:], b.t0[:], b.var[:], ALU.mult))
    link(nc.vector.tensor_scalar(b.t0[:], b.t0[:], -0.5, 1.5, ALU.mult, ALU.add))
    link(nc.vector.tensor_tensor(b.rstd[:], b.rstd[:], b.t0[:], ALU.mult))


RING = 8
XR = 4
LEAD = 2

NORM_SEMS = "stats stat_step var_ready root_ready normed transposed kept xT_ready projected"


NormBuffers = namedtuple("NormBuffers", "stats mean var rstd t0 t1 tile xT")


def norm_buffers(nc, ctx, name):
    def sb(n, shape, dt=F32):
        return ctx.enter_context(nc.sbuf_tensor(f"{name}_{n}", shape, dt))

    return NormBuffers(
        stats=sb("stats", [P, NT, 6]), mean=sb("mean", [P, NT]), var=sb("var", [P, NT]),
        rstd=sb("rstd", [P, NT]), t0=sb("t0", [P, NT]), t1=sb("t1", [P, NT]),
        tile=sb("tile", [P, RING, D]), xT=sb("xT", [P, XR, D]))


def norm_loop_dve(nc, dve, s, m, b, keeps_turned=False):
    with dve.Fori(0, NT // RING) as g:
        for j in range(RING):
            t = g * RING + j
            dve.wait_ge(s.transposed, t + 1)
            if not keeps_turned:
                dve.wait_ge(s.kept, t + 1)
            nc.vector.tensor_scalar(b.tile[:, j, :], m.x[:, t, :], b.mean[:, bass.ds(t, 1)],
                                    b.rstd[:, bass.ds(t, 1)],
                                    ALU.subtract, ALU.mult).then_inc(s.normed, 1)


def norm_loop_act(nc, act, s, b, psT, keeps_turned=False):
    act.wait_ge(s.var_ready, 1)
    nc.scalar.activation(b.rstd[:], b.t1[:], ACT.Sqrt).then_inc(s.root_ready, 1)
    with act.Fori(0, NT // RING) as g:
        for j in range(RING):
            t = g * RING + j
            act.wait_ge(s.transposed, t + 1 + RING)
            act.wait_ge(s.projected, t + 1)
            if keeps_turned:
                act.wait_ge(s.kept, t + (RING + 1 - XR))
            nc.scalar.copy(b.xT[:, j % XR], psT[:, j % XR, 0:D]).then_inc(s.xT_ready, 1)


def norm_loop_pe(nc, pe, s, m, b, psT, project):
    pe.sem_inc(s.transposed, RING)
    pe.sem_inc(s.projected, XR)

    def transposes(t, j):
        pe.wait_ge(s.normed, t + 1)
        for k in range(KC):
            last = nc.tensor.transpose(psT[:, j % XR, k * P:(k + 1) * P], b.tile[:, j, k * P:(k + 1) * P],
                                       m.ident[:])
        last.then_inc(s.transposed, 1)

    def projection(t, j):
        pe.wait_ge(s.xT_ready, t + 1)
        project(t, j).then_inc(s.projected, 1)

    def tiles(g, last):
        for j in range(RING):
            if not last or j + LEAD < RING:
                transposes(g * RING + (j + LEAD), (j + LEAD) % RING)
            projection(g * RING + j, j)

    for t in range(LEAD):
        transposes(t, t)
    with pe.Fori(0, NT // RING - 1) as g:
        tiles(g, False)
    tiles(NT // RING - 1, True)



class Steps:

    def __init__(self, eng, sem):
        self.eng, self.sem, self.n = eng, sem, 0

    def __call__(self, ins):
        self.n += 1
        ins.then_inc(self.sem, 1)
        self.eng.wait_ge(self.sem, self.n)


def first_hot(nc, link, hot, values, top, t3, t1, eidx8):
    full = [P, NT, E]
    link(nc.vector.tensor_tensor(t3, values, bc(top.unsqueeze(2), full), ALU.is_equal))
    link(nc.vector.tensor_tensor(t3, t3, bc(eidx8.unsqueeze(1), full), ALU.mult))
    link(nc.vector.tensor_reduce(t1, t3, AX.X, ALU.min))
    link(nc.vector.tensor_tensor(hot, bc(eidx8.unsqueeze(1), full), bc(t1.unsqueeze(2), full), ALU.is_equal))


def route_stage(nc, m, w, top2):
    K = 2 if top2 else 1
    cap = TOP2_CAP if top2 else SWITCH_CAP
    name = w.name
    with ExitStack() as ctx:
        def sb(n, shape, dt=F32):
            return ctx.enter_context(nc.sbuf_tensor(f"{name}_{n}", shape, dt))

        b = norm_buffers(nc, ctx, name)
        wr = sb("wr", [P, KC, E])
        br = sb("br", [P, E])
        lg = sb("lg", [P, NT, E])
        ex = sb("ex", [P, NT, E])
        t3 = sb("t3", [P, NT, E])
        hots = [sb(f"hot{k}", [P, NT, E], BF16) for k in range(K)]
        top = [sb(f"top{k}", [P, NT]) for k in range(K)]
        r0, r1 = sb("r0", [P, NT]), sb("r1", [P, NT])
        count_in = sb("count_in", [P, NT, E], BF16)
        scanned = sb("scanned", [P, E, NT])
        restart = sb("restart", [P, E, NT])
        keep = sb("keep", [P, NT, E])
        wt = sb("wt", [P, NT, E])
        ebase = sb("ebase", [P, E])
        cur, cand, cnt = (sb(n, [P, E]) for n in ("cur", "cand", "cnt"))
        psT = ctx.enter_context(nc.psum_tensor(f"{name}_psT", [P, XR, 512], F32))
        psL = ctx.enter_context(nc.psum_tensor(f"{name}_psL", [P, NT, E], F32))
        psP = ctx.enter_context(nc.psum_tensor(f"{name}_psP", [P, NT, E], F32))
        psS = ctx.enter_context(nc.psum_tensor(f"{name}_psS", [P, NT, E], F32))
        full = [P, NT, E]
        turn = 5

        with stage(nc, name, NORM_SEMS + " w_in made step to_exp exped asked counted asked_bit "
                                         "counted_bit bit_step") as (block, s):
            def prefix(dve, link, asked):
                dve.wait_ge(s.counted, asked)
                sums = psS[:].rearrange("p t e -> p e t")
                link(nc.vector.tensor_copy(scanned[:], sums))
                link(nc.vector.tensor_tensor_scan(lg[:].rearrange("p t e -> p (t e)"),
                                                  restart[:].rearrange("p e t -> p (e t)"),
                                                  scanned[:].rearrange("p e t -> p (e t)"), 0.0,
                                                  ALU.mult, ALU.add))
                tiles = lg[:].rearrange("p t e -> p (t e)").rearrange("p (e t) -> p t e", e=E)
                link(nc.vector.tensor_tensor(t3[:], tiles, psS[:], ALU.subtract))
                link(nc.vector.tensor_tensor(t3[:], t3[:], psP[:], ALU.add))

            @block.sync
            def _(sp):
                sp.dma_start(wr[:], w.router.rearrange("(k p) e -> p k e", p=P)).then_inc(s.w_in, 16)
                if not top2:
                    sp.dma_start(br[:], w.router_b.partition_broadcast(P)).then_inc(s.w_in, 16)

            @block.gpsimd
            def _(pool):
                pool.iota(ebase[:], pattern=[[cap, E]], base=-1, channel_multiplier=0,
                          allow_small_or_imprecise_dtypes=True).then_inc(s.made, 1)
                pool.memset(restart[:], 1.0).then_inc(s.made, 1)
                pool.wait_ge(s.made, 2)
                pool.memset(restart[:, :, 0], 0.0).then_inc(s.made, 1)
                pool.sem_inc(s.kept, RING)
                with pool.Fori(0, NT // RING) as g:
                    for j in range(RING):
                        t = g * RING + j
                        pool.wait_ge(s.normed, t + 1)
                        nc.gpsimd.tensor_copy(m.xn[:, t, :], b.tile[:, j, :]).then_inc(s.kept, 1)

            @block.scalar
            def _(act):
                norm_loop_act(nc, act, s, b, psT)
                act.wait_ge(s.to_exp, 1)
                nc.scalar.activation(ex[:], ex[:], ACT.Exp).then_inc(s.exped, 1)

            @block.tensor
            def _(pe):
                pe.wait_ge(s.w_in, 16 if top2 else 32)

                def logits(t, j):
                    for k in range(KC):
                        last = nc.tensor.matmul(psL[:, t, :], b.xT[:, j % XR, k * P:(k + 1) * P], wr[:, k, :],
                                                start=(k == 0), stop=(k == KC - 1))
                    return last

                norm_loop_pe(nc, pe, s, m, b, psT, logits)

                def counts(asked):
                    pe.wait_ge(s.asked, asked)
                    nc.tensor.matmul(psP[:], m.upto[:], count_in[:], start=True, stop=True)
                    nc.tensor.matmul(psS[:], m.ones[:], count_in[:], start=True, stop=True).then_inc(s.counted, 1)

                if top2:
                    with pe.Fori(0, 31) as i:
                        pe.wait_ge(s.asked_bit, i + 1)
                        nc.tensor.matmul(psS[:], m.ones[:], count_in[:], start=True, stop=True)\
                            .then_inc(s.counted_bit, 1)
                    counts(1)
                    counts(2)
                else:
                    counts(1)

            @block.vector
            def _(dve):
                norm_statistics(nc, dve, s, m, b)
                norm_loop_dve(nc, dve, s, m, b)
                link = Steps(dve, s.step)
                dve.wait_ge(s.made, 3)
                dve.wait_ge(s.projected, XR + NT)
                if top2:
                    link(nc.vector.tensor_copy(lg[:], psL[:]))
                else:
                    link(nc.vector.tensor_tensor(lg[:], psL[:], bc(br[:].unsqueeze(1), full), ALU.add))
                link(nc.vector.tensor_reduce(top[0][:], lg[:], AX.X, ALU.max))
                nc.vector.tensor_tensor(ex[:], lg[:], bc(top[0][:].unsqueeze(2), full), ALU.subtract)\
                    .then_inc(s.to_exp, 1)
                if not top2:
                    first_hot(nc, link, hots[0][:], lg[:], top[0][:], t3[:], r0[:], m.eidx8[:])
                    dve.wait_ge(s.exped, 1)
                    link(nc.vector.tensor_reduce(r0[:], ex[:], AX.X, ALU.add))
                    link(nc.vector.reciprocal(r0[:], r0[:]))
                    link(nc.vector.reciprocal(r1[:], r0[:]))
                    link(nc.vector.scalar_tensor_tensor(out=m.gate[0][:], in0=r0[:], scalar=0.5, in1=r1[:],
                                                        op0=ALU.mult, op1=ALU.mult))
                else:
                    dve.wait_ge(s.exped, 1)
                    link(nc.vector.tensor_reduce(r0[:], ex[:], AX.X, ALU.add))
                    link(nc.vector.reciprocal(r0[:], r0[:]))
                    link(nc.vector.tensor_tensor(ex[:], ex[:], bc(r0[:].unsqueeze(2), full), ALU.mult))
                    link(nc.vector.tensor_reduce(top[0][:], ex[:], AX.X, ALU.max))
                    first_hot(nc, link, hots[0][:], ex[:], top[0][:], t3[:], r0[:], m.eidx8[:])
                    link(nc.vector.scalar_tensor_tensor(out=ex[:], in0=hots[0][:], scalar=-2.0, in1=ex[:],
                                                        op0=ALU.mult, op1=ALU.add))
                    link(nc.vector.tensor_reduce(top[1][:], ex[:], AX.X, ALU.max))
                    first_hot(nc, link, hots[1][:], ex[:], top[1][:], t3[:], r0[:], m.eidx8[:])
                    link(nc.vector.tensor_tensor(r0[:], top[0][:], top[1][:], ALU.add))
                    link(nc.vector.tensor_scalar(r0[:], r0[:], 1e-6, None, ALU.add))
                    link(nc.vector.reciprocal(r0[:], r0[:]))
                    for k in range(2):
                        link(nc.vector.tensor_tensor(top[k][:], top[k][:], r0[:], ALU.mult))
                    link(nc.vector.tensor_tensor(wt[:], hots[0][:], bc(top[0][:].unsqueeze(2), full), ALU.mult))
                    link(nc.vector.tensor_tensor(t3[:], hots[1][:], bc(top[1][:].unsqueeze(2), full), ALU.mult))
                    link(nc.vector.tensor_tensor(wt[:], wt[:], t3[:], ALU.add))
                    link(nc.vector.tensor_tensor(t3[:], hots[0][:], hots[1][:], ALU.add))
                    link(nc.vector.scalar_tensor_tensor(out=wt[:], in0=t3[:], scalar=-1.0, in1=wt[:],
                                                        op0=ALU.add, op1=ALU.add))
                    link(nc.vector.memset(cur[:], 0.0))
                    link(nc.vector.memset(m.bits[:], float(1 << 29)))
                    with dve.Fori(0, 30) as i:
                        nc.vector.tensor_tensor(cand[:].bitcast(U32), cur[:].bitcast(U32),
                                                bc(m.bits[:], [P, E]), ALU.bitwise_or).then_inc(s.bit_step, 1)
                        dve.wait_ge(s.bit_step, i * turn + 1)
                        nc.vector.tensor_tensor(count_in[:], wt[:], bc(cand[:].unsqueeze(1), full), ALU.is_ge)\
                            .then_inc(s.asked_bit, 1)
                        nc.vector.tensor_scalar(m.bits[:], m.bits[:], 1, None, ALU.logical_shift_right)\
                            .then_inc(s.bit_step, 1)
                        dve.wait_ge(s.counted_bit, i + 1)
                        nc.vector.tensor_reduce(cnt[:], psS[:].rearrange("p t e -> p e t"), AX.X, ALU.add)\
                            .then_inc(s.bit_step, 1)
                        dve.wait_ge(s.bit_step, i * turn + 3)
                        nc.vector.scalar_tensor_tensor(out=cand[:], in0=cnt[:], scalar=float(cap), in1=cand[:],
                                                       op0=ALU.is_ge, op1=ALU.mult).then_inc(s.bit_step, 1)
                        dve.wait_ge(s.bit_step, i * turn + 4)
                        nc.vector.tensor_tensor(cur[:], cur[:], cand[:], ALU.max).then_inc(s.bit_step, 1)
                        dve.wait_ge(s.bit_step, i * turn + 5)
                    thr = bc(cur[:].unsqueeze(1), full)
                    link(nc.vector.tensor_tensor(keep[:], wt[:], thr, ALU.is_gt))
                    nc.vector.tensor_copy(count_in[:], keep[:]).then_inc(s.asked_bit, 1)
                    dve.wait_ge(s.counted_bit, 31)
                    link(nc.vector.tensor_reduce(cnt[:], psS[:].rearrange("p t e -> p e t"), AX.X, ALU.add))
                    link(nc.vector.tensor_scalar(cnt[:], cnt[:], -1.0, float(cap), ALU.mult, ALU.add))
                    link(nc.vector.tensor_tensor(wt[:], wt[:], thr, ALU.is_equal))
                    nc.vector.tensor_copy(count_in[:], wt[:]).then_inc(s.asked, 1)
                    prefix(dve, link, 1)
                    link(nc.vector.tensor_tensor(t3[:], t3[:], bc(cnt[:].unsqueeze(1), full), ALU.is_le))
                    link(nc.vector.tensor_tensor(t3[:], t3[:], wt[:], ALU.mult))
                    link(nc.vector.tensor_tensor(keep[:], keep[:], t3[:], ALU.add))
                link(nc.vector.tensor_copy(count_in[:], (keep if top2 else hots[0])[:]))
                nc.vector.nop().then_inc(s.asked, 1)
                prefix(dve, link, K)
                if not top2:
                    link(nc.vector.tensor_scalar(keep[:], t3[:], float(cap), None, ALU.is_le))
                link(nc.vector.tensor_tensor(t3[:], t3[:], bc(ebase[:].unsqueeze(1), full), ALU.add))
                for k in range(K):
                    link(nc.vector.tensor_tensor(ex[:], t3[:], hots[k][:], ALU.mult))
                    link(nc.vector.tensor_reduce(r0[:], ex[:], AX.X, ALU.add))
                    link(nc.vector.tensor_tensor(ex[:], keep[:], hots[k][:], ALU.mult))
                    link(nc.vector.tensor_reduce(r1[:], ex[:], AX.X, ALU.add))
                    if top2:
                        link(nc.vector.tensor_tensor(m.fetch[k][:], r0[:], r1[:], ALU.mult))
                        link(nc.vector.scalar_tensor_tensor(out=m.gate[k][:], in0=top[k][:], scalar=0.5,
                                                            in1=r1[:], op0=ALU.mult, op1=ALU.mult))
                    link(nc.vector.tensor_scalar(r1[:], r1[:], -float(FAR), float(FAR), ALU.mult, ALU.add))
                    link(nc.vector.tensor_tensor(m.place[k][:], r0[:], r1[:], ALU.add))



def zero_slots_stage(nc, m):
    with ExitStack() as ctx:
        zeros = ctx.enter_context(nc.sbuf_tensor("zeros", [P, 8, D], F32))
        with stage(nc, "zero", "zeroed written") as (block, s):
            @block.vector
            def _(dve):
                nc.vector.memset(zeros[:], 0.0).then_inc(s.zeroed, 1)

            @block.sync
            def _(sp):
                sp.wait_ge(s.zeroed, 1)
                rows = P * 8
                for r in range(E * TOP2_CAP // rows):
                    sp.dma_start(m.slots[r * rows:(r + 1) * rows, :].rearrange("(p a) d -> p a d", p=P),
                                 zeros[:]).then_inc(s.written, 16)
                sp.wait_ge(s.written, 16 * (E * TOP2_CAP // rows))


def dispatch_stage(nc, m, name, top2):
    K, cap = (2, TOP2_CAP) if top2 else (1, SWITCH_CAP)
    scattered, past = pool_semaphore(m, 0, NT * K)
    with stage(nc, name, "") as (block, s):
        @block.gpsimd
        def _(pool):
            for t in range(NT):
                for k in range(K):
                    pool.indirect_dma_start(
                        out=m.slots[0:E * cap, :], out_offset=bass.IndirectOffsetOnAxis(ap=m.place[k][:, t:t + 1], axis=0),
                        in_=m.xn[:, t, :], in_offset=None, bounds_check=E * cap - 1,
                        oob_is_err=False).then_inc(scattered, 16)
            pool.wait_ge(scattered, past + 16 * NT * K)


def experts_stage(nc, m, w, top2):
    cap = TOP2_CAP if top2 else SWITCH_CAP
    S = cap // P
    NP = 2 if top2 else 1
    W = cap // NP
    UP = 2 if top2 else 1
    name = w.name + "_x"
    with ExitStack() as ctx:
        def sb(n, shape, dt=F32):
            return ctx.enter_context(nc.sbuf_tensor(f"{name}_{n}", shape, dt))

        def ps(n):
            return ctx.enter_context(nc.psum_tensor(f"{name}_{n}", [P, 2, 512], F32))

        w1 = [sb(f"w1_{h}", [P, UP, KC, F]) for h in range(2)]
        w2 = [sb(f"w2_{h}", [P, FC, D]) for h in range(2)]
        a = [sb(f"a_{h}", [P, S, D]) for h in range(2)]
        aT = [sb(f"aT_{h}", [P, KC, cap]) for h in range(2)]
        hid = sb("hid", [P, FC, cap])
        yo = [sb(f"yo_{h}", [P, S, D]) for h in range(2)]
        if top2:
            sg = sb("sg", [P, 2, W])
        else:
            b1 = sb("b1", [P, E * FC])
            b1r = sb("b1r", [E * FC, P])
            b2 = sb("b2", [P, E, D])
        psT, psG, psU, psY = ps("psT"), ps("psG"), ps("psU"), ps("psY")
        slots = m.slots[0:E * cap, :].rearrange("(e s p) d -> e p s d", e=E, p=P)
        outs = m.outs[0:E * cap, :].rearrange("(e s p) d -> e p s d", e=E, p=P)
        w1_dram = [v.rearrange("e (k p) f -> e p k f", p=P) for v in w.up]
        w2_dram = w.down.rearrange("e (c p) d -> e p c d", p=P)

        def over_experts(eng, body):
            with eng.Fori(0, E // 2 - 1) as pair:
                for h in range(2):
                    body(pair * 2 + h, h, pair, False)
            for h in range(2):
                body(E - 2 + h, h, E // 2 - 1, h == 1)

        with stage(nc, name, "a_in0 a_in1 w1_in0 w1_in1 w2_in0 w2_in1 bias_in b1_turned b1_ready "
                                   "turned turned_out hidden gated done y_ready y_out yo_free") as (block, s):
            a_in, w1_in, w2_in = (s.a_in0, s.a_in1), (s.w1_in0, s.w1_in1), (s.w2_in0, s.w2_in1)
            stored = [pool_semaphore(m, h, E // 2) for h in range(2)]
            hid_done = s.done if top2 else s.gated

            @block.sync
            def _(sp):
                def loads(e, h):
                    sp.dma_start(a[h][:], slots[e]).then_inc(a_in[h], 16)
                    for u in range(UP):
                        sp.dma_start(w1[h][:, u], w1_dram[u][e]).then_inc(w1_in[h], 16)
                    sp.dma_start(w2[h][:], w2_dram[e]).then_inc(w2_in[h], 16)

                loads(0, 0)
                if not top2:
                    sp.dma_start(b1r[:], w.up_b.rearrange("e (c p) -> (e c) p", p=P)).then_inc(s.bias_in, 16)
                    sp.dma_start(b2[:], w.down_b.partition_broadcast(P)).then_inc(s.bias_in, 16)
                loads(1, 1)
                with sp.Fori(1, E // 2) as pair:
                    for h in range(2):
                        sp.wait_ge(s.y_ready, (pair * 2 + h - 1) * S)
                        loads(pair * 2 + h, h)

            @block.tensor
            def _(pe):
                def turn(e, h, pair):
                    pe.wait_ge(a_in[h], pair * 16 + 16)
                    for i in range(S):
                        n = e * S + i
                        pe.wait_ge(s.turned_out, n + 1)
                        for k in range(KC):
                            last = nc.tensor.transpose(psT[:, (h * S + i) % 2, k * P:(k + 1) * P],
                                                       a[h][:, i, k * P:(k + 1) * P], m.ident[:])
                        last.then_inc(s.turned, 1)

                def hidden(e, h, pair):
                    pe.wait_ge(s.turned_out, e * S + S + 2)
                    pe.wait_ge(w1_in[h], pair * (16 * UP) + 16 * UP)
                    for c in range(FC):
                        for q in range(NP):
                            n = (e * FC + c) * NP + q
                            slot = (c * NP + q) % 2
                            pe.wait_ge(s.gated, n + 1)
                            if top2:
                                pe.wait_ge(s.done, n + 1)
                            for u, ps_u in enumerate((psG, psU)[:UP]):
                                for k in range(KC):
                                    last = nc.tensor.matmul(ps_u[:, slot, 0:W], w1[h][:, u, k, c * P:(c + 1) * P],
                                                            aT[h][:, k, q * W:(q + 1) * W],
                                                            start=(k == 0), stop=(k == KC - 1))
                            last.then_inc(s.hidden, 1)

                def down(e, h, pair):
                    pe.wait_ge(w2_in[h], pair * 16 + 16)
                    pe.wait_ge(hid_done, e * (FC * NP) + (FC * NP + 2))
                    for i in range(S):
                        pe.wait_ge(s.y_out, e * S + i + 1)
                        for c in range(FC):
                            last = nc.tensor.matmul(psY[:, (h * S + i) % 2, 0:D], hid[:, c, i * P:(i + 1) * P],
                                                    w2[h][:, c, :], start=(c == 0), stop=(c == FC - 1))
                        last.then_inc(s.y_ready, 1)

                pe.sem_inc(s.turned_out, 2)
                pe.sem_inc(s.gated, 2)
                pe.sem_inc(s.y_out, 2)
                if top2:
                    pe.sem_inc(s.done, 2)
                else:
                    pe.wait_ge(s.bias_in, 32)
                    nc.tensor.transpose(psU[:, 0, 0:E * FC], b1r[:], m.ident[0:E * FC, 0:E * FC])\
                        .then_inc(s.b1_turned, 1)
                turn(0, 0, 0)

                def body(e, h, pair, last):
                    hidden(e, h, pair)
                    if not last:
                        turn(e + 1, 1 - h, pair + h)
                    down(e, h, pair)

                over_experts(pe, body)

            @block.scalar
            def _(act):
                def turned(e, h):
                    for i in range(S):
                        act.wait_ge(s.turned, e * S + i + 1)
                        nc.scalar.copy(aT[h][:, :, i * P:(i + 1) * P],
                                       psT[:, (h * S + i) % 2, 0:D].rearrange("p (k n) -> p k n", k=KC))\
                            .then_inc(s.turned_out, 1)

                turned(0, 0)
                if not top2:
                    act.wait_ge(s.b1_ready, 1)

                def body(e, h, pair, last):
                    for c in range(FC):
                        for q in range(NP):
                            n = (e * FC + c) * NP + q
                            slot = (c * NP + q) % 2
                            act.wait_ge(s.hidden, n + 1)
                            if top2:
                                act.wait_ge(s.done, n + 1)
                                nc.scalar.activation(sg[:, slot, :], psG[:, slot, 0:W], ACT.Silu)\
                                    .then_inc(s.gated, 1)
                            else:
                                nc.scalar.activation(hid[:, c, :], psG[:, slot, 0:W], ACT.Relu,
                                                     bias=b1[:, bass.ds(e * FC + c, 1)]).then_inc(s.gated, 1)
                    if not last:
                        turned(e + 1, 1 - h)

                over_experts(act, body)

            @block.vector
            def _(dve):
                if not top2:
                    dve.wait_ge(s.b1_turned, 1)
                    nc.vector.tensor_copy(b1[:], psU[:, 0, 0:E * FC]).then_inc(s.b1_ready, 1)

                def body(e, h, pair, last):
                    if top2:
                        for c in range(FC):
                            for q in range(NP):
                                n = (e * FC + c) * NP + q
                                slot = (c * NP + q) % 2
                                dve.wait_ge(s.gated, n + 3)
                                nc.vector.tensor_tensor(hid[:, c, q * W:(q + 1) * W], sg[:, slot, :],
                                                        psU[:, slot, 0:W], ALU.mult).then_inc(s.done, 1)
                    dve.wait_ge(s.yo_free, e + 1)
                    for i in range(S):
                        dve.wait_ge(s.y_ready, e * S + i + 1)
                        src = psY[:, (h * S + i) % 2, 0:D]
                        if top2:
                            nc.vector.tensor_copy(yo[h][:, i, :], src).then_inc(s.y_out, 1)
                        else:
                            nc.vector.tensor_tensor(yo[h][:, i, :], src, b2[:, e, :], ALU.add).then_inc(s.y_out, 1)

                over_experts(dve, body)

            @block.gpsimd
            def _(pool):
                pool.sem_inc(s.yo_free, 2)

                def body(e, h, pair, last):
                    pool.wait_ge(s.y_out, e * S + S + 2)
                    in_dram, past = stored[h]
                    pool.dma_start(outs[e], yo[h][:]).then_inc(in_dram, 16)
                    pool.wait_ge(in_dram, pair * 16 + (past + 16))
                    pool.sem_inc(s.yo_free, 1)

                over_experts(pool, body)


def combine_stage(nc, m, name, top2):
    K, cap = (2, TOP2_CAP) if top2 else (1, SWITCH_CAP)
    with ExitStack() as ctx:
        got = [m.xn, ctx.enter_context(nc.sbuf_tensor(name + "_got1", [P, NT, D], F32)) if top2 else None]
        groups = NT // FETCH
        fetched = [pool_semaphore(m, n, FETCH) for n in range(K * groups)]
        with stage(nc, name, "added") as (block, s):

            @block.gpsimd
            def _(pool):
                for t in range(NT):
                    for k in range(K):
                        where = (m.fetch if top2 else m.place)[k]
                        pool.indirect_dma_start(
                            out=got[k][:, t, :], out_offset=None, in_=m.outs[0:E * cap, :],
                            in_offset=bass.IndirectOffsetOnAxis(ap=where[:, t:t + 1], axis=0),
                            bounds_check=E * cap - 1, oob_is_err=False)\
                            .then_inc(fetched[k * groups + t // FETCH][0], 16)

            @block.vector
            def _(dve):
                for g in range(NT // FETCH):
                    for k in range(K):
                        got_in, past = fetched[k * groups + g]
                        dve.wait_ge(got_in, past + 16 * FETCH)
                        if k:
                            dve.wait_ge(s.added, (g * K + k) * FETCH)
                        for t in range(g * FETCH, g * FETCH + FETCH):
                            nc.vector.scalar_tensor_tensor(
                                out=m.x[:, t, :], in0=got[k][:, t, :], scalar=m.gate[k][:, t:t + 1],
                                in1=m.x[:, t, :], op0=ALU.mult, op1=ALU.add).then_inc(s.added, 1)


def ffn(nc, m, w, top2):
    K = 2 if top2 else 1
    with ExitStack() as ctx:
        m.place = [ctx.enter_context(nc.sbuf_tensor(f"{w.name}_place{k}", [P, NT], U32)) for k in range(K)]
        m.fetch = [ctx.enter_context(nc.sbuf_tensor(f"{w.name}_fetch{k}", [P, NT], U32)) for k in range(K)]
        m.gate = [ctx.enter_context(nc.sbuf_tensor(f"{w.name}_gate{k}", [P, NT], F32)) for k in range(K)]
        route_stage(nc, m, w, top2)
        dispatch_stage(nc, m, w.name + "_dispatch", top2)
        experts_stage(nc, m, w, top2)
        combine_stage(nc, m, w.name + "_combine", top2)



QB = 512
NB = T // QB
TB = QB // P
H = 16
DH = D // H
EVEN = 8


def norm_and_values_stage(nc, m, name, wv_dram, values, bias_dram=None, stats=None):
    xnT = turned_view(m)
    with ExitStack() as ctx:
        def sb(n, shape, dt=F32):
            return ctx.enter_context(nc.sbuf_tensor(f"{name}_{n}", shape, dt))

        b = norm_buffers(nc, ctx, name)
        if stats is not None:
            b = b._replace(mean=stats[0], rstd=stats[1])
        wv = sb("wv", [P, KC, D])
        bv = sb("bv", [P, D])
        psT = ctx.enter_context(nc.psum_tensor(f"{name}_psT", [P, XR, 512], F32))
        psV = ctx.enter_context(nc.psum_tensor(f"{name}_psV", [P, 2, 512], F32))
        with stage(nc, name, NORM_SEMS + " w_in v_done ones_made") as (block, s):
            @block.sync
            def _(sp):
                sp.dma_start(wv[:], wv_dram.rearrange("(k p) n -> p k n", p=P)).then_inc(s.w_in, 16)
                if bias_dram is not None:
                    sp.dma_start(bv[:], bias_dram.partition_broadcast(P)).then_inc(s.w_in, 16)

            @block.gpsimd
            def _(pool):
                if values.shape[3] > DH:
                    pool.memset(values[:, :, :, DH:], 1.0).then_inc(s.ones_made, 1)
                pool.sem_inc(s.kept, RING)
                with pool.Fori(0, NT // RING) as g:
                    for j in range(RING):
                        t = g * RING + j
                        pool.wait_ge(s.xT_ready, t + 1)
                        nc.gpsimd.tensor_copy(xnT[:, :, bass.ds(t * P, P)],
                                              b.xT[:, j % XR].rearrange("p (k n) -> p k n", k=KC))\
                            .then_inc(s.kept, 1)

            @block.scalar
            def _(act):
                norm_loop_act(nc, act, s, b, psT, keeps_turned=True)

            @block.tensor
            def _(pe):
                pe.wait_ge(s.w_in, 16 if bias_dram is None else 32)
                pe.sem_inc(s.v_done, 2)

                def v(t, j):
                    pe.wait_ge(s.v_done, t + 1)
                    for k in range(KC):
                        last = nc.tensor.matmul(psV[:, j % 2, 0:D], b.xT[:, j % XR, k * P:(k + 1) * P], wv[:, k, :],
                                                start=(k == 0), stop=(k == KC - 1))
                    return last

                norm_loop_pe(nc, pe, s, m, b, psT, v)

            @block.vector
            def _(dve):
                norm_statistics(nc, dve, s, m, b)
                norm_loop_dve_values(nc, dve, s, m, b, psV, values, bv if bias_dram is not None else None)


def norm_loop_dve_values(nc, dve, s, m, b, psV, values, bv):
    def normed(t, j):
        dve.wait_ge(s.transposed, t + 1)
        nc.vector.tensor_scalar(b.tile[:, j, :], m.x[:, t, :], b.mean[:, bass.ds(t, 1)],
                                b.rstd[:, bass.ds(t, 1)], ALU.subtract, ALU.mult).then_inc(s.normed, 1)

    def value(t, j):
        dve.wait_ge(s.projected, t + (1 + XR))
        out = values[:, t, :, 0:DH]
        src = psV[:, j % 2, 0:D].rearrange("p (h d) -> p h d", h=H)
        if bv is None:
            nc.vector.tensor_copy(out, src).then_inc(s.v_done, 1)
        else:
            nc.vector.tensor_tensor(out, src, bv[:].rearrange("p (h d) -> p h d", h=H), ALU.add)\
                .then_inc(s.v_done, 1)

    def tiles(g, last):
        for j in range(RING):
            if not last or j + 2 * LEAD < RING:
                normed(g * RING + (j + 2 * LEAD), (j + 2 * LEAD) % RING)
            value(g * RING + j, j)

    for t in range(2 * LEAD):
        normed(t, t)
    with dve.Fori(0, NT // RING - 1) as g:
        tiles(g, False)
    tiles(NT // RING - 1, True)


def turned_view(m):
    return m.xn[:].rearrange("p t d -> p (t d)").rearrange("p (k n) -> p k n", k=KC)



Q_PART = (0, 0, 0, 1, 1, 2)
K_PART = (0, 1, 2, 0, 1, 0)
STACK = len(Q_PART) * DH
G = 4
NG = H // G
LN8 = 2.0794415416798357
FAR_BELOW = -1e30


def runs(parts):
    found, r = [], 0
    while r < len(parts):
        n = 1
        while r + n < len(parts) and parts[r + n] == parts[r] + n:
            n += 1
        found.append((r, parts[r], n))
        r += n
    return found


def load_stack(sp, m, which, heads, parts, cols, out, sem):
    for r, part, n in runs(parts):
        sp.dma_start(out[r * DH:(r + n) * DH],
                     m.stacks[which, heads, part * DH:(part + n) * DH, cols]
                     .rearrange("h r n -> r h n")).then_inc(sem, 16)


def stack_loads(parts):
    return 16 * len(runs(parts))


def split_stage(nc, m, name, w, bias=None):
    xnT = turned_view(m)
    favor_kind = bias is not None
    with ExitStack() as ctx:
        def sb(n, shape, dt=F32):
            return ctx.enter_context(nc.sbuf_tensor(f"{name}_{n}", shape, dt))

        wqk = [sb(f"w{i}", [P, KC, D]) for i in range(2)]
        PR = 4
        parts = sb("parts", [P, PR, 3, QB], BF16)
        rest = sb("rest", [P, 2, QB])
        ps = ctx.enter_context(nc.psum_tensor(f"{name}_ps", [P, 2, QB], F32))
        tasks = [(i, c) for i in range(2) for c in range(KC)]
        n_tasks = len(tasks)
        if favor_kind:
            b = sb("b", [P, 2, KC])
            val, sq = sb("val", [P, 2, QB]), sb("sq", [P, 2, QB])
            halves = sb("halves", [P, 32])
            norm, norm_rest = sb("norm", [P, QB]), sb("norm_rest", [P, QB])
            norm_parts = sb("norm_parts", [P, 3, QB], BF16)
            psC = ctx.enter_context(nc.psum_tensor(f"{name}_psC", [P, QB], F32))
        with stage(nc, name, "w_in ready taken high rest1 mid low put0 put1 put2 put3 part_free filled made squared summed "
                             "sum_taken sum_step sums_ready sums_put") as (block, s):
            put = (s.put0, s.put1, s.put2, s.put3)

            @block.sync
            def _(sp):
                for i in range(2):
                    sp.dma_start(wqk[i][:], w[i].rearrange("(k p) n -> p k n", p=P)).then_inc(s.w_in, 16)
                    if favor_kind:
                        sp.dma_start(b[:, i, :], bias[i].rearrange("(k p) -> p k", p=P),
                                     allow_slow_non_contiguous=True).then_inc(s.w_in, 16)
                with sp.Fori(0, NB) as blk:
                    cols = bass.ds(blk * QB, QB)
                    for j, (i, c) in enumerate(tasks):
                        sp.wait_ge(s.low, blk * n_tasks + (j + 1))
                        rows = m.stacks[i, c * EVEN:(c + 1) * EVEN]
                        for part in range(3):
                            sp.dma_start(rows[:, part * DH:(part + 1) * DH, cols],
                                         parts[:, j, part, :]).then_inc(put[j], 16)
                    if favor_kind:
                        sp.wait_ge(s.sums_ready, blk + 1)
                        for j, (i, c) in enumerate(tasks):
                            for part in range(3):
                                sp.dma_start(m.stacks[i, c * EVEN:(c + 1) * EVEN, 3 * DH + part, cols],
                                             norm_parts[32 * j:32 * j + EVEN, part, :]).then_inc(s.sums_put, 16)
                for one in put:
                    sp.wait_ge(one, 48 * NB)
                if favor_kind:
                    sp.wait_ge(s.sums_put, 48 * n_tasks * NB)

            if favor_kind:
                @block.gpsimd
                def _(pool):
                    pool.memset(halves[:], 0.5).then_inc(s.filled, 1)
                    pool.wait_ge(s.filled, 1)
                    pool.affine_select(out=halves[:], in_=halves[:], compare_op=ALU.is_ge, fill=0.0, base=0,
                                       pattern=[[-DH, 32]], channel_multiplier=1).then_inc(s.filled, 1)
                    pool.wait_ge(s.filled, 2)
                    pool.affine_select(out=halves[:], in_=halves[:], compare_op=ALU.is_ge, fill=0.0, base=DH - 1,
                                       pattern=[[DH, 32]], channel_multiplier=-1).then_inc(s.made, 1)

            @block.tensor
            def _(pe):
                pe.wait_ge(s.w_in, 64 if favor_kind else 32)
                pe.sem_inc(s.taken, 2)
                if favor_kind:
                    pe.wait_ge(s.made, 1)
                    pe.sem_inc(s.summed, 2)
                    pe.sem_inc(s.sum_taken, 1)

                def square_sums(blk, j):
                    pe.wait_ge(s.squared, blk * n_tasks + (j + 1))
                    if j == 0:
                        pe.wait_ge(s.sum_taken, blk + 1)
                    nc.tensor.matmul(psC[32 * j:32 * j + 32, :], halves[:], sq[:, j % 2, :],
                                     start=True, stop=True).then_inc(s.summed, 1)

                with pe.Fori(0, NB) as blk:
                    for j, (i, c) in enumerate(tasks):
                        pe.wait_ge(s.taken, blk * n_tasks + (j + 1))
                        for k in range(KC):
                            last = nc.tensor.matmul(ps[:, j % 2, :], wqk[i][:, k, c * P:(c + 1) * P],
                                                    xnT[:, k, bass.ds(blk * QB, QB)],
                                                    start=(k == 0), stop=(k == KC - 1))
                        last.then_inc(s.ready, 1)
                        if favor_kind and j:
                            square_sums(blk, j - 1)
                    if favor_kind:
                        square_sums(blk, n_tasks - 1)

            @block.scalar
            def _(act):
                def block_parts(blk, first):
                    for j in range(n_tasks):
                        n = blk * n_tasks + j
                        if not first:
                            act.wait_ge(put[j], blk * 48)
                        if favor_kind:
                            act.wait_ge(s.taken, n + 3)
                            nc.scalar.copy(parts[:, j, 0, :], val[:, j % 2, :]).then_inc(s.high, 1)
                            act.wait_ge(s.summed, n + 1)
                            nc.scalar.activation(sq[:, j % 2, :], val[:, j % 2, :], ACT.Square,
                                                 scale=DH ** -0.5).then_inc(s.squared, 1)
                        else:
                            act.wait_ge(s.ready, n + 1)
                            nc.scalar.copy(parts[:, j, 0, :], ps[:, j % 2, :]).then_inc(s.high, 1)
                        act.wait_ge(s.rest1, n + 1)
                        nc.scalar.copy(parts[:, j, 1, :], rest[:, j % 2, :]).then_inc(s.mid, 1)

                block_parts(0, True)
                with act.Fori(1, NB) as blk:
                    block_parts(blk, False)

            @block.vector
            def _(dve):
                if favor_kind:
                    dve.wait_ge(s.w_in, 64)

                def block_parts(blk, first):
                    for j, (i, c) in enumerate(tasks):
                        n = blk * n_tasks + j
                        if favor_kind:
                            dve.wait_ge(s.ready, n + 1)
                            nc.vector.tensor_scalar(val[:, j % 2, :], ps[:, j % 2, :], b[:, i, c:c + 1], None,
                                                    ALU.add).then_inc(s.taken, 1)
                            dve.wait_ge(s.high, n + 1)
                            nc.vector.tensor_tensor(rest[:, j % 2, :], val[:, j % 2, :], parts[:, j, 0, :],
                                                    ALU.subtract).then_inc(s.rest1, 1)
                        else:
                            dve.wait_ge(s.high, n + 1)
                            nc.vector.tensor_tensor(rest[:, j % 2, :], ps[:, j % 2, :], parts[:, j, 0, :],
                                                    ALU.subtract).then_inc(s.rest1, 1)
                        dve.wait_ge(s.mid, n + 1)
                        nc.vector.tensor_tensor(parts[:, j, 2, :], rest[:, j % 2, :], parts[:, j, 1, :],
                                                ALU.subtract).then_inc(s.low, 1)
                        if not favor_kind:
                            dve.sem_inc(s.taken, 1)
                    if favor_kind:
                        step = blk * 3
                        dve.wait_ge(s.summed, blk * n_tasks + (n_tasks + 2))
                        nc.vector.tensor_scalar(norm[:], psC[:], LN8, None, ALU.add).then_inc(s.sum_taken, 1)
                        dve.wait_ge(s.sum_taken, blk + 2)
                        if not first:
                            dve.wait_ge(s.sums_put, blk * (48 * n_tasks))
                        nc.vector.tensor_copy(norm_parts[:, 0, :], norm[:]).then_inc(s.sum_step, 1)
                        dve.wait_ge(s.sum_step, step + 1)
                        nc.vector.tensor_tensor(norm_rest[:], norm[:], norm_parts[:, 0, :], ALU.subtract)\
                            .then_inc(s.sum_step, 1)
                        dve.wait_ge(s.sum_step, step + 2)
                        nc.vector.tensor_copy(norm_parts[:, 1, :], norm_rest[:]).then_inc(s.sum_step, 1)
                        dve.wait_ge(s.sum_step, step + 3)
                        nc.vector.tensor_tensor(norm_parts[:, 2, :], norm_rest[:], norm_parts[:, 1, :],
                                                ALU.subtract).then_inc(s.sums_ready, 1)

                block_parts(0, True)
                with dve.Fori(1, NB) as blk:
                    block_parts(blk, False)


def attention_plan():
    def maxima(i):
        return [("max", i, qt, h, c) for qt in range(TB) for h in range(G) for c in range(i + 1)]

    def turns(i):
        return [("turn", i, h) for h in range(G)]

    begin = [G * TB * i * (i + 1) // 2 for i in range(NB + 1)]
    lead = 15
    plan = maxima(0) + [("rows", 0)]
    waiting = []
    ahead = maxima(1)
    done = len(ahead) * lead // begin[1]
    plan += ahead[:done] + turns(0)
    nxt = 1
    for i in range(NB):
        for kt in range(TB * (i + 1)):
            for h in range(G):
                plan.append(("score", i, kt, h))
                slot = begin[i] + G * kt + h + 1
                if nxt < NB:
                    upto = len(ahead) * (slot + lead - begin[nxt - 1]) // (begin[nxt] - begin[nxt - 1])
                    plan += ahead[done:upto]
                    done = upto
                    if done == len(ahead):
                        plan.append(("rows", nxt))
                        nxt += 1
                        ahead, done = maxima(nxt) if nxt < NB else [], 0
                left = begin[i + 1] - slot
                if i + 1 < NB and left < G + 1 and left > 0:
                    plan.append(("turn", i + 1, G - left))
                if h == 0 and len(waiting) >= 2:
                    plan += waiting.pop(0)
            waiting.append([("pv", i, kt)] + ([("out", i)] if kt == TB * (i + 1) - 1 else []))
            if i and kt == 2:
                plan.append(("den", i - 1))
            if i and kt == 4:
                plan += [("proj", i - 1, half) for half in range(2)]
    for left in waiting:
        plan += left
    last = NB - 1
    return plan + [("den", last), ("proj", last, 0), ("proj", last, 1)]


def attention_stage(nc, m, w_out, values):
    name = "attn"
    plan = attention_plan()
    max_unit = {ev: n for n, ev in enumerate(e for e in plan if e[0] == "max")}
    act_unit = {ev: n for n, ev in enumerate(e for e in plan if e[0] in ("score", "turn"))}
    ps_unit = {ev: n for n, ev in enumerate(e for e in plan if e in max_unit or e in act_unit)}
    ps_user = list(ps_unit)
    ktg = {(i, kt): n for n, (i, kt) in enumerate((i, kt) for i in range(NB) for kt in range(TB * (i + 1)))}
    QR = 3
    PR = 3
    SR = 6
    with ExitStack() as ctx:
        def sb(n, shape, dt=F32):
            return ctx.enter_context(nc.sbuf_tensor(f"{name}_{n}", shape, dt))

        def ps(n, shape):
            return ctx.enter_context(nc.psum_tensor(f"{name}_{n}", shape, F32))

        K = sb("K", [STACK + 2, G, T], BF16)
        Q = [sb(f"Q{i}", [STACK + 2, G, QB], BF16) for i in range(QR)]
        V = sb("V", [P, NT, G, 32])
        prob = sb("prob", [P, PR, G, QB])
        pmax = sb("pmax", [P, 2, TB * G, NB])
        mx, low = sb("mx", [P, TB * G]), sb("low", [P, TB * G])
        rows = sb("rows", [P, 2, TB * G, 2], BF16)
        oT = sb("oT", [P, 2, QB])
        rden, aT = sb("rden", [P, QB]), sb("aT", [P, QB])
        wo = sb("wo", [P, NG, D])
        spread = sb("spread", [P, P])
        identb = sb("identb", [P, P], BF16)
        mask_q = sb("mask_q", [P, P], BF16)
        mask_k = sb("mask_k", [P, P], BF16)
        psS = ps("psS", [P, SR, QB])
        psO = ps("psO", [P, QB])
        psM = ps("psM", [P, QB])

        with stage(nc, name + "_prep", "filled made wo_in") as (block, s):
            @block.gpsimd
            def _(pool):
                for ap, v in ((wo[:], 0.0), (V[:], 0.0), (spread[:], 0.0),
                              (mask_q[:], 0.0), (mask_k[:], 0.0)):
                    pool.memset(ap, v).then_inc(s.filled, 1)
                pool.wait_ge(s.filled, 5)
                pool.memset(V[:, :, :, DH:DH + 1], 1.0).then_inc(s.made, 1)
                pool.affine_select(out=mask_q[:], in_=mask_q[:], compare_op=ALU.is_ge, fill=FAR_BELOW, base=0,
                                   pattern=[[-1, P]], channel_multiplier=1).then_inc(s.made, 1)
                pool.affine_select(out=mask_k[:], in_=mask_k[:], compare_op=ALU.is_ge, fill=FAR_BELOW, base=0,
                                   pattern=[[1, P]], channel_multiplier=-1).then_inc(s.made, 1)
                pool.affine_select(out=spread[:].rearrange("p (h r) -> p h r", h=G),
                                   in_=spread[:].rearrange("p (h r) -> p h r", h=G),
                                   compare_op=ALU.not_equal, fill=1.0, base=-DH,
                                   pattern=[[-32, G], [0, 32]], channel_multiplier=1).then_inc(s.made, 1)

            @block.vector
            def _(dve):
                nc.vector.tensor_copy(identb[:], m.ident[:]).then_inc(s.made, 1)
                nc.vector.memset(K[STACK:STACK + 2], 1.0).then_inc(s.made, 1)

            @block.sync
            def _(sp):
                sp.wait_ge(s.filled, 1)
                for h in range(G):
                    sp.dma_start(wo[32 * h:32 * h + DH],
                                 w_out.rearrange("(g h d) n -> h d g n", g=NG, h=G)[h]).then_inc(s.wo_in, 16)
                sp.wait_ge(s.wo_in, 16 * G)

        with nc.Fori(0, NG) as g:
            names = " ".join(f"k_in{i}" for i in range(NB))
            with stage(nc, name, names + " q_in0 q_in1 q_in2 v_in s_ready s_used rows_step rows_ready st_ready st_done "
                                         "pv_done out_done den_ready recip_done mul_done proj_ready added")                    as (block, s):
                k_in = s[0:NB]
                q_in = (s.q_in0, s.q_in1, s.q_in2)

                def key_cols(i, kt):
                    return max(0, kt - TB * i) * P

                @block.sync
                def _(sp):
                    for i in range(NB):
                        cols = slice(i * QB, (i + 1) * QB)
                        load_stack(sp, m, 1, bass.ds(g * G, G), K_PART, cols, K[0:STACK, :, cols], k_in[i])
                        if i >= QR:
                            sp.wait_ge(s.st_ready, act_unit["score", i - QR, TB * (i - QR + 1) - 1, G - 1] + 1)
                        load_stack(sp, m, 0, bass.ds(g * G, G), Q_PART, cols, Q[i % QR][0:STACK], q_in[i % QR])

                @block.gpsimd
                def _(pool):
                    for i in range(NB):
                        tiles = slice(i * TB, (i + 1) * TB)
                        for h in range(G):
                            nc.gpsimd.tensor_copy(V[:, tiles, h, 0:DH],
                                                  values[:, tiles, bass.ds(g * G + h, 1), :]
                                                  .rearrange("p t a d -> p t (a d)")).then_inc(s.v_in, 1)
                    for i in range(NB):
                        pool.wait_ge(s.recip_done, i + 1)
                        if i:
                            pool.wait_ge(s.proj_ready, 2 * i)
                        nc.gpsimd.tensor_tensor(aT[:], oT[:, i % 2, :], rden[:], ALU.mult).then_inc(s.mul_done, 1)

                @block.tensor
                def _(pe):
                    for ev in plan:
                        kind, i = ev[0:2]
                        if ev in ps_unit:
                            u = ps_unit[ev]
                            before = ps_user[u - SR] if u >= SR else None
                            if before in max_unit:
                                pe.wait_ge(s.s_used, max_unit[before] + 1)
                            elif before in act_unit:
                                pe.wait_ge(s.st_done, act_unit[before] + 1)
                        if kind == "max":
                            _, i, qt, h, c = ev
                            if (qt, h, c) == (0, 0, 0):
                                pe.wait_ge(q_in[i % QR], stack_loads(Q_PART) * (i // QR + 1))
                                pe.wait_ge(k_in[i], stack_loads(K_PART))
                            n = QB if c < i else (qt + 1) * P
                            diagonal = c == i
                            mm = nc.tensor.matmul(psS[:, u % SR, 0:n], Q[i % QR][0:STACK, h, qt * P:(qt + 1) * P],
                                                  K[0:STACK, h, c * QB:c * QB + n], start=True, stop=not diagonal,
                                                  skip_group_check=True)
                            if diagonal:
                                mm = nc.tensor.matmul(psS[:, u % SR, n - P:n], identb[:], mask_q[:],
                                                      start=False, stop=True, skip_group_check=True)
                            mm.then_inc(s.s_ready, 1)
                        elif kind == "turn":
                            h = ev[2]
                            pe.wait_ge(s.rows_ready, i + 1)
                            for qt in range(TB):
                                mm = nc.tensor.matmul(psS[STACK:STACK + 2, u % SR, qt * P:(qt + 1) * P],
                                                      rows[:, i % 2, qt * G + h, :], identb[:],
                                                      start=True, stop=True)
                            mm.then_inc(s.st_ready, 1)
                        elif kind == "score":
                            _, i, kt, h = ev
                            if kt == 0:
                                pe.wait_ge(s.st_done, act_unit["turn", i, h] + 1)
                            q0 = key_cols(i, kt)
                            diagonal = kt >= TB * i
                            mm = nc.tensor.matmul(psS[:, u % SR, q0:QB], K[:, h, kt * P:(kt + 1) * P],
                                                  Q[i % QR][:, h, q0:QB], start=True, stop=not diagonal,
                                                  skip_group_check=True)
                            if diagonal:
                                mm = nc.tensor.matmul(psS[:, u % SR, q0:q0 + P], identb[:], mask_k[:],
                                                      start=False, stop=True, skip_group_check=True)
                            mm.then_inc(s.st_ready, 1)
                        elif kind == "pv":
                            _, i, kt = ev
                            n = ktg[i, kt]
                            pe.wait_ge(s.st_done, act_unit["score", i, kt, G - 1] + 1)
                            if kt == 0 and i:
                                pe.wait_ge(s.out_done, i)
                            if kt >= TB * i:
                                pe.wait_ge(s.v_in, G * (i + 1))
                            q0 = key_cols(i, kt)
                            for h in range(G):
                                mm = nc.tensor.matmul(psO[32 * h:32 * h + 32, q0:QB], V[:, kt, h, :],
                                                      prob[:, n % PR, h, q0:QB], start=(kt == 0),
                                                      stop=(kt == TB * (i + 1) - 1), skip_group_check=True)
                            mm.then_inc(s.pv_done, 1)
                        elif kind == "den":
                            pe.wait_ge(s.out_done, i + 1)
                            if i:
                                pe.wait_ge(s.added, 2 * i)
                            nc.tensor.matmul(psM[:], spread[:], oT[:, i % 2, :], start=True, stop=True)\
                                .then_inc(s.den_ready, 1)
                        elif kind == "proj":
                            half = ev[2]
                            pe.wait_ge(s.mul_done, i + 1)
                            if half:
                                pe.wait_ge(s.added, 2 * i + 1)
                            for j in range(2):
                                t = half * 2 + j
                                mm = nc.tensor.matmul(psM[:, j * D:(j + 1) * D], aT[:, t * P:(t + 1) * P],
                                                      wo[:, g, :], start=True, stop=True)
                            mm.then_inc(s.proj_ready, 1)

                @block.scalar
                def _(act):
                    for ev in plan:
                        kind, i = ev[0:2]
                        if kind == "score":
                            _, i, kt, h = ev
                            k = ktg[i, kt]
                            n = act_unit[ev]
                            act.wait_ge(s.st_ready, n + 1)
                            if k >= PR and h == 0:
                                act.wait_ge(s.pv_done, k - PR + 1)
                            q0 = key_cols(i, kt)
                            nc.scalar.activation(prob[:, k % PR, h, q0:QB], psS[:, ps_unit[ev] % SR, q0:QB], ACT.Exp,
                                                 scale=DH ** -0.5).then_inc(s.st_done, 1)
                        elif kind == "turn":
                            n = act_unit[ev]
                            act.wait_ge(s.st_ready, n + 1)
                            nc.scalar.copy(Q[i % QR][STACK:STACK + 2, ev[2], :], psS[STACK:STACK + 2, ps_unit[ev] % SR, :])\
                                .then_inc(s.st_done, 1)
                        elif kind == "out":
                            act.wait_ge(s.pv_done, ktg[i, TB * (i + 1) - 1] + 1)
                            if i >= 2:
                                act.wait_ge(s.mul_done, i - 1)
                            nc.scalar.copy(oT[:, i % 2, :], psO[:]).then_inc(s.out_done, 1)

                @block.vector
                def _(dve):
                    for ev in plan:
                        kind, i = ev[0:2]
                        if kind == "max":
                            _, i, qt, h, c = ev
                            u = ps_unit[ev]
                            n = QB if c < i else (qt + 1) * P
                            dve.wait_ge(s.s_ready, max_unit[ev] + 1)
                            nc.vector.tensor_reduce(pmax[:, i % 2, qt * G + h, c:c + 1], psS[:, u % SR, 0:n],
                                                    AX.X, ALU.max).then_inc(s.s_used, 1)
                        elif kind == "rows":
                            dve.wait_ge(s.s_used, max_unit["max", i, TB - 1, G - 1, i] + 1)
                            nc.vector.tensor_reduce(mx[:], pmax[:, i % 2, :, 0:i + 1], AX.X, ALU.max)\
                                .then_inc(s.rows_step, 1)
                            dve.wait_ge(s.rows_step, 3 * i + 1)
                            nc.vector.tensor_scalar(rows[:, i % 2, :, 0], mx[:], -1.0, None, ALU.mult)\
                                .then_inc(s.rows_step, 1)
                            dve.wait_ge(s.rows_step, 3 * i + 2)
                            nc.vector.tensor_tensor(low[:], mx[:], rows[:, i % 2, :, 0], ALU.add)\
                                .then_inc(s.rows_step, 1)
                            dve.wait_ge(s.rows_step, 3 * i + 3)
                            nc.vector.tensor_scalar(rows[:, i % 2, :, 1], low[:], -1.0, None, ALU.mult)\
                                .then_inc(s.rows_ready, 1)
                        elif kind == "den":
                            dve.wait_ge(s.den_ready, i + 1)
                            if i:
                                dve.wait_ge(s.mul_done, i)
                            nc.vector.reciprocal(rden[:], psM[:]).then_inc(s.recip_done, 1)
                        elif kind == "proj":
                            half = ev[2]
                            dve.wait_ge(s.proj_ready, 2 * i + half + 1)
                            t = i * TB + half * 2
                            nc.vector.tensor_tensor(m.x[:, t:t + 2, :], psM[:].rearrange("p (t d) -> p t d", t=2),
                                                    m.x[:, t:t + 2, :], ALU.add).then_inc(s.added, 1)


def causal(nc, m, i):
    with ExitStack() as ctx:
        values = ctx.enter_context(nc.sbuf_tensor("causal_values", [P, NT, H, DH], F32))
        norm_and_values_stage(nc, m, "causal_norm", i["L1_attn_WV"], values)
        split_stage(nc, m, "causal_split", (i["L1_attn_WQ"], i["L1_attn_WK"]))
        attention_stage(nc, m, i["L1_attn_WO"], values)



MF = 64
PAIRS = H // 2
VW = DH + 1


def favor_stage(nc, m, projT, values, out_w, out_b, stats):
    name = "favor"
    LB = 2 * P
    BODY = 4
    with ExitStack() as ctx:
        def sb(n, shape, dt=F32):
            return ctx.enter_context(nc.sbuf_tensor(f"{name}_{n}", shape, dt))

        def ps(n, shape):
            return ctx.enter_context(nc.psum_tensor(f"{name}_{n}", shape, F32))

        R = STACK + 3
        qs = [sb(f"qs{i}", [R, H, LB], BF16) for i in range(2)]
        ks = [sb(f"ks{i}", [R, H, LB], BF16) for i in range(2)]
        fw = sb("fw", [R, MF], BF16)
        pt, pr = sb("pt", [DH, MF]), sb("pr", [DH, MF])
        pp = sb("pp", [DH, 3, MF], BF16)
        qfT = sb("qfT", [P, 2, PAIRS, P])
        kfT = sb("kfT", [P, 2, PAIRS, P])
        kf = sb("kf", [P, 2, H, MF])
        a = sb("a", [P, H, P])
        mask = sb("mask", [P, P])
        vt = sb("vt", [P, 2, H, 32])
        state = sb("state", [P, 2, H, 32])
        oT, rden, aT = sb("oT", [P, 4 * P]), sb("rden", [P, 4 * P]), sb("aT", [P, 4 * P])
        wo = sb("wo", [P, H // 4, D])
        spread = sb("spread", [P, P])
        ob, xb = sb("ob", [P, D]), sb("xb", [P, 2, D])
        mean, rstd = stats
        psF = ps("psF", [P, 3, 512])
        psA = ps("psA", [P, 2, 4, P])
        psN = ps("psN", [P, 4, P])
        psD = ps("psD", [P, 512])
        psM = ps("psM", [P, 512])

        with stage(nc, name + "_prep", "p_in step moved filled made w_in") as (block, s):
            @block.sync
            def _(sp):
                sp.dma_start(pt[:], projT).then_inc(s.p_in, 16)
                sp.wait_ge(s.step, 5)
                for r, part in enumerate(K_PART):
                    sp.dma_start(fw[r * DH:(r + 1) * DH, :], pp[:, part, :]).then_inc(s.moved, 16)
                sp.dma_start(ob[:], out_b.partition_broadcast(P)).then_inc(s.w_in, 16)
                sp.wait_ge(s.filled, 1)
                for h in range(4):
                    sp.dma_start(wo[32 * h:32 * h + DH],
                                 out_w.rearrange("(g h d) n -> h d g n", g=H // 4, h=4)[h]).then_inc(s.w_in, 16)
                sp.wait_ge(s.moved, 16 * len(K_PART))
                sp.wait_ge(s.w_in, 16 * 5)

            @block.gpsimd
            def _(pool):
                for ap, v in ((wo[:], 0.0), (mask[:], 1.0), (state[:], 0.0), (vt[:], 0.0), (spread[:], 0.0)):
                    pool.memset(ap, v).then_inc(s.filled, 1)
                pool.wait_ge(s.filled, 5)
                pool.memset(vt[:, :, :, DH:DH + 1], 1.0).then_inc(s.made, 1)
                pool.affine_select(out=mask[:], in_=mask[:], compare_op=ALU.is_ge, fill=0.0, base=0,
                                   pattern=[[1, P]], channel_multiplier=-1).then_inc(s.made, 1)
                pool.affine_select(out=spread[:].rearrange("p (h r) -> p h r", h=4),
                                   in_=spread[:].rearrange("p (h r) -> p h r", h=4),
                                   compare_op=ALU.not_equal, fill=1.0, base=-DH,
                                   pattern=[[-32, 4], [0, 32]], channel_multiplier=1).then_inc(s.made, 1)

            @block.vector
            def _(dve):
                link = Steps(dve, s.step)
                dve.wait_ge(s.p_in, 16)
                link(nc.vector.tensor_scalar(pt[:], pt[:], DH ** -0.5, None, ALU.mult))
                link(nc.vector.tensor_copy(pp[:, 0, :], pt[:]))
                link(nc.vector.tensor_tensor(pr[:], pt[:], pp[:, 0, :], ALU.subtract))
                link(nc.vector.tensor_copy(pp[:, 1, :], pr[:]))
                link(nc.vector.tensor_tensor(pp[:, 2, :], pr[:], pp[:, 1, :], ALU.subtract))
                nc.vector.memset(fw[STACK:STACK + 3, :], -1.0).then_inc(s.made, 1)

        with stage(nc, name, "in0 in1 f_ready f_exp a_ready a_masked d_ready d_added num_ready v_moved o_out "
                             "den_ready recip_done mul_done proj_ready normed based added") as (block, s):
            stacks_in = (s.in0, s.in1)
            per_load = 2 * (stack_loads(Q_PART) + 16)

            @block.sync
            def _(sp):
                def loads(blk, i):
                    cols = bass.ds(blk * LB, LB)
                    for which, dst in ((0, qs), (1, ks)):
                        load_stack(sp, m, which, slice(0, H), Q_PART, cols, dst[i], stacks_in[i])
                        sp.dma_start(dst[i][STACK:], m.stacks[which, :, 3 * DH:, cols]
                                     .rearrange("h r n -> r h n")).then_inc(stacks_in[i], 16)

                loads(0, 0)
                loads(1, 1)
                with sp.Fori(1, NT // BODY) as turn:
                    for i in range(2):
                        sp.wait_ge(s.f_ready, turn * (6 * BODY) - (6 * BODY - 12 * (i + 1)))
                        loads(turn * 2 + i, i)

            @block.tensor
            def _(pe):
                pe.sem_inc(s.f_exp, 3)
                pe.sem_inc(s.a_masked, 2)
                pe.sem_inc(s.num_ready, 2)
                pe.sem_inc(s.d_added, 2)
                pe.sem_inc(s.added, 2)

                def features(t, j, u):
                    pe.wait_ge(s.f_exp, t * 6 + (u + 1))
                    half, kind = u // 3, u % 3
                    cols = slice((j % 2) * P, (j % 2 + 1) * P)
                    for n in range(4 if kind < 2 else 8):
                        if kind < 2:
                            src = (qs, ks)[kind][j // 2]
                            for b in range(2):
                                last = nc.tensor.matmul(psF[64 * b:64 * b + 64, u % 3, n * P:(n + 1) * P], fw[:],
                                                        src[:, 2 * (4 * half + n) + b, cols], start=True, stop=True)
                        else:
                            last = nc.tensor.matmul(psF[:, u % 3, n * MF:(n + 1) * MF],
                                                    ks[j // 2][:, 8 * half + n, cols], fw[:], start=True, stop=True)
                    last.then_inc(s.f_ready, 1)

                def products(t, j, half):
                    pe.wait_ge(s.f_exp, t * 6 + (3 * half + 2 + 3))
                    pe.wait_ge(s.a_masked, t * 4 + (2 * half + 2))
                    for n in range(4):
                        for b in range(2):
                            rows = slice(64 * b, 64 * b + 64)
                            last = nc.tensor.matmul(psA[:, b, n, :], kfT[rows, j % 2, 4 * half + n, :],
                                                    qfT[rows, j % 2, 4 * half + n, :], start=True, stop=True)
                            if n == 3:
                                last.then_inc(s.a_ready, 1)

                def tile_sums(t, j):
                    pe.wait_ge(s.f_exp, t * 6 + (6 + 3))
                    pe.wait_ge(s.d_added, t * 2 + 2)
                    pe.wait_ge(s.v_moved, t + 1)
                    for p in range(PAIRS):
                        last = nc.tensor.matmul(psD[:, p * 2 * VW:(p + 1) * 2 * VW], kf[:, j % 2, 2 * p:2 * p + 2, :],
                                                vt[:, j % 2, 2 * p:2 * p + 2, 0:VW], start=True, stop=True)
                    last.then_inc(s.d_ready, 1)

                def outputs(t, j):
                    pe.wait_ge(s.a_masked, t * 4 + 6)
                    for h in range(H):
                        nc.tensor.matmul(psN[32 * (h % 4):32 * (h % 4) + 32, h // 4, :], vt[:, j % 2, h, :],
                                         a[:, h, :], start=(h < 4), stop=False, skip_group_check=True)
                    for h in range(H):
                        last = nc.tensor.matmul(psN[32 * (h % 4):32 * (h % 4) + 32, h // 4, :],
                                                state[:, j % 2, h, :], qfT[:, j % 2, h // 2, :],
                                                start=False, stop=True, skip_group_check=True)
                    last.then_inc(s.num_ready, 1)

                def divisors(t):
                    pe.wait_ge(s.o_out, t + 1)
                    pe.wait_ge(s.added, t + 2)
                    nc.tensor.matmul(psM[:], spread[:], oT[:], start=True, stop=True).then_inc(s.den_ready, 1)

                def projection(t):
                    pe.wait_ge(s.mul_done, t + 1)
                    for g in range(4):
                        last = nc.tensor.matmul(psM[:, 0:D], aT[:, g * P:(g + 1) * P], wo[:, g, :],
                                                start=(g == 0), stop=(g == 3))
                    last.then_inc(s.proj_ready, 1)

                def tile(turn, j, first, last):
                    t = turn * BODY + j
                    following = (j + 1) % BODY

                    def next_features(u):
                        if not last:
                            features(t + 1, following, u)

                    if not last and following % 2 == 0:
                        pe.wait_ge(stacks_in[following // 2], (turn + (j + 1) // BODY) * per_load + per_load)
                    next_features(0)
                    products(t, j, 0)
                    if not first:
                        divisors(t - 1)
                    next_features(1)
                    next_features(2)
                    products(t, j, 1)
                    next_features(3)
                    tile_sums(t, j)
                    next_features(4)
                    if not first:
                        projection(t - 1)
                    next_features(5)
                    outputs(t, j)

                pe.wait_ge(stacks_in[0], per_load)
                for u in range(6):
                    features(0, 0, u)
                for j in range(BODY):
                    tile(0, j, j == 0, False)
                with pe.Fori(1, NT // BODY - 1) as turn:
                    for j in range(BODY):
                        tile(turn, j, False, False)
                for j in range(BODY):
                    tile(NT // BODY - 1, j, False, j == BODY - 1)
                divisors(NT - 1)
                projection(NT - 1)

            @block.scalar
            def _(act):
                def outputs_out(t):
                    act.wait_ge(s.num_ready, t + 3)
                    nc.scalar.copy(oT[:], psN[:].rearrange("p g n -> p (g n)")).then_inc(s.o_out, 1)

                def tiles(turn, first):
                    for j in range(BODY):
                        t = turn * BODY + j
                        for u in range(6):
                            half, kind = u // 3, u % 3
                            act.wait_ge(s.f_ready, t * 6 + (u + 1))
                            if u == 0:
                                act.wait_ge(s.num_ready, t + 1)
                            dst = (qfT, kfT)[kind][:, j % 2, 4 * half:4 * half + 4, :] if kind < 2 else \
                                kf[:, j % 2, 8 * half:8 * half + 8, :]
                            nc.scalar.activation(dst, psF[:, u % 3, :].rearrange(
                                "p (a b) -> p a b", a=4 if kind < 2 else 8), ACT.Exp).then_inc(s.f_exp, 1)
                        if j or not first:
                            outputs_out(t - 1)

                tiles(0, True)
                with act.Fori(1, NT // BODY) as turn:
                    tiles(turn, False)
                outputs_out(NT - 1)

            @block.gpsimd
            def _(pool):
                def values_in(t, j):
                    pool.wait_ge(s.num_ready, t + 1)
                    nc.gpsimd.tensor_copy(vt[:, j % 2, :, 0:DH], values[:, t, :, :]).then_inc(s.v_moved, 1)

                def divided(t, j):
                    pool.wait_ge(s.recip_done, t + 1)
                    nc.gpsimd.tensor_tensor(aT[:], oT[:], rden[:], ALU.mult).then_inc(s.mul_done, 1)
                    pool.wait_ge(s.normed, t + 1)
                    nc.gpsimd.tensor_tensor(xb[:, j % 2, :], xb[:, j % 2, :], ob[:], ALU.add).then_inc(s.based, 1)

                def tiles(turn, first):
                    for j in range(BODY):
                        t = turn * BODY + j
                        values_in(t, j)
                        if j or not first:
                            divided(t - 1, j - 1)

                tiles(0, True)
                with pool.Fori(1, NT // BODY) as turn:
                    tiles(turn, False)
                divided(NT - 1, NT - 1)

            @block.vector
            def _(dve):
                def divisors(t, j):
                    dve.wait_ge(s.den_ready, t + 1)
                    nc.vector.reciprocal(rden[:], psM[:]).then_inc(s.recip_done, 1)
                    dve.wait_ge(s.added, t + 1)
                    nc.vector.tensor_scalar(xb[:, j % 2, :], m.x[:, t, :], mean[:, bass.ds(t, 1)],
                                            rstd[:, bass.ds(t, 1)], ALU.subtract, ALU.mult).then_inc(s.normed, 1)

                def added(t, j):
                    dve.wait_ge(s.proj_ready, t + 1)
                    dve.wait_ge(s.based, t + 1)
                    nc.vector.tensor_tensor(m.xn[:, t, :], psM[:, 0:D], xb[:, j % 2, :], ALU.add)\
                        .then_inc(s.added, 1)

                def turns(turn, first):
                    for j in range(BODY):
                        t = turn * BODY + j
                        dve.wait_ge(s.num_ready, t + 2)
                        for half in range(2):
                            for b in range(2):
                                dve.wait_ge(s.a_ready, t * 4 + (2 * half + b + 1))
                                nc.vector.tensor_tensor(a[:, 8 * half + b:8 * half + 8:2, :], psA[:, b],
                                                        bc(mask[:].unsqueeze(1), [P, 4, P]), ALU.mult)\
                                    .then_inc(s.a_masked, 1)
                            if half == 0 and (j or not first):
                                divisors(t - 1, j - 1)
                        dve.wait_ge(s.d_ready, t + 1)
                        for b in range(2):
                            rows, cols = slice(64 * b, 64 * b + 64), slice(VW * b, VW * b + VW)
                            nc.vector.tensor_tensor(state[rows, (j + 1) % 2, b::2, 0:VW], state[rows, j % 2, b::2, 0:VW],
                                                    psD[rows, 0:PAIRS * 2 * VW].rearrange(
                                                        "p (a b) -> p a b", a=PAIRS)[:, :, cols],
                                                    ALU.add).then_inc(s.d_added, 1)
                        if j or not first:
                            added(t - 1, j - 1)

                turns(0, True)
                with dve.Fori(1, NT // BODY) as turn:
                    turns(turn, False)
                divisors(NT - 1, NT - 1)
                added(NT - 1, NT - 1)


def favor_norm_stage(nc, m, gamma_dram, beta_dram):
    name = "favor_norm"
    YR = 4
    with ExitStack() as ctx:
        def sb(n, shape, dt=F32):
            return ctx.enter_context(nc.sbuf_tensor(f"{name}_{n}", shape, dt))

        b = norm_buffers(nc, ctx, name)
        gamma, beta, y = sb("gamma", [P, D]), sb("beta", [P, D]), sb("y", [P, YR, D])
        with stage(nc, name, "w_in stats stat_step var_ready root_ready normed scaled based added") as (block, s):
            @block.sync
            def _(sp):
                sp.dma_start(gamma[:], gamma_dram.partition_broadcast(P)).then_inc(s.w_in, 16)
                sp.dma_start(beta[:], beta_dram.partition_broadcast(P)).then_inc(s.w_in, 16)

            @block.scalar
            def _(act):
                act.wait_ge(s.var_ready, 1)
                nc.scalar.activation(b.rstd[:], b.t1[:], ACT.Sqrt).then_inc(s.root_ready, 1)

            @block.gpsimd
            def _(pool):
                pool.wait_ge(s.w_in, 32)
                with pool.Fori(0, NT // YR) as g:
                    for j in range(YR):
                        t = g * YR + j
                        nc.gpsimd.tensor_tensor(m.x[:, t, :], m.x[:, t, :], beta[:], ALU.add).then_inc(s.based, 1)

            @block.vector
            def _(dve):
                norm_statistics(nc, dve, s, m, b, src=m.xn, eps=1e-6)
                dve.wait_ge(s.w_in, 32)
                dve.sem_inc(s.added, YR)
                with dve.Fori(0, NT // YR) as g:
                    for j in range(YR):
                        t = g * YR + j
                        dve.wait_ge(s.added, t + 1)
                        nc.vector.tensor_scalar(y[:, j, :], m.xn[:, t, :], b.mean[:, bass.ds(t, 1)],
                                                b.rstd[:, bass.ds(t, 1)], ALU.subtract, ALU.mult)\
                            .then_inc(s.normed, 1)
                    for j in range(YR):
                        dve.wait_ge(s.normed, g * YR + (j + 1))
                        nc.vector.tensor_tensor(y[:, j, :], y[:, j, :], gamma[:], ALU.mult).then_inc(s.scaled, 1)
                    for j in range(YR):
                        t = g * YR + j
                        dve.wait_ge(s.scaled, t + 1)
                        dve.wait_ge(s.based, t + 1)
                        nc.vector.tensor_tensor(m.x[:, t, :], m.x[:, t, :], y[:, j, :], ALU.add).then_inc(s.added, 1)


def favor(nc, m, i):
    with ExitStack() as ctx:
        mean = ctx.enter_context(nc.sbuf_tensor("favor_mean", [P, NT], F32))
        rstd = ctx.enter_context(nc.sbuf_tensor("favor_rstd", [P, NT], F32))
        with nc.sbuf_tensor("favor_values", [P, NT, H, DH], F32) as values:
            norm_and_values_stage(nc, m, "favor_in", i["L0_attn_v_w"], values, i["L0_attn_v_b"], (mean, rstd))
            split_stage(nc, m, "favor_split", (i["L0_attn_q_w"], i["L0_attn_k_w"]),
                        (i["L0_attn_q_b"], i["L0_attn_k_b"]))
            favor_stage(nc, m, i["L0_attn_proj"], values, i["L0_attn_out_w"], i["L0_attn_out_b"], (mean, rstd))
        favor_norm_stage(nc, m, i["L0_attn_gamma"], i["L0_attn_beta"])



Ffn = namedtuple("Ffn", "name router router_b up up_b down down_b")
STAGES = (0, 1, 2, 3, 4, 5)


def build(nc, i, out):
    with ExitStack() as ctx:
        m = make_constants(nc, ctx)
        m.slots = nc.dram_tensor("slots", [E * TOP2_CAP, D], F32).ap()
        m.outs = nc.dram_tensor("expert_outs", [E * TOP2_CAP, D], F32).ap()
        m.stacks = nc.dram_tensor("qk_stacks", [2, H, 3 * DH + 3, T], BF16).ap()
        constants_stage(nc, m, i["L0_attn_x"])
        zero_slots_stage(nc, m)

        def switch(name):
            ffn(nc, m, Ffn(name=name, router=i["L0_ffn_w_switch"], router_b=i["L0_ffn_b_switch"],
                                       up=[i["L0_ffn_w1"]], up_b=i["L0_ffn_b1"], down=i["L0_ffn_w2"],
                                       down_b=i["L0_ffn_b2"]), False)

        def top2(name):
            ffn(nc, m, Ffn(name=name, router=i["L1_ffn_router_w"], router_b=None,
                             up=[i["L1_ffn_wg"], i["L1_ffn_wu"]], up_b=None, down=i["L1_ffn_wd"],
                             down_b=None), True)

        parts = [lambda: switch("switch_a"), lambda: favor(nc, m, i), lambda: switch("switch_b"),
                 lambda: top2("top2_a"), lambda: causal(nc, m, i), lambda: top2("top2_b")]
        for n in STAGES:
            parts[n]()
        store_stage(nc, m, out)


_TURNED = ("L1_ffn_router_w", "L1_attn_WQ", "L1_attn_WK", "L1_attn_WV", "L1_attn_WO", "L0_attn_proj")


def kernel(**inputs):
    import numpy as _np
    import concourse.bacc as _bacc
    from concourse import mybir as _mybir
    from concourse.bass_utils import run_bass_kernel_spmd as _run

    nc = _bacc.Bacc("TRN2", target_bir_lowering=False, num_devices=1)
    arrays, aps = {}, {}
    for name, value in inputs.items():
        a = _np.asarray(value)
        a = _np.ascontiguousarray(a.T if name in _TURNED else a)
        arrays[f"in_{name}"] = a
        aps[name] = nc.dram_tensor(f"in_{name}", a.shape, _mybir.dt.from_np(a.dtype), kind="ExternalInput").ap()
    out = nc.dram_tensor("out", (1, T, D), _mybir.dt.float32, kind="ExternalOutput").ap()
    build(nc, aps, out)
    return _run(nc, [arrays], core_ids=[0]).results[0]["out"]
```

```python
from collections import namedtuple
from contextlib import ExitStack, contextmanager

import concourse.bass as bass
from concourse import mybir

ALU = mybir.AluOpType
ACT = mybir.ActivationFunctionType
AX = mybir.AxisListType
F32 = mybir.dt.float32
BF16 = mybir.dt.bfloat16
F32R = mybir.dt.float32r
U32 = mybir.dt.uint32
I32 = mybir.dt.int32

P = 128
T = 4096
D = 256
NT = T // P
KC = D // P
F = 1024
FC = F // P
E = 8
FETCH = 8
FAR = 65536
SWITCH_CAP = int(0.5 * T / E)
TOP2_CAP = int(1.25 * T / E)


@contextmanager
def stage(nc, name, sems):
    with ExitStack() as ctx:
        s = namedtuple("Semaphores", sems)(*(ctx.enter_context(nc.semaphore(f"{name}_{n}")) for n in sems.split()))
        with nc.Block() as block:
            yield block, s
        for one in s:
            nc.sync.sem_clear(one)
        nc.all_engine_barrier()


def pool_semaphore(m, n, increments):
    past = m.pool_past[n]
    m.pool_past[n] += 16 * increments
    return m.pool_dma[n], past


def bc(ap, shape):
    return ap.to_broadcast(shape)



class Memory:
    pass


def make_constants(nc, ctx):
    def sb(name, shape, dt):
        return ctx.enter_context(nc.sbuf_tensor(name, shape, dt))

    m = Memory()
    m.x = sb("x_stream", [P, NT, D], F32)
    m.xn = sb("x_normed", [P, NT, D], F32)
    m.ident = sb("ident", [P, P], F32)
    m.ones = sb("ones_bf", [P, P], BF16)
    m.upto = sb("upto_bf", [P, P], BF16)
    m.eidx8 = sb("eidx8", [P, E], F32)
    m.bits = sb("bits", [P, 4, 1], U32)
    m.pool_dma = [ctx.enter_context(nc.semaphore(f"pool_dma{n}")) for n in range(4)]
    m.pool_past = [0] * len(m.pool_dma)
    return m


def constants_stage(nc, m):
    with stage(nc, "const", "filled made") as (block, s):
        @block.gpsimd
        def _(pool):
            pool.memset(m.ident[:], 0.0).then_inc(s.filled, 1)
            pool.memset(m.ones[:], 1.0).then_inc(s.filled, 1)
            pool.memset(m.upto[:], 1.0).then_inc(s.filled, 1)
            pool.wait_ge(s.filled, 3)
            pool.affine_select(out=m.ident[:], in_=m.ident[:], compare_op=ALU.not_equal, fill=1.0, base=0,
                               pattern=[[-1, P]], channel_multiplier=1).then_inc(s.made, 1)
            pool.affine_select(out=m.upto[:], in_=m.upto[:], compare_op=ALU.is_ge, fill=0.0, base=0,
                               pattern=[[1, P]], channel_multiplier=-1).then_inc(s.made, 1)
            pool.iota(m.eidx8[:], pattern=[[1, E]], base=-E, channel_multiplier=0,
                      allow_small_or_imprecise_dtypes=True).then_inc(s.made, 1)
            pool.wait_ge(s.made, 3)


def token_tiles(dram, n):
    return dram.rearrange("b (t p) d -> (b p) t d", p=P)[:, n * FETCH:(n + 1) * FETCH, :]



def norm_statistics(nc, dve, s, m, b, eps=1e-5, arrivals=(), gathered=False):
    n = 0

    def link(ins):
        nonlocal n
        n += 1
        ins.then_inc(s.stat_step, 1)
        dve.wait_ge(s.stat_step, n)

    def tiles(g):
        for j in range(RING):
            t = g * RING + j
            nc.vector.bn_stats(b.stats[:, t, :], m.x[:, t, :]).then_inc(s.stats, 1)

    if arrivals:
        for g, arrived in enumerate(arrivals):
            dve.wait_ge(arrived, 16)
            tiles(g)
    elif not gathered:
        with dve.Fori(0, NT // RING) as g:
            tiles(g)
    if not gathered:
        dve.wait_ge(s.stats, NT)
    mean_e, m2_e, mean_o, m2_o = (b.stats[:, :, i] for i in (1, 2, 4, 5))
    link(nc.vector.tensor_tensor(b.mean[:], mean_e, mean_o, ALU.add))
    link(nc.vector.tensor_scalar(b.mean[:], b.mean[:], 0.5, None, ALU.mult))
    link(nc.vector.tensor_tensor(b.t0[:], mean_e, mean_o, ALU.subtract))
    link(nc.vector.tensor_tensor(b.t0[:], b.t0[:], b.t0[:], ALU.mult))
    link(nc.vector.tensor_tensor(b.t1[:], m2_e, m2_o, ALU.add))
    link(nc.vector.tensor_scalar(b.t1[:], b.t1[:], 1.0 / D, eps, ALU.mult, ALU.add))
    link(nc.vector.scalar_tensor_tensor(out=b.var[:], in0=b.t0[:], scalar=0.25, in1=b.t1[:],
                                        op0=ALU.mult, op1=ALU.add))
    link(nc.vector.reciprocal(b.t1[:], b.var[:]))
    nc.vector.nop().then_inc(s.var_ready, 1)
    dve.wait_ge(s.root_ready, 1)
    link(nc.vector.tensor_tensor(b.t0[:], b.rstd[:], b.rstd[:], ALU.mult))
    link(nc.vector.tensor_tensor(b.t0[:], b.t0[:], b.var[:], ALU.mult))
    link(nc.vector.tensor_scalar(b.t0[:], b.t0[:], -0.5, 1.5, ALU.mult, ALU.add))
    link(nc.vector.tensor_tensor(b.rstd[:], b.rstd[:], b.t0[:], ALU.mult))


RING = 8
XR = 4
LEAD = 2

NORM_SEMS = "stats stat_step var_ready root_ready normed transposed kept xT_ready projected"


NormBuffers = namedtuple("NormBuffers", "stats mean var rstd t0 t1 tile xT")


def norm_buffers(nc, ctx, name):
    def sb(n, shape, dt=F32):
        return ctx.enter_context(nc.sbuf_tensor(f"{name}_{n}", shape, dt))

    return NormBuffers(
        stats=sb("stats", [P, NT, 6]), mean=sb("mean", [P, NT]), var=sb("var", [P, NT]),
        rstd=sb("rstd", [P, NT]), t0=sb("t0", [P, NT]), t1=sb("t1", [P, NT]),
        tile=sb("tile", [P, RING, D]), xT=sb("xT", [P, XR, D]))


def norm_loop_dve(nc, dve, s, m, b):
    with dve.Fori(0, NT // RING) as g:
        for j in range(RING):
            t = g * RING + j
            dve.wait_ge(s.transposed, t + 1)
            for out, sem in ((b.tile[:, j, :], s.normed), (m.xn[:, t, :], s.kept)):
                nc.vector.tensor_scalar(out, m.x[:, t, :], b.mean[:, bass.ds(t, 1)], b.rstd[:, bass.ds(t, 1)],
                                        ALU.subtract, ALU.mult).then_inc(sem, 1)


def norm_loop_act(nc, act, s, b, psT, keeps_turned=False, extra=None):
    act.wait_ge(s.var_ready, 1)
    nc.scalar.activation(b.rstd[:], b.t1[:], ACT.Sqrt).then_inc(s.root_ready, 1)

    def tiles(g, first):
        for j in range(RING):
            t = g * RING + j
            act.wait_ge(s.transposed, t + 1 + RING)
            act.wait_ge(s.projected, t + 1)
            if keeps_turned:
                act.wait_ge(s.kept, t + (RING + 1 - XR))
            nc.scalar.copy(b.xT[:, j % XR], psT[:, j % XR, 0:D]).then_inc(s.xT_ready, 1)
            if extra and j == RING // 2 - 1 and not first:
                extra(g - 1, 1)
            if extra and j == RING - 1:
                extra(g, 0)

    tiles(0, True)
    with act.Fori(1, NT // RING) as g:
        tiles(g, False)
    if extra:
        extra(NT // RING - 1, 1)


def norm_loop_pe(nc, pe, s, m, b, psT, project):
    pe.sem_inc(s.transposed, RING)
    pe.sem_inc(s.projected, XR)

    def transposes(t, j):
        pe.wait_ge(s.normed, t + 1)
        for k in range(KC):
            last = nc.tensor.transpose(psT[:, j % XR, k * P:(k + 1) * P], b.tile[:, j, k * P:(k + 1) * P],
                                       m.ident[:])
        last.then_inc(s.transposed, 1)

    def projection(g, j):
        pe.wait_ge(s.xT_ready, g * RING + (j + 1))
        project(g, j).then_inc(s.projected, 1)

    def tiles(g, last):
        for j in range(RING):
            if not last or j + LEAD < RING:
                transposes(g * RING + (j + LEAD), (j + LEAD) % RING)
            projection(g, j)

    for t in range(LEAD):
        transposes(t, t)
    with pe.Fori(0, NT // RING - 1) as g:
        tiles(g, False)
    tiles(NT // RING - 1, True)



class Steps:

    def __init__(self, eng, sem):
        self.eng, self.sem, self.n = eng, sem, 0

    def __call__(self, ins):
        self.n += 1
        ins.then_inc(self.sem, 1)
        self.eng.wait_ge(self.sem, self.n)


def first_hot(nc, link, hot, values, top, t3, t1, eidx8):
    full = [P, NT, E]
    link(nc.vector.tensor_tensor(t3, values, bc(top.unsqueeze(2), full), ALU.is_equal))
    link(nc.vector.tensor_tensor(t3, t3, bc(eidx8.unsqueeze(1), full), ALU.mult))
    link(nc.vector.tensor_reduce(t1, t3, AX.X, ALU.min))
    link(nc.vector.tensor_tensor(hot, bc(eidx8.unsqueeze(1), full), bc(t1.unsqueeze(2), full), ALU.is_equal))


def route_stage(nc, m, w, top2, x_in):
    K = 2 if top2 else 1
    cap = TOP2_CAP if top2 else SWITCH_CAP
    name = w.name
    first = x_in is not None
    with ExitStack() as ctx:
        def sb(n, shape, dt=F32):
            return ctx.enter_context(nc.sbuf_tensor(f"{name}_{n}", shape, dt))

        b = norm_buffers(nc, ctx, name)
        wr = sb("wr", [P, KC, 32])
        turned = sb("turned", [P, NT // 4, P])
        br = sb("br", [P, E])
        lg = sb("lg", [P, NT, E])
        ex = sb("ex", [P, NT, E])
        t3 = sb("t3", [P, NT, E])
        hots = [sb(f"hot{k}", [P, NT, E], BF16) for k in range(K)]
        top = [sb(f"top{k}", [P, NT]) for k in range(K)]
        r0, r1 = sb("r0", [P, NT]), sb("r1", [P, NT])
        NS = E * cap // P
        KT = K * NT
        place = sb("slot_of", [P, KT], U32)
        part_u, part = sb("part_u", [P, KT], U32), sb("part", [P, KT])
        col_u, col = sb("col_u", [P, KT], U32), sb("col", [P, KT])
        lane, lanes = sb("lane", [P, 1]), sb("lanes", [P, P])
        tile_of = sb("tile_of", [P, KT])
        part_hot = sb("part_hot", [P, KT, P], BF16)
        col_hot = sb("col_hot", [P, KT, 3, NS], BF16)
        found = sb("found", [P, 3, NS])
        token, goes = sb("token", [P, NS]), sb("goes", [P, NS])
        zeros = sb("zeros", [P, FETCH, D]) if first else None
        count_in = sb("count_in", [P, NT, E], BF16)
        scanned = sb("scanned", [P, E, NT])
        restart = sb("restart", [P, E, NT])
        keep = sb("keep", [P, NT, E])
        wt = sb("wt", [P, NT, E])
        ebase = sb("ebase", [P, E])
        cnt = sb("cnt", [P, E])
        cur, cand = sb("cur", [P, 1, E]), sb("cand", [P, 4, E])
        above, counts_of = sb("above", [P, 3, NT, E], BF16), sb("counts_of", [P, 3, E])
        psT = ctx.enter_context(nc.psum_tensor(f"{name}_psT", [P, XR, 512], F32))
        psR = ctx.enter_context(nc.psum_tensor(f"{name}_psR", [P, 2, 512], F32))
        psL = psT[:, 2:4, :].rearrange("p b (t e) -> p (b t) e", e=32)
        psC = ctx.enter_context(nc.psum_tensor(f"{name}_psC", [P, 2, NT, E], F32))
        psP, psS = psC[:, 0], psC[:, 1]
        psB = psT[:, 1:4, 0:NT * E]
        psF = psT[:, 0, 0:3 * NS].rearrange("p (a n) -> p a n", a=3)
        full = [P, NT, E]
        turn = 5
        ROUNDS = 15

        with stage(nc, name, NORM_SEMS + " w_in made step to_exp exped asked counted asked_bit "
                                         "counted_bit bit_step hot table_made stored zeroed w_padded read turned_back x_in0 x_in1 x_in2 x_in3") as (block, s):
            def prefix(dve, link, asked):
                dve.wait_ge(s.counted, asked)
                sums = psS.rearrange("p t e -> p e t")
                link(nc.vector.tensor_copy(scanned[:], sums))
                link(nc.vector.tensor_tensor_scan(lg[:].rearrange("p t e -> p (t e)"),
                                                  restart[:].rearrange("p e t -> p (e t)"),
                                                  scanned[:].rearrange("p e t -> p (e t)"), 0.0,
                                                  ALU.mult, ALU.add))
                tiles = lg[:].rearrange("p t e -> p (t e)").rearrange("p (e t) -> p t e", e=E)
                link(nc.vector.tensor_tensor(t3[:], tiles, psS, ALU.subtract))
                link(nc.vector.tensor_tensor(t3[:], t3[:], psP, ALU.add))

            arrivals = (s.x_in0, s.x_in1, s.x_in2, s.x_in3) if first else ()

            @block.sync
            def _(sp):
                for f, arrived in enumerate(arrivals):
                    sp.dma_start(m.x[:, f * FETCH:(f + 1) * FETCH, :], token_tiles(x_in, f)).then_inc(arrived, 16)
                sp.wait_ge(s.w_padded, 1)
                sp.dma_start(wr[:, :, 0:E], w.router.rearrange("(k p) e -> p k e", p=P)).then_inc(s.w_in, 16)
                if not top2:
                    sp.dma_start(br[:], w.router_b.partition_broadcast(P)).then_inc(s.w_in, 16)
                copies = [m.tokens] if top2 else [m.tokens, m.outs[0:T, :]]
                for f in range(NT // FETCH):
                    tiles = slice(f * FETCH, (f + 1) * FETCH)
                    rows = slice(f * FETCH * P, (f + 1) * FETCH * P)
                    sp.wait_ge(s.kept, (f + 1) * FETCH)
                    for dst in copies:
                        sp.dma_start(dst[rows, :].rearrange("(t p) d -> p t d", p=P), m.xn[:, tiles, :])\
                            .then_inc(s.stored, 16)
                if first:
                    sp.wait_ge(s.zeroed, 1)
                    for f in range(NT // FETCH):
                        rows = slice(T + f * FETCH * P, T + (f + 1) * FETCH * P)
                        sp.dma_start(m.outs[rows, :].rearrange("(t p) d -> p t d", p=P), zeros[:])\
                            .then_inc(s.stored, 16)
                sp.wait_ge(s.stored, 16 * (NT // FETCH) * (len(copies) + (1 if first else 0)))

            @block.gpsimd
            def _(pool):
                pool.memset(wr[:], 0.0).then_inc(s.w_padded, 1)
                pool.iota(lane[:], pattern=[[0, 1]], base=0, channel_multiplier=1,
                          allow_small_or_imprecise_dtypes=True).then_inc(s.table_made, 1)
                pool.iota(lanes[:], pattern=[[1, P]], base=0, channel_multiplier=0,
                          allow_small_or_imprecise_dtypes=True).then_inc(s.table_made, 1)
                pool.iota(tile_of[:], pattern=[[0, K], [1, NT]], base=0, channel_multiplier=0,
                          allow_small_or_imprecise_dtypes=True).then_inc(s.table_made, 1)
                if first:
                    pool.memset(zeros[:], 0.0).then_inc(s.zeroed, 1)
                pool.iota(ebase[:], pattern=[[cap, E]], base=-1, channel_multiplier=0,
                          allow_small_or_imprecise_dtypes=True).then_inc(s.made, 1)
                pool.memset(restart[:], 1.0).then_inc(s.made, 1)
                pool.wait_ge(s.made, 2)
                pool.memset(restart[:, :, 0], 0.0).then_inc(s.made, 1)

            @block.scalar
            def _(act):
                def logits_out(g, half):
                    act.wait_ge(s.projected, g * RING + (4 * half + 4 + XR))
                    nc.scalar.copy(turned[:, bass.ds(g * (RING // 4) + half, 1), :],
                                   psR[:, half:half + 1, 0:P]).then_inc(s.read, 1)

                norm_loop_act(nc, act, s, b, psT, extra=logits_out)
                act.wait_ge(s.to_exp, 1)
                nc.scalar.activation(ex[:], ex[:], ACT.Exp).then_inc(s.exped, 1)

            @block.tensor
            def _(pe):
                pe.wait_ge(s.w_in, 16 if top2 else 32)

                pe.sem_inc(s.read, 2)

                def logits(g, j):
                    if j % 4 == 0:
                        pe.wait_ge(s.read, g * (RING // 4) + (j // 4 + 1))
                    rows = slice(32 * (j % 4), 32 * (j % 4) + 32)
                    for k in range(KC):
                        last = nc.tensor.matmul(psR[rows, j // 4, 0:P], wr[:, k, :], b.xT[:, j % XR, k * P:(k + 1) * P],
                                                start=(k == 0), stop=(k == KC - 1))
                    return last

                norm_loop_pe(nc, pe, s, m, b, psT, logits)
                for four in range(NT // 4):
                    pe.wait_ge(s.read, four + 3)
                    last = nc.tensor.transpose(psL[:, 4 * four:4 * four + 4, :], turned[:, four, :], m.ident[:])
                last.then_inc(s.turned_back, 1)

                def counts(asked):
                    pe.wait_ge(s.asked, asked)
                    nc.tensor.matmul(psP, m.upto[:], count_in[:], start=True, stop=True)
                    nc.tensor.matmul(psS, m.ones[:], count_in[:], start=True, stop=True).then_inc(s.counted, 1)

                if top2:
                    with pe.Fori(0, ROUNDS // 3) as turn3:
                        for i in range(3):
                            pe.wait_ge(s.asked_bit, turn3 * 3 + (i + 1))
                            for k in range(3):
                                last = nc.tensor.matmul(psB[:, k, :], m.ones[:], above[:, k], start=True, stop=True)
                            last.then_inc(s.counted_bit, 1)
                    pe.wait_ge(s.asked_bit, ROUNDS + 1)
                    nc.tensor.matmul(psS, m.ones[:], count_in[:], start=True, stop=True).then_inc(s.counted_bit, 1)
                    counts(1)
                    counts(2)
                else:
                    counts(1)
                for c in range(KT):
                    if c % FETCH == 0:
                        pe.wait_ge(s.hot, c // FETCH + 1)
                    last = nc.tensor.matmul(psF, part_hot[:, c, :], col_hot[:, c], start=(c == 0),
                                            stop=(c == KT - 1))
                last.then_inc(s.hot, 1)

            @block.vector
            def _(dve):
                norm_statistics(nc, dve, s, m, b, arrivals=arrivals)
                norm_loop_dve(nc, dve, s, m, b)
                link = Steps(dve, s.step)
                dve.wait_ge(s.made, 3)
                dve.wait_ge(s.turned_back, 1)
                if top2:
                    link(nc.vector.tensor_copy(lg[:], psL[:, :, 0:E]))
                else:
                    link(nc.vector.tensor_tensor(lg[:], psL[:, :, 0:E], bc(br[:].unsqueeze(1), full), ALU.add))
                link(nc.vector.tensor_reduce(top[0][:], lg[:], AX.X, ALU.max))
                nc.vector.tensor_tensor(ex[:], lg[:], bc(top[0][:].unsqueeze(2), full), ALU.subtract)\
                    .then_inc(s.to_exp, 1)
                if not top2:
                    first_hot(nc, link, hots[0][:], lg[:], top[0][:], t3[:], r0[:], m.eidx8[:])
                    dve.wait_ge(s.exped, 1)
                    link(nc.vector.tensor_reduce(r0[:], ex[:], AX.X, ALU.add))
                    link(nc.vector.reciprocal(r0[:], r0[:]))
                    link(nc.vector.reciprocal(r1[:], r0[:]))
                    link(nc.vector.scalar_tensor_tensor(out=m.gate[0][:], in0=r0[:], scalar=0.5, in1=r1[:],
                                                        op0=ALU.mult, op1=ALU.mult))
                else:
                    dve.wait_ge(s.exped, 1)
                    link(nc.vector.tensor_reduce(r0[:], ex[:], AX.X, ALU.add))
                    link(nc.vector.reciprocal(r0[:], r0[:]))
                    link(nc.vector.tensor_tensor(ex[:], ex[:], bc(r0[:].unsqueeze(2), full), ALU.mult))
                    link(nc.vector.tensor_reduce(top[0][:], ex[:], AX.X, ALU.max))
                    first_hot(nc, link, hots[0][:], ex[:], top[0][:], t3[:], r0[:], m.eidx8[:])
                    link(nc.vector.scalar_tensor_tensor(out=ex[:], in0=hots[0][:], scalar=-2.0, in1=ex[:],
                                                        op0=ALU.mult, op1=ALU.add))
                    link(nc.vector.tensor_reduce(top[1][:], ex[:], AX.X, ALU.max))
                    first_hot(nc, link, hots[1][:], ex[:], top[1][:], t3[:], r0[:], m.eidx8[:])
                    link(nc.vector.tensor_tensor(r0[:], top[0][:], top[1][:], ALU.add))
                    link(nc.vector.tensor_scalar(r0[:], r0[:], 1e-6, None, ALU.add))
                    link(nc.vector.reciprocal(r0[:], r0[:]))
                    for k in range(2):
                        link(nc.vector.tensor_tensor(top[k][:], top[k][:], r0[:], ALU.mult))
                    link(nc.vector.tensor_tensor(wt[:], hots[0][:], bc(top[0][:].unsqueeze(2), full), ALU.mult))
                    link(nc.vector.tensor_tensor(t3[:], hots[1][:], bc(top[1][:].unsqueeze(2), full), ALU.mult))
                    link(nc.vector.tensor_tensor(wt[:], wt[:], t3[:], ALU.add))
                    link(nc.vector.tensor_tensor(t3[:], hots[0][:], hots[1][:], ALU.add))
                    link(nc.vector.scalar_tensor_tensor(out=wt[:], in0=t3[:], scalar=-1.0, in1=wt[:],
                                                        op0=ALU.add, op1=ALU.add))
                    link(nc.vector.memset(cur[:], 0.0))
                    for k in range(4):
                        link(nc.vector.memset(m.bits[:, k, :], float(k << 28)))
                    four = [P, 4, E]
                    each = [P, 3, NT, E]
                    with dve.Fori(0, ROUNDS // 3) as turn3:
                        for i in range(3):
                            step = turn3 * (3 * turn) + i * turn
                            nc.vector.tensor_tensor(cand[:].bitcast(U32), bc(cur[:].bitcast(U32), four),
                                                    bc(m.bits[:], four), ALU.bitwise_or).then_inc(s.bit_step, 1)
                            dve.wait_ge(s.bit_step, step + 1)
                            nc.vector.tensor_tensor(above[:], bc(wt[:].unsqueeze(1), each), bc(cand[:, 1:4, :].unsqueeze(2), each),
                                                    ALU.is_ge).then_inc(s.asked_bit, 1)
                            nc.vector.tensor_scalar(m.bits[:], m.bits[:], 2, None, ALU.logical_shift_right)\
                                .then_inc(s.bit_step, 1)
                            dve.wait_ge(s.counted_bit, turn3 * 3 + (i + 1))
                            nc.vector.tensor_reduce(counts_of[:], psB.rearrange("p k (t e) -> p k e t", e=E), AX.X,
                                                    ALU.add).then_inc(s.bit_step, 1)
                            dve.wait_ge(s.bit_step, step + 3)
                            nc.vector.scalar_tensor_tensor(out=cand[:, 1:4, :], in0=counts_of[:], scalar=float(cap),
                                                           in1=cand[:, 1:4, :], op0=ALU.is_ge, op1=ALU.mult)\
                                .then_inc(s.bit_step, 1)
                            dve.wait_ge(s.bit_step, step + 4)
                            nc.vector.tensor_reduce(cur[:, 0, :], cand[:].rearrange("p k e -> p e k"), AX.X, ALU.max)\
                                .then_inc(s.bit_step, 1)
                            dve.wait_ge(s.bit_step, step + 5)
                    thr = bc(cur[:], full)
                    link(nc.vector.tensor_tensor(keep[:], wt[:], thr, ALU.is_gt))
                    nc.vector.tensor_copy(count_in[:], keep[:]).then_inc(s.asked_bit, 1)
                    dve.wait_ge(s.counted_bit, ROUNDS + 1)
                    link(nc.vector.tensor_reduce(cnt[:], psS.rearrange("p t e -> p e t"), AX.X, ALU.add))
                    link(nc.vector.tensor_scalar(cnt[:], cnt[:], -1.0, float(cap), ALU.mult, ALU.add))
                    link(nc.vector.tensor_tensor(wt[:], wt[:], thr, ALU.is_equal))
                    nc.vector.tensor_copy(count_in[:], wt[:]).then_inc(s.asked, 1)
                    prefix(dve, link, 1)
                    link(nc.vector.tensor_tensor(t3[:], t3[:], bc(cnt[:].unsqueeze(1), full), ALU.is_le))
                    link(nc.vector.tensor_tensor(t3[:], t3[:], wt[:], ALU.mult))
                    link(nc.vector.tensor_tensor(keep[:], keep[:], t3[:], ALU.add))
                link(nc.vector.tensor_copy(count_in[:], (keep if top2 else hots[0])[:]))
                nc.vector.nop().then_inc(s.asked, 1)
                prefix(dve, link, K)
                if not top2:
                    link(nc.vector.tensor_scalar(keep[:], t3[:], float(cap), None, ALU.is_le))
                link(nc.vector.tensor_tensor(t3[:], t3[:], bc(ebase[:].unsqueeze(1), full), ALU.add))
                for k in range(K):
                    link(nc.vector.tensor_tensor(ex[:], t3[:], hots[k][:], ALU.mult))
                    link(nc.vector.tensor_reduce(r0[:], ex[:], AX.X, ALU.add))
                    link(nc.vector.tensor_tensor(ex[:], keep[:], hots[k][:], ALU.mult))
                    link(nc.vector.tensor_reduce(r1[:], ex[:], AX.X, ALU.add))
                    if top2:
                        link(nc.vector.scalar_tensor_tensor(out=m.gate[k][:], in0=top[k][:], scalar=0.5,
                                                            in1=r1[:], op0=ALU.mult, op1=ALU.mult))
                    link(nc.vector.tensor_scalar(r1[:], r1[:], -float(FAR), float(FAR), ALU.mult, ALU.add))
                    link(nc.vector.tensor_tensor(place[:, k * NT:(k + 1) * NT], r0[:], r1[:], ALU.add))
                link(nc.vector.tensor_scalar(part_u[:], place[:], P - 1, None, ALU.bitwise_and))
                link(nc.vector.tensor_scalar(col_u[:], place[:], 7, None, ALU.logical_shift_right))
                link(nc.vector.tensor_copy(part[:], part_u[:]))
                link(nc.vector.tensor_copy(col[:], col_u[:]))
                dve.wait_ge(s.table_made, 3)
                hots_of = [P, KT, NS]
                link(nc.vector.tensor_tensor(col_hot[:, :, 0, :], bc(lanes[:, 0:NS].unsqueeze(1), hots_of),
                                             bc(col[:].unsqueeze(2), hots_of), ALU.is_equal))
                link(nc.vector.tensor_scalar(col_hot[:, :, 1, :], col_hot[:, :, 0, :], lane[:], None, ALU.mult))
                link(nc.vector.tensor_tensor(col_hot[:, :, 2, :], col_hot[:, :, 0, :],
                                             bc(tile_of[:].unsqueeze(2), hots_of), ALU.mult))
                if top2:
                    link(nc.vector.tensor_scalar(col_hot[:, NT:, 0, :], col_hot[:, NT:, 0, :], 2.0, None, ALU.mult))
                for c in range(0, KT, FETCH):
                    nc.vector.tensor_tensor(part_hot[:, c:c + FETCH, :], bc(lanes[:].unsqueeze(1), [P, FETCH, P]),
                                            bc(part[:, c:c + FETCH].unsqueeze(2), [P, FETCH, P]), ALU.is_equal)\
                        .then_inc(s.hot, 1)
                dve.wait_ge(s.hot, KT // FETCH + 1)
                link(nc.vector.tensor_copy(found[:], psF))
                link(nc.vector.scalar_tensor_tensor(out=token[:], in0=found[:, 2, :], scalar=float(P),
                                                    in1=found[:, 1, :], op0=ALU.mult, op1=ALU.add))
                link(nc.vector.tensor_copy(m.fetch[:], token[:]))
                link(nc.vector.tensor_scalar(goes[:], found[:, 0, :], -1.0, 0.0, ALU.add, ALU.max))
                link(nc.vector.scalar_tensor_tensor(out=token[:], in0=goes[:], scalar=float(T), in1=token[:],
                                                    op0=ALU.mult, op1=ALU.add))
                link(nc.vector.tensor_scalar(goes[:], found[:, 0, :], 0.0, float(FAR), ALU.is_equal, ALU.mult))
                link(nc.vector.tensor_tensor(m.place[:], token[:], goes[:], ALU.add))



def experts_stage(nc, m, w, top2):
    cap = TOP2_CAP if top2 else SWITCH_CAP
    S = cap // P
    NP = 2 if top2 else 1
    W = cap // NP
    UP = 2 if top2 else 1
    U = FC * NP
    RAW = 1 if top2 else 2
    PIECES = 4
    PF = F // PIECES
    PR = 4
    HC = FC // 2
    name = w.name + "_x"
    HIGH, LOW = 0, 1
    with ExitStack() as ctx:
        def sb(n, shape, dt=F32):
            return ctx.enter_context(nc.sbuf_tensor(f"{name}_{n}", shape, dt))

        def ps(n):
            return ctx.enter_context(nc.psum_tensor(f"{name}_{n}", [P, 2, 512], F32))

        free = m.xn[:].rearrange("p t d -> p (t d)")
        first, second = UP * KC * F, FC * D
        w1 = [free[:, r * first:(r + 1) * first].rearrange("p (u k f) -> p u k f", u=UP, k=KC) for r in range(RAW)]
        free = free[:, RAW * first:]
        w2 = [free[:, r * second:(r + 1) * second].rearrange("p (c d) -> p c d", c=FC) for r in range(RAW)]
        w1p = sb("w1p", [P, 2, UP, KC, F], F32R)
        w2p = [sb(f"w2p_{r}", [P, 2, FC, D], F32R) for r in range(RAW)]
        a = [sb(f"a_{h}", [P, S, D]) for h in range(2)]
        aTp = sb("aTp", [P, 2, KC, cap], F32R)
        prod = free[:, RAW * second:RAW * second + PR * W].rearrange("p (r n) -> p r n", r=PR) if top2 else \
            sb("prod", [P, PR, W])
        hidp = sb("hidp", [P, 2, FC, cap], F32R)
        yo = [sb(f"yo_{h}", [P, S, D]) for h in range(2)]
        if top2:
            sg = sb("sg", [P, 2, W])
        else:
            b1 = sb("b1", [P, E * FC])
            b1r = sb("b1r", [E * FC, P])
            b2 = sb("b2", [P, E, D])
        psT, psG, psU, psY = ps("psT"), ps("psG"), ps("psU"), ps("psY")
        w1_dram = [v.rearrange("e (k p) f -> e p k f", p=P) for v in w.up]
        w2_dram = w.down.rearrange("e (c p) d -> e p c d", p=P)

        def split_product(out, parts_l, parts_r, first=True, final=True):
            n = len(parts_l)
            for k in range(n):
                for i, (sl, sr) in enumerate(((HIGH, HIGH), (HIGH, LOW), (LOW, HIGH))):
                    last = nc.tensor.matmul(out, parts_l[k][sl], parts_r[k][sr], start=(first and k == 0 and i == 0),
                                            stop=(final and k == n - 1 and i == 2))
            return last

        def over_experts(eng, body):
            with eng.Fori(0, E // 2 - 1) as pair:
                for h in range(2):
                    body(pair * 2 + h, h, pair, False)
            for h in range(2):
                body(E - 2 + h, h, E // 2 - 1, h == 1)

        with stage(nc, name, "w1_in0 w1_in1 w2_in0 w2_in1 bias_in b1_turned b1_ready turned turned_high turned_out "
                             "w1_high w1_low w2_high w2_low hidden gated done hid_high hid_low y_ready y_out yo_free")\
                as (block, s):
            w1_in, w2_in = (s.w1_in0, s.w1_in1), (s.w2_in0, s.w2_in1)
            a_in = [pool_semaphore(m, h, S * E // 2) for h in range(2)]
            stored = [pool_semaphore(m, 2 + h, S * E // 2) for h in range(2)]

            def raw(e, h, pair):
                return (h, pair + 1) if RAW == 2 else (0, e + 1)

            @block.sync
            def _(sp):
                def load(e, r):
                    for u in range(UP):
                        sp.dma_start(w1[r][:, u], w1_dram[u][e]).then_inc(w1_in[r], 16)

                def load_down(e, r):
                    sp.dma_start(w2[r], w2_dram[e]).then_inc(w2_in[r], 16)

                load(0, 0)
                load_down(0, 0)
                if not top2:
                    sp.dma_start(b1r[:], w.up_b.rearrange("e (c p) -> (e c) p", p=P)).then_inc(s.bias_in, 16)
                    sp.dma_start(b2[:], w.down_b.partition_broadcast(P)).then_inc(s.bias_in, 16)
                if RAW == 2:
                    load(1, 1)
                    load_down(1, 1)
                with sp.Fori(RAW, E) if RAW == 1 else sp.Fori(1, E // 2) as turn:
                    for r in range(RAW):
                        e = turn * RAW + r
                        sp.wait_ge(s.w1_low, (e - RAW + 1) * PIECES)
                        load(e, r)
                        sp.wait_ge(s.w2_low, (e - RAW + 1) * 2)
                        load_down(e, r)

            @block.tensor
            def _(pe):
                def turn(e, h, pair, tiles):
                    gathered, past = a_in[h]
                    if 0 in tiles:
                        pe.wait_ge(gathered, pair * (16 * S) + (past + 16 * S))
                    for i in tiles:
                        n = e * S + i
                        pe.wait_ge(s.turned_out, n + 1)
                        for k in range(KC):
                            last = nc.tensor.transpose(psT[:, (h * S + i) % 2, k * P:(k + 1) * P],
                                                       a[h][:, i, k * P:(k + 1) * P], m.ident[:])
                        last.then_inc(s.turned, 1)

                def hidden(e, h, pair):
                    pe.wait_ge(s.turned_out, e * S + S + 2)
                    for c in range(FC):
                        if c % (FC // PIECES) == 0:
                            pe.wait_ge(s.w1_low, e * PIECES + (c // (FC // PIECES) + 1))
                        for q in range(NP):
                            n = e * U + (c * NP + q)
                            slot = (c * NP + q) % 2
                            pe.wait_ge(s.gated, n + 1)
                            if top2:
                                pe.wait_ge(s.done, n + 1)
                            for u, ps_u in enumerate((psG, psU)[:UP]):
                                last = split_product(
                                    ps_u[:, slot, 0:W],
                                    [[w1p[:, part, u, k, c * P:(c + 1) * P] for part in range(2)] for k in range(KC)],
                                    [[aTp[:, part, k, q * W:(q + 1) * W] for part in range(2)] for k in range(KC)])
                            last.then_inc(s.hidden, 1)

                def down(e, h, pair, i):
                    if i == 0:
                        pe.wait_ge(s.w2_low, e * 2 + 2)
                    pe.wait_ge(s.y_out, e * S + i + 1)
                    for c in range(FC):
                        if i == 0:
                            pe.wait_ge(s.hid_low, e * U + ((c + 1) * NP + PR))
                        last = split_product(psY[:, (h * S + i) % 2, 0:D],
                                             [[hidp[:, part, c, i * P:(i + 1) * P] for part in range(2)]],
                                             [[w2p[h % RAW][:, part, c, :] for part in range(2)]],
                                             c == 0, c == FC - 1)
                    last.then_inc(s.y_ready, 1)

                pe.sem_inc(s.turned_out, 2)
                pe.sem_inc(s.gated, 2)
                pe.sem_inc(s.y_out, 2)
                pe.sem_inc(s.hid_low, PR)
                if top2:
                    pe.sem_inc(s.done, 2)
                else:
                    pe.wait_ge(s.bias_in, 32)
                    nc.tensor.transpose(psU[:, 0, 0:E * FC], b1r[:], m.ident[0:E * FC, 0:E * FC])\
                        .then_inc(s.b1_turned, 1)
                turn(0, 0, 0, range(S))

                def body(e, h, pair, last):
                    hidden(e, h, pair)
                    if not last:
                        turn(e + 1, 1 - h, pair + h, range(2))
                    for i in range(S):
                        down(e, h, pair, i)
                        if not last and i + 2 < S:
                            turn(e + 1, 1 - h, pair + h, range(i + 2, i + 3))

                over_experts(pe, body)

            @block.scalar
            def _(act):
                def turned(e, h, tiles):
                    for i in tiles:
                        act.wait_ge(s.turned, e * S + i + 1)
                        nc.scalar.copy(aTp[:, HIGH, :, i * P:(i + 1) * P],
                                       psT[:, (h * S + i) % 2, 0:D].rearrange("p (k n) -> p k n", k=KC))\
                            .then_inc(s.turned_high, 1)

                def split_up(e, h, pair, q):
                    r, loads = raw(e, h, pair)
                    act.wait_ge(w1_in[r], loads * (16 * UP))
                    cols = slice(q * PF, (q + 1) * PF)
                    for u in range(UP):
                        last = nc.scalar.copy(w1p[:, HIGH, u, :, cols], w1[r][:, u, :, cols])
                    last.then_inc(s.w1_high, 1)

                def split_down(e, h, pair, piece):
                    r, loads = raw(e, h, pair)
                    act.wait_ge(w2_in[r], loads * 16)
                    chunks = slice(piece * HC, (piece + 1) * HC)
                    nc.scalar.copy(w2p[r][:, HIGH, chunks, :], w2[r][:, chunks, :]).then_inc(s.w2_high, 1)

                def high(e, j):
                    c, q = j // NP, j % NP
                    act.wait_ge(s.done if top2 else s.gated, e * U + (j + 3))
                    nc.scalar.copy(hidp[:, HIGH, c, q * W:(q + 1) * W], prod[:, j % PR, :]).then_inc(s.hid_high, 1)

                turned(0, 0, range(S))
                for q in range(PIECES):
                    split_up(0, 0, 0, q)
                if not top2:
                    for piece in range(2):
                        split_down(0, 0, 0, piece)
                    act.wait_ge(s.b1_ready, 1)

                def body(e, h, pair, last):
                    for j in range(U):
                        c = j // NP
                        n = e * U + j
                        act.wait_ge(s.hidden, n + 1)
                        if top2:
                            act.wait_ge(s.done, n + 1)
                            nc.scalar.activation(sg[:, j % 2, :], psG[:, j % 2, 0:W], ACT.Silu).then_inc(s.gated, 1)
                        else:
                            act.wait_ge(s.hid_low, n + 1)
                            nc.scalar.activation(prod[:, j % PR, :], psG[:, j % 2, 0:W], ACT.Relu,
                                                 bias=b1[:, bass.ds(e * FC + c, 1)]).then_inc(s.gated, 1)
                        if j:
                            high(e, j - 1)
                        if top2 and j in (U // 4, U // 2):
                            split_down(e, h, pair, j // (U // 4) - 1)
                    high(e, U - 1)
                    if not last:
                        turned(e + 1, 1 - h, range(2))
                        for q in range(PIECES):
                            split_up(e + 1, 1 - h, pair + h, q)
                            if q + 2 < S:
                                turned(e + 1, 1 - h, range(q + 2, q + 3))
                        if not top2:
                            for piece in range(2):
                                split_down(e + 1, 1 - h, pair + h, piece)

                over_experts(act, body)

            @block.vector
            def _(dve):
                def turned(e, h, tiles):
                    for i in tiles:
                        dve.wait_ge(s.turned_high, e * S + i + 1)
                        cols = slice(i * P, (i + 1) * P)
                        nc.vector.tensor_tensor(aTp[:, LOW, :, cols],
                                                psT[:, (h * S + i) % 2, 0:D].rearrange("p (k n) -> p k n", k=KC),
                                                aTp[:, HIGH, :, cols].bitcast(F32), ALU.subtract)\
                            .then_inc(s.turned_out, 1)

                def split_up(e, h, pair, q):
                    r, loads = raw(e, h, pair)
                    dve.wait_ge(s.w1_high, e * PIECES + (q + 1))
                    cols = slice(q * PF, (q + 1) * PF)
                    for u in range(UP):
                        last = nc.vector.tensor_tensor(w1p[:, LOW, u, :, cols], w1[r][:, u, :, cols],
                                                       w1p[:, HIGH, u, :, cols].bitcast(F32), ALU.subtract)
                    last.then_inc(s.w1_low, 1)

                def split_down(e, h, pair, piece):
                    r, loads = raw(e, h, pair)
                    dve.wait_ge(s.w2_high, e * 2 + (piece + 1))
                    chunks = slice(piece * HC, (piece + 1) * HC)
                    nc.vector.tensor_tensor(w2p[r][:, LOW, chunks, :], w2[r][:, chunks, :],
                                            w2p[r][:, HIGH, chunks, :].bitcast(F32), ALU.subtract)\
                        .then_inc(s.w2_low, 1)

                def low(e, j):
                    c, q = j // NP, j % NP
                    dve.wait_ge(s.hid_high, e * U + (j + 1))
                    cols = slice(q * W, (q + 1) * W)
                    nc.vector.tensor_tensor(hidp[:, LOW, c, cols], prod[:, j % PR, :],
                                            hidp[:, HIGH, c, cols].bitcast(F32), ALU.subtract).then_inc(s.hid_low, 1)

                turned(0, 0, range(S))
                for q in range(PIECES):
                    split_up(0, 0, 0, q)
                if not top2:
                    for piece in range(2):
                        split_down(0, 0, 0, piece)
                    dve.wait_ge(s.b1_turned, 1)
                    nc.vector.tensor_copy(b1[:], psU[:, 0, 0:E * FC]).then_inc(s.b1_ready, 1)

                def body(e, h, pair, last):
                    for j in range(U):
                        n = e * U + j
                        if top2:
                            dve.wait_ge(s.gated, n + 3)
                            dve.wait_ge(s.hid_low, n + 1)
                            nc.vector.tensor_tensor(prod[:, j % PR, :], sg[:, j % 2, :], psU[:, j % 2, 0:W],
                                                    ALU.mult).then_inc(s.done, 1)
                        if j:
                            low(e, j - 1)
                        if top2 and j in (U // 4 + 1, U // 2 + 1):
                            split_down(e, h, pair, j // (U // 4) - 1)
                    low(e, U - 1)
                    if not last:
                        turned(e + 1, 1 - h, range(2))
                    dve.wait_ge(s.yo_free, e + 1)

                    def y(i):
                        dve.wait_ge(s.y_ready, e * S + i + 1)
                        src = psY[:, (h * S + i) % 2, 0:D]
                        if top2:
                            nc.vector.tensor_copy(yo[h][:, i, :], src).then_inc(s.y_out, 1)
                        else:
                            nc.vector.tensor_tensor(yo[h][:, i, :], src, b2[:, e, :], ALU.add).then_inc(s.y_out, 1)

                    def up(q):
                        if not last:
                            split_up(e + 1, 1 - h, pair + h, q)

                    def down(piece):
                        if not last:
                            split_down(e + 1, 1 - h, pair + h, piece)

                    if top2:
                        for i in range(S):
                            if i < PIECES:
                                up(i)
                            y(i)
                            if not last and i + 2 < S:
                                turned(e + 1, 1 - h, range(i + 2, i + 3))
                    else:
                        for q in range(PIECES):
                            up(q)
                            if q == PIECES - 2:
                                y(0)
                        down(0)
                        y(1)
                        down(1)

                over_experts(dve, body)

            @block.gpsimd
            def _(pool):
                def gather(e):
                    if e >= 2:
                        pool.wait_ge(s.turned, (e - 1) * S)
                    for i in range(S):
                        pool.indirect_dma_start(
                            out=a[e % 2][:, i, :], out_offset=None, in_=m.tokens,
                            in_offset=bass.IndirectOffsetOnAxis(ap=m.fetch[:, e * S + i:e * S + i + 1], axis=0),
                            bounds_check=T - 1, oob_is_err=False).then_inc(a_in[e % 2][0], 16)

                pool.sem_inc(s.yo_free, 2)
                gather(0)
                gather(1)
                for e in range(E):
                    in_dram, past = stored[e % 2]
                    if e >= 2:
                        pool.wait_ge(in_dram, past + 16 * S * (e // 2))
                        pool.sem_inc(s.yo_free, 1)
                    if e + 2 < E:
                        gather(e + 2)
                    for i in range(S):
                        pool.wait_ge(s.y_out, e * S + (i + 3))
                        pool.indirect_dma_start(
                            out=m.outs, out_offset=bass.IndirectOffsetOnAxis(
                                ap=m.place[:, e * S + i:e * S + i + 1], axis=0),
                            in_=yo[e % 2][:, i, :], in_offset=None, bounds_check=2 * T - 1,
                            oob_is_err=False).then_inc(in_dram, 16)
                for in_dram, past in stored:
                    pool.wait_ge(in_dram, past + 16 * S * E // 2)


def combine_stage(nc, m, name, top2, out):
    K = 2 if top2 else 1
    groups = NT // FETCH
    with ExitStack() as ctx:
        got = [m.xn, ctx.enter_context(nc.sbuf_tensor(name + "_got1", [P, NT, D], F32)) if top2 else None]
        with stage(nc, name, "added stored " + " ".join(f"in{n}" for n in range(K * groups))) as (block, s):
            fetched = s[2:]

            @block.sync
            def _(sp):
                for g in range(groups):
                    for k in range(K):
                        rows = slice(k * T + g * FETCH * P, k * T + (g + 1) * FETCH * P)
                        sp.dma_start(got[k][:, g * FETCH:(g + 1) * FETCH, :],
                                     m.outs[rows, :].rearrange("(t p) d -> p t d", p=P))\
                            .then_inc(fetched[g * K + k], 16)
                if out is not None:
                    for g in range(groups):
                        sp.wait_ge(s.added, (g + 1) * K * FETCH)
                        sp.dma_start(token_tiles(out, g), m.x[:, g * FETCH:(g + 1) * FETCH, :])\
                            .then_inc(s.stored, 16)
                    sp.wait_ge(s.stored, 16 * groups)

            @block.vector
            def _(dve):
                for g in range(NT // FETCH):
                    for k in range(K):
                        dve.wait_ge(fetched[g * K + k], 16)
                        if k:
                            dve.wait_ge(s.added, (g * K + k) * FETCH)
                        for t in range(g * FETCH, g * FETCH + FETCH):
                            nc.vector.scalar_tensor_tensor(
                                out=m.x[:, t, :], in0=got[k][:, t, :], scalar=m.gate[k][:, t:t + 1],
                                in1=m.x[:, t, :], op0=ALU.mult, op1=ALU.add).then_inc(s.added, 1)


def ffn(nc, m, w, top2, x_in=None, out=None):
    K, cap = (2, TOP2_CAP) if top2 else (1, SWITCH_CAP)
    with ExitStack() as ctx:
        m.place = ctx.enter_context(nc.sbuf_tensor(f"{w.name}_place", [P, E * cap // P], U32))
        m.fetch = ctx.enter_context(nc.sbuf_tensor(f"{w.name}_fetch", [P, E * cap // P], U32))
        m.gate = [ctx.enter_context(nc.sbuf_tensor(f"{w.name}_gate{k}", [P, NT], F32)) for k in range(K)]
        route_stage(nc, m, w, top2, x_in)
        experts_stage(nc, m, w, top2)
        combine_stage(nc, m, w.name + "_combine", top2, out)



QB = 512
NB = T // QB
TB = QB // P
H = 16
DH = D // H
EVEN = 8


def norm_and_values_stage(nc, m, name, wv_dram, values, bias_dram=None, stats=None):
    xnT = turned_view(m)
    with ExitStack() as ctx:
        def sb(n, shape, dt=F32):
            return ctx.enter_context(nc.sbuf_tensor(f"{name}_{n}", shape, dt))

        b = norm_buffers(nc, ctx, name)
        if stats is not None:
            b = b._replace(mean=stats[0], rstd=stats[1])
        wv = sb("wv", [P, KC, D])
        bv = sb("bv", [P, D])
        psT = ctx.enter_context(nc.psum_tensor(f"{name}_psT", [P, XR, 512], F32))
        psV = ctx.enter_context(nc.psum_tensor(f"{name}_psV", [P, 2, 512], F32))
        with stage(nc, name, NORM_SEMS + " w_in v_done ones_made") as (block, s):
            @block.sync
            def _(sp):
                sp.dma_start(wv[:], wv_dram.rearrange("(k p) n -> p k n", p=P)).then_inc(s.w_in, 16)
                if bias_dram is not None:
                    sp.dma_start(bv[:], bias_dram.partition_broadcast(P)).then_inc(s.w_in, 16)

            @block.gpsimd
            def _(pool):
                if values.shape[3] > DH:
                    pool.memset(values[:, :, :, DH:], 1.0).then_inc(s.ones_made, 1)
                pool.sem_inc(s.kept, RING)
                with pool.Fori(0, NT // RING) as g:
                    for j in range(RING):
                        t = g * RING + j
                        pool.wait_ge(s.xT_ready, t + 1)
                        nc.gpsimd.tensor_copy(xnT[:, :, bass.ds(t * P, P)],
                                              b.xT[:, j % XR].rearrange("p (k n) -> p k n", k=KC))\
                            .then_inc(s.kept, 1)

            @block.scalar
            def _(act):
                norm_loop_act(nc, act, s, b, psT, keeps_turned=True)

            @block.tensor
            def _(pe):
                pe.wait_ge(s.w_in, 16 if bias_dram is None else 32)
                pe.sem_inc(s.v_done, 2)

                def v(g, j):
                    pe.wait_ge(s.v_done, g * RING + (j + 1))
                    for k in range(KC):
                        last = nc.tensor.matmul(psV[:, j % 2, 0:D], b.xT[:, j % XR, k * P:(k + 1) * P], wv[:, k, :],
                                                start=(k == 0), stop=(k == KC - 1))
                    return last

                norm_loop_pe(nc, pe, s, m, b, psT, v)

            @block.vector
            def _(dve):
                norm_statistics(nc, dve, s, m, b)
                norm_loop_dve_values(nc, dve, s, m, b, psV, values, bv if bias_dram is not None else None)


def norm_loop_dve_values(nc, dve, s, m, b, psV, values, bv):
    def normed(t, j):
        dve.wait_ge(s.transposed, t + 1)
        nc.vector.tensor_scalar(b.tile[:, j, :], m.x[:, t, :], b.mean[:, bass.ds(t, 1)],
                                b.rstd[:, bass.ds(t, 1)], ALU.subtract, ALU.mult).then_inc(s.normed, 1)

    def value(t, j):
        dve.wait_ge(s.projected, t + (1 + XR))
        out = values[:, t, :, 0:DH]
        src = psV[:, j % 2, 0:D].rearrange("p (h d) -> p h d", h=H)
        if bv is None:
            nc.vector.tensor_copy(out, src).then_inc(s.v_done, 1)
        else:
            nc.vector.tensor_tensor(out, src, bv[:].rearrange("p (h d) -> p h d", h=H), ALU.add)\
                .then_inc(s.v_done, 1)

    def tiles(g, last):
        for j in range(RING):
            if not last or j + 2 * LEAD < RING:
                normed(g * RING + (j + 2 * LEAD), (j + 2 * LEAD) % RING)
            value(g * RING + j, j)

    for t in range(2 * LEAD):
        normed(t, t)
    with dve.Fori(0, NT // RING - 1) as g:
        tiles(g, False)
    tiles(NT // RING - 1, True)


def turned_view(m):
    return m.xn[:].rearrange("p t d -> p (t d)").rearrange("p (k n) -> p k n", k=KC)



Q_PART = (0, 0, 0, 1, 1, 2)
K_PART = (0, 1, 2, 0, 1, 0)
STACK = len(Q_PART) * DH
G = 4
NG = H // G
LN8 = 2.0794415416798357
FAR_BELOW = -1e30


def load_stack(sp, m, which, heads, parts, cols, out, sem):
    first, n = heads
    for r, part in enumerate(parts):
        sp.dma_start(out[r * DH:(r + 1) * DH],
                     m.parts[which, part, bass.ds(first * DH, n * DH), cols]
                     .rearrange("(h r) n -> r h n", r=DH)).then_inc(sem, 16)


STACK_LOADS = 16 * len(Q_PART)


def split_stage(nc, m, name, w, bias=None):
    xnT = turned_view(m)
    favor_kind = bias is not None
    with ExitStack() as ctx:
        def sb(n, shape, dt=F32):
            return ctx.enter_context(nc.sbuf_tensor(f"{name}_{n}", shape, dt))

        wqk = [sb(f"w{i}", [P, KC, D]) for i in range(2)]
        PR = 4
        parts = sb("parts", [P, PR, 3, QB], BF16)
        rest = sb("rest", [P, 2, QB])
        ps = ctx.enter_context(nc.psum_tensor(f"{name}_ps", [P, PR, QB], F32))
        tasks = [(i, c) for i in range(2) for c in range(KC)]
        n_tasks = len(tasks)
        if favor_kind:
            b = sb("b", [P, 2, KC])
            val, sq = sb("val", [P, 2, QB]), sb("sq", [P, 2, QB])
            halves = sb("halves", [P, 32])
            norm, norm_rest = sb("norm", [P, QB]), sb("norm_rest", [P, QB])
            norm_parts = sb("norm_parts", [P, 3, QB], BF16)
            psC = ctx.enter_context(nc.psum_tensor(f"{name}_psC", [P, QB], F32))
        with stage(nc, name, "w_in ready taken high rest1 mid low put0 put1 put2 put3 part_free filled made squared summed "
                             "sum_taken sum_step sums_ready sums_put") as (block, s):
            put = (s.put0, s.put1, s.put2, s.put3)

            @block.sync
            def _(sp):
                for i in range(2):
                    sp.dma_start(wqk[i][:], w[i].rearrange("(k p) n -> p k n", p=P)).then_inc(s.w_in, 16)
                    if favor_kind:
                        sp.dma_start(b[:, i, :], bias[i].rearrange("(k p) -> p k", p=P),
                                     allow_slow_non_contiguous=True).then_inc(s.w_in, 16)
                with sp.Fori(0, NB) as blk:
                    cols = bass.ds(blk * QB, QB)
                    for j, (i, c) in enumerate(tasks):
                        sp.wait_ge(s.low, blk * n_tasks + (j + 1))
                        sp.dma_start(m.parts[i, :, c * P:(c + 1) * P, cols].rearrange("a p n -> p a n"),
                                     parts[:, j]).then_inc(put[j], 16)
                    if favor_kind:
                        sp.wait_ge(s.sums_ready, blk + 1)
                        for j, (i, c) in enumerate(tasks):
                            sp.dma_start(m.norms[i, c * EVEN:(c + 1) * EVEN, :, cols],
                                         norm_parts[32 * j:32 * j + EVEN]).then_inc(s.sums_put, 16)
                for one in put:
                    sp.wait_ge(one, 16 * NB)
                if favor_kind:
                    sp.wait_ge(s.sums_put, 16 * n_tasks * NB)

            if favor_kind:
                @block.gpsimd
                def _(pool):
                    pool.memset(halves[:], 0.5).then_inc(s.filled, 1)
                    pool.wait_ge(s.filled, 1)
                    pool.affine_select(out=halves[:], in_=halves[:], compare_op=ALU.is_ge, fill=0.0, base=0,
                                       pattern=[[-DH, 32]], channel_multiplier=1).then_inc(s.filled, 1)
                    pool.wait_ge(s.filled, 2)
                    pool.affine_select(out=halves[:], in_=halves[:], compare_op=ALU.is_ge, fill=0.0, base=DH - 1,
                                       pattern=[[DH, 32]], channel_multiplier=-1).then_inc(s.made, 1)

            @block.tensor
            def _(pe):
                pe.wait_ge(s.w_in, 64 if favor_kind else 32)
                if not favor_kind:
                    pe.sem_inc(s.taken, PR)
                if favor_kind:
                    pe.wait_ge(s.made, 1)
                    pe.sem_inc(s.summed, 2)
                    pe.sem_inc(s.sum_taken, 1)

                def square_sums(blk, j):
                    pe.wait_ge(s.squared, blk * n_tasks + (j + 1))
                    if j == 0:
                        pe.wait_ge(s.sum_taken, blk + 1)
                    nc.tensor.matmul(psC[32 * j:32 * j + 32, :], halves[:], sq[:, j % 2, :],
                                     start=True, stop=True).then_inc(s.summed, 1)

                def block_products(blk, first):
                    for j, (i, c) in enumerate(tasks):
                        if not favor_kind:
                            pe.wait_ge(s.taken, blk * n_tasks + (j + 1))
                        elif not first:
                            pe.wait_ge(s.high, blk * n_tasks + (j + 1 - PR))
                        for k in range(KC):
                            last = nc.tensor.matmul(ps[:, j, :], wqk[i][:, k, c * P:(c + 1) * P],
                                                    xnT[:, k, bass.ds(blk * QB, QB)],
                                                    start=(k == 0), stop=(k == KC - 1))
                        last.then_inc(s.ready, 1)
                        if favor_kind and j:
                            square_sums(blk, j - 1)
                        elif favor_kind and not first:
                            square_sums(blk - 1, n_tasks - 1)

                block_products(0, True)
                with pe.Fori(1, NB) as blk:
                    block_products(blk, False)
                if favor_kind:
                    square_sums(NB - 1, n_tasks - 1)

            def before(blk, j, back):
                return (blk, j - back) if j >= back else (blk - 1, j - back + n_tasks)


            @block.scalar
            def _(act):
                def middle(blk, j):
                    act.wait_ge(s.rest1, blk * n_tasks + (j + 1))
                    nc.scalar.copy(parts[:, j, 1, :], rest[:, j % 2, :]).then_inc(s.mid, 1)

                if favor_kind:
                    act.wait_ge(s.w_in, 64)

                def block_parts(blk, first):
                    for j, (i, c) in enumerate(tasks):
                        n = blk * n_tasks + j
                        if not first:
                            act.wait_ge(put[j], blk * 16)
                        if favor_kind:
                            act.wait_ge(s.ready, n + 1)
                            if j > 1 or not first:
                                act.wait_ge(s.rest1, n - 1)
                                act.wait_ge(s.squared, n - 1)
                            bias_of = b[:, i, c:c + 1]
                            nc.scalar.activation(val[:, j % 2, :], ps[:, j, :], ACT.Identity, bias=bias_of)\
                                .then_inc(s.taken, 1)
                            nc.scalar.activation(parts[:, j, 0, :], ps[:, j, :], ACT.Identity, bias=bias_of)\
                                .then_inc(s.high, 1)
                            act.wait_ge(s.taken, n + 1)
                            act.wait_ge(s.summed, n + 1)
                            nc.scalar.activation(sq[:, j % 2, :], val[:, j % 2, :], ACT.Square,
                                                 scale=DH ** -0.5).then_inc(s.squared, 1)
                        else:
                            act.wait_ge(s.ready, n + 1)
                            nc.scalar.copy(parts[:, j, 0, :], ps[:, j, :]).then_inc(s.high, 1)
                        if j or not first:
                            middle(*before(blk, j, 1))

                block_parts(0, True)
                with act.Fori(1, NB) as blk:
                    block_parts(blk, False)
                middle(NB - 1, n_tasks - 1)

            @block.vector
            def _(dve):
                def rest_of(blk, j):
                    dve.wait_ge(s.high, blk * n_tasks + (j + 1))
                    if j > 1 or type(blk) is not int or blk:
                        dve.wait_ge(s.low, blk * n_tasks + (j - 1))
                    src = val[:, j % 2, :] if favor_kind else ps[:, j, :]
                    nc.vector.tensor_tensor(rest[:, j % 2, :], src, parts[:, j, 0, :], ALU.subtract)\
                        .then_inc(s.rest1, 1)

                def low_of(blk, j):
                    dve.wait_ge(s.mid, blk * n_tasks + (j + 1))
                    nc.vector.tensor_tensor(parts[:, j, 2, :], rest[:, j % 2, :], parts[:, j, 1, :],
                                            ALU.subtract).then_inc(s.low, 1)
                    if not favor_kind:
                        dve.sem_inc(s.taken, 1)

                def block_parts(blk, first):
                    for j in range(n_tasks):
                        if j or not first:
                            rest_of(*before(blk, j, 1))
                        if j > 1 or not first:
                            low_of(*before(blk, j, 2))
                        if favor_kind and j == 0 and not first:
                            square_parts(blk - 1, type(blk) is int and blk == 1)

                def square_parts(blk, first):
                    step = blk * 3
                    dve.wait_ge(s.summed, blk * n_tasks + (n_tasks + 2))
                    nc.vector.tensor_scalar(norm[:], psC[:], LN8, None, ALU.add).then_inc(s.sum_taken, 1)
                    dve.wait_ge(s.sum_taken, blk + 2)
                    if not first:
                        dve.wait_ge(s.sums_put, blk * (16 * n_tasks))
                    nc.vector.tensor_copy(norm_parts[:, 0, :], norm[:]).then_inc(s.sum_step, 1)
                    dve.wait_ge(s.sum_step, step + 1)
                    nc.vector.tensor_tensor(norm_rest[:], norm[:], norm_parts[:, 0, :], ALU.subtract)\
                        .then_inc(s.sum_step, 1)
                    dve.wait_ge(s.sum_step, step + 2)
                    nc.vector.tensor_copy(norm_parts[:, 1, :], norm_rest[:]).then_inc(s.sum_step, 1)
                    dve.wait_ge(s.sum_step, step + 3)
                    nc.vector.tensor_tensor(norm_parts[:, 2, :], norm_rest[:], norm_parts[:, 1, :],
                                            ALU.subtract).then_inc(s.sums_ready, 1)

                block_parts(0, True)
                block_parts(1, False)
                with dve.Fori(2, NB) as blk:
                    block_parts(blk, False)
                rest_of(NB - 1, n_tasks - 1)
                low_of(NB - 1, n_tasks - 2)
                low_of(NB - 1, n_tasks - 1)
                if favor_kind:
                    square_parts(NB - 1, False)


def attention_plan():
    def maxima(i):
        return [("max", i, qt, h, c) for qt in range(TB) for h in range(G) for c in range(i + 1)]

    def turns(i):
        return [("turn", i, h) for h in range(G)]

    begin = [G * TB * i * (i + 1) // 2 for i in range(NB + 1)]
    lead = 15
    plan = maxima(0) + [("rows", 0)]
    waiting = []
    ahead = maxima(1)
    done = len(ahead) * lead // begin[1]
    plan += ahead[:done] + turns(0)
    nxt = 1
    for i in range(NB):
        for kt in range(TB * (i + 1)):
            for h in range(G):
                plan.append(("score", i, kt, h))
                slot = begin[i] + G * kt + h + 1
                if nxt < NB:
                    upto = len(ahead) * (slot + lead - begin[nxt - 1]) // (begin[nxt] - begin[nxt - 1])
                    plan += ahead[done:upto]
                    done = upto
                    if done == len(ahead):
                        plan.append(("rows", nxt))
                        nxt += 1
                        ahead, done = maxima(nxt) if nxt < NB else [], 0
                left = begin[i + 1] - slot
                if i + 1 < NB and left < G + 1 and left > 0:
                    plan.append(("turn", i + 1, G - left))
                if h == 0 and len(waiting) >= 2:
                    plan += waiting.pop(0)
            waiting.append([("pv", i, kt)] + ([("out", i)] if kt == TB * (i + 1) - 1 else []))
            if i and kt == 2:
                plan.append(("den", i - 1))
            if i and kt == 4:
                plan += [("proj", i - 1, half) for half in range(2)]
    for left in waiting:
        plan += left
    last = NB - 1
    return plan + [("den", last), ("proj", last, 0), ("proj", last, 1)]


def attention_stage(nc, m, w_out, values):
    name = "attn"
    plan = attention_plan()
    max_unit = {ev: n for n, ev in enumerate(e for e in plan if e[0] == "max")}
    act_unit = {ev: n for n, ev in enumerate(e for e in plan if e[0] in ("score", "turn"))}
    ps_unit = {ev: n for n, ev in enumerate(e for e in plan if e in max_unit or e in act_unit)}
    ps_user = list(ps_unit)
    ktg = {(i, kt): n for n, (i, kt) in enumerate((i, kt) for i in range(NB) for kt in range(TB * (i + 1)))}
    QR = 3
    PR = 3
    SR = 6
    with ExitStack() as ctx:
        def sb(n, shape, dt=F32):
            return ctx.enter_context(nc.sbuf_tensor(f"{name}_{n}", shape, dt))

        def ps(n, shape):
            return ctx.enter_context(nc.psum_tensor(f"{name}_{n}", shape, F32))

        K = sb("K", [STACK + 2, G, T], BF16)
        Q = [sb(f"Q{i}", [STACK + 2, G, QB], BF16) for i in range(QR)]
        V = sb("V", [P, NT, G, 32])
        prob = sb("prob", [P, PR, G, QB])
        pmax = sb("pmax", [P, 2, TB * G, NB])
        mx, low = sb("mx", [P, TB * G]), sb("low", [P, TB * G])
        rows = sb("rows", [P, 2, TB * G, 2], BF16)
        oT = sb("oT", [P, 2, QB])
        rden, aT = sb("rden", [P, QB]), sb("aT", [P, QB])
        wo = sb("wo", [P, NG, D])
        spread = sb("spread", [P, P])
        identb = sb("identb", [P, P], BF16)
        mask_q = sb("mask_q", [P, P], BF16)
        mask_k = sb("mask_k", [P, P], BF16)
        psS = ps("psS", [P, SR, QB])
        psO = ps("psO", [P, QB])
        psM = ps("psM", [P, QB])

        with stage(nc, name + "_prep", "filled made wo_in") as (block, s):
            @block.gpsimd
            def _(pool):
                for ap, v in ((wo[:], 0.0), (V[:], 0.0), (spread[:], 0.0),
                              (mask_q[:], 0.0), (mask_k[:], 0.0)):
                    pool.memset(ap, v).then_inc(s.filled, 1)
                pool.wait_ge(s.filled, 5)
                pool.memset(V[:, :, :, DH:DH + 1], 1.0).then_inc(s.made, 1)
                pool.affine_select(out=mask_q[:], in_=mask_q[:], compare_op=ALU.is_ge, fill=FAR_BELOW, base=0,
                                   pattern=[[-1, P]], channel_multiplier=1).then_inc(s.made, 1)
                pool.affine_select(out=mask_k[:], in_=mask_k[:], compare_op=ALU.is_ge, fill=FAR_BELOW, base=0,
                                   pattern=[[1, P]], channel_multiplier=-1).then_inc(s.made, 1)
                pool.affine_select(out=spread[:].rearrange("p (h r) -> p h r", h=G),
                                   in_=spread[:].rearrange("p (h r) -> p h r", h=G),
                                   compare_op=ALU.not_equal, fill=1.0, base=-DH,
                                   pattern=[[-32, G], [0, 32]], channel_multiplier=1).then_inc(s.made, 1)

            @block.vector
            def _(dve):
                nc.vector.tensor_copy(identb[:], m.ident[:]).then_inc(s.made, 1)
                nc.vector.memset(K[STACK:STACK + 2, 0:G // 2], 1.0).then_inc(s.made, 1)

            @block.scalar
            def _(act):
                nc.scalar.copy(K[STACK:STACK + 2, G // 2:].rearrange("p h n -> p (h n)"),
                               bc(m.ones[STACK:STACK + 2, 0:1], [2, (G - G // 2) * T])).then_inc(s.made, 1)

            @block.sync
            def _(sp):
                sp.wait_ge(s.filled, 1)
                for h in range(G):
                    sp.dma_start(wo[32 * h:32 * h + DH],
                                 w_out.rearrange("(g h d) n -> h d g n", g=NG, h=G)[h]).then_inc(s.wo_in, 16)
                sp.wait_ge(s.wo_in, 16 * G)

        with nc.Fori(0, NG) as g:
            names = " ".join(f"k_in{i}" for i in range(NB))
            with stage(nc, name, names + " q_in0 q_in1 q_in2 v_in s_ready s_used rows_step rows_ready st_ready st_done "
                                         "pv_done out_done den_ready recip_done mul_done proj_ready added")                    as (block, s):
                k_in = s[0:NB]
                q_in = (s.q_in0, s.q_in1, s.q_in2)

                def key_cols(i, kt):
                    return max(0, kt - TB * i) * P

                @block.sync
                def _(sp):
                    for i in range(NB):
                        cols = slice(i * QB, (i + 1) * QB)
                        load_stack(sp, m, 1, (g * G, G), K_PART, cols, K[0:STACK, :, cols], k_in[i])
                        if i >= QR:
                            sp.wait_ge(s.st_ready, act_unit["score", i - QR, TB * (i - QR + 1) - 1, G - 1] + 1)
                        load_stack(sp, m, 0, (g * G, G), Q_PART, cols, Q[i % QR][0:STACK], q_in[i % QR])

                @block.gpsimd
                def _(pool):
                    for i in range(NB):
                        tiles = slice(i * TB, (i + 1) * TB)
                        for h in range(G):
                            nc.gpsimd.tensor_copy(V[:, tiles, h, 0:DH],
                                                  values[:, tiles, bass.ds(g * G + h, 1), :]
                                                  .rearrange("p t a d -> p t (a d)")).then_inc(s.v_in, 1)
                    for i in range(NB):
                        pool.wait_ge(s.recip_done, i + 1)
                        if i:
                            pool.wait_ge(s.proj_ready, 2 * i)
                        nc.gpsimd.tensor_tensor(aT[:], oT[:, i % 2, :], rden[:], ALU.mult).then_inc(s.mul_done, 1)

                @block.tensor
                def _(pe):
                    for ev in plan:
                        kind, i = ev[0:2]
                        if ev in ps_unit:
                            u = ps_unit[ev]
                            before = ps_user[u - SR] if u >= SR else None
                            if before in max_unit:
                                pe.wait_ge(s.s_used, max_unit[before] + 1)
                            elif before in act_unit:
                                pe.wait_ge(s.st_done, act_unit[before] + 1)
                        if kind == "max":
                            _, i, qt, h, c = ev
                            if (qt, h, c) == (0, 0, 0):
                                pe.wait_ge(q_in[i % QR], STACK_LOADS * (i // QR + 1))
                                pe.wait_ge(k_in[i], STACK_LOADS)
                            n = QB if c < i else (qt + 1) * P
                            diagonal = c == i
                            mm = nc.tensor.matmul(psS[:, u % SR, 0:n], Q[i % QR][0:STACK, h, qt * P:(qt + 1) * P],
                                                  K[0:STACK, h, c * QB:c * QB + n], start=True, stop=not diagonal,
                                                  skip_group_check=True)
                            if diagonal:
                                mm = nc.tensor.matmul(psS[:, u % SR, n - P:n], identb[:], mask_q[:],
                                                      start=False, stop=True, skip_group_check=True)
                            mm.then_inc(s.s_ready, 1)
                        elif kind == "turn":
                            h = ev[2]
                            pe.wait_ge(s.rows_ready, i + 1)
                            for qt in range(TB):
                                mm = nc.tensor.matmul(psS[STACK:STACK + 2, u % SR, qt * P:(qt + 1) * P],
                                                      rows[:, i % 2, qt * G + h, :], identb[:],
                                                      start=True, stop=True)
                            mm.then_inc(s.st_ready, 1)
                        elif kind == "score":
                            _, i, kt, h = ev
                            if kt == 0:
                                pe.wait_ge(s.st_done, act_unit["turn", i, h] + 1)
                            q0 = key_cols(i, kt)
                            diagonal = kt >= TB * i
                            mm = nc.tensor.matmul(psS[:, u % SR, q0:QB], K[:, h, kt * P:(kt + 1) * P],
                                                  Q[i % QR][:, h, q0:QB], start=True, stop=not diagonal,
                                                  skip_group_check=True)
                            if diagonal:
                                mm = nc.tensor.matmul(psS[:, u % SR, q0:q0 + P], identb[:], mask_k[:],
                                                      start=False, stop=True, skip_group_check=True)
                            mm.then_inc(s.st_ready, 1)
                        elif kind == "pv":
                            _, i, kt = ev
                            n = ktg[i, kt]
                            pe.wait_ge(s.st_done, act_unit["score", i, kt, G - 1] + 1)
                            if kt == 0 and i:
                                pe.wait_ge(s.out_done, i)
                            if kt >= TB * i:
                                pe.wait_ge(s.v_in, G * (i + 1))
                            q0 = key_cols(i, kt)
                            for h in range(G):
                                mm = nc.tensor.matmul(psO[32 * h:32 * h + 32, q0:QB], V[:, kt, h, :],
                                                      prob[:, n % PR, h, q0:QB], start=(kt == 0),
                                                      stop=(kt == TB * (i + 1) - 1), skip_group_check=True)
                            mm.then_inc(s.pv_done, 1)
                        elif kind == "den":
                            pe.wait_ge(s.out_done, i + 1)
                            if i:
                                pe.wait_ge(s.added, 2 * i)
                            nc.tensor.matmul(psM[:], spread[:], oT[:, i % 2, :], start=True, stop=True)\
                                .then_inc(s.den_ready, 1)
                        elif kind == "proj":
                            half = ev[2]
                            pe.wait_ge(s.mul_done, i + 1)
                            if half:
                                pe.wait_ge(s.added, 2 * i + 1)
                            for j in range(2):
                                t = half * 2 + j
                                mm = nc.tensor.matmul(psM[:, j * D:(j + 1) * D], aT[:, t * P:(t + 1) * P],
                                                      wo[:, g, :], start=True, stop=True)
                            mm.then_inc(s.proj_ready, 1)

                @block.scalar
                def _(act):
                    for ev in plan:
                        kind, i = ev[0:2]
                        if kind == "score":
                            _, i, kt, h = ev
                            k = ktg[i, kt]
                            n = act_unit[ev]
                            act.wait_ge(s.st_ready, n + 1)
                            if k >= PR and h == 0:
                                act.wait_ge(s.pv_done, k - PR + 1)
                            q0 = key_cols(i, kt)
                            nc.scalar.activation(prob[:, k % PR, h, q0:QB], psS[:, ps_unit[ev] % SR, q0:QB], ACT.Exp,
                                                 scale=DH ** -0.5).then_inc(s.st_done, 1)
                        elif kind == "turn":
                            n = act_unit[ev]
                            act.wait_ge(s.st_ready, n + 1)
                            nc.scalar.copy(Q[i % QR][STACK:STACK + 2, ev[2], :], psS[STACK:STACK + 2, ps_unit[ev] % SR, :])\
                                .then_inc(s.st_done, 1)
                        elif kind == "out":
                            act.wait_ge(s.pv_done, ktg[i, TB * (i + 1) - 1] + 1)
                            if i >= 2:
                                act.wait_ge(s.mul_done, i - 1)
                            nc.scalar.copy(oT[:, i % 2, :], psO[:]).then_inc(s.out_done, 1)

                @block.vector
                def _(dve):
                    for ev in plan:
                        kind, i = ev[0:2]
                        if kind == "max":
                            _, i, qt, h, c = ev
                            u = ps_unit[ev]
                            n = QB if c < i else (qt + 1) * P
                            dve.wait_ge(s.s_ready, max_unit[ev] + 1)
                            nc.vector.tensor_reduce(pmax[:, i % 2, qt * G + h, c:c + 1], psS[:, u % SR, 0:n],
                                                    AX.X, ALU.max).then_inc(s.s_used, 1)
                        elif kind == "rows":
                            dve.wait_ge(s.s_used, max_unit["max", i, TB - 1, G - 1, i] + 1)
                            nc.vector.tensor_reduce(mx[:], pmax[:, i % 2, :, 0:i + 1], AX.X, ALU.max)\
                                .then_inc(s.rows_step, 1)
                            dve.wait_ge(s.rows_step, 3 * i + 1)
                            nc.vector.tensor_scalar(rows[:, i % 2, :, 0], mx[:], -1.0, None, ALU.mult)\
                                .then_inc(s.rows_step, 1)
                            dve.wait_ge(s.rows_step, 3 * i + 2)
                            nc.vector.tensor_tensor(low[:], mx[:], rows[:, i % 2, :, 0], ALU.add)\
                                .then_inc(s.rows_step, 1)
                            dve.wait_ge(s.rows_step, 3 * i + 3)
                            nc.vector.tensor_scalar(rows[:, i % 2, :, 1], low[:], -1.0, None, ALU.mult)\
                                .then_inc(s.rows_ready, 1)
                        elif kind == "den":
                            dve.wait_ge(s.den_ready, i + 1)
                            if i:
                                dve.wait_ge(s.mul_done, i)
                            nc.vector.reciprocal(rden[:], psM[:]).then_inc(s.recip_done, 1)
                        elif kind == "proj":
                            half = ev[2]
                            dve.wait_ge(s.proj_ready, 2 * i + half + 1)
                            t = i * TB + half * 2
                            nc.vector.tensor_tensor(m.x[:, t:t + 2, :], psM[:].rearrange("p (t d) -> p t d", t=2),
                                                    m.x[:, t:t + 2, :], ALU.add).then_inc(s.added, 1)


def causal(nc, m, i):
    with ExitStack() as ctx:
        values = ctx.enter_context(nc.sbuf_tensor("causal_values", [P, NT, H, DH], F32))
        norm_and_values_stage(nc, m, "causal_norm", i["L1_attn_WV"], values)
        split_stage(nc, m, "causal_split", (i["L1_attn_WQ"], i["L1_attn_WK"]))
        attention_stage(nc, m, i["L1_attn_WO"], values)



MF = 64
PAIRS = H // 2
VW = DH + 1


def favor_stage(nc, m, projT, values, out_w, out_b, stats, out_stats):
    name = "favor"
    LB = 2 * P
    BODY = 4
    with ExitStack() as ctx:
        def sb(n, shape, dt=F32):
            return ctx.enter_context(nc.sbuf_tensor(f"{name}_{n}", shape, dt))

        def ps(n, shape):
            return ctx.enter_context(nc.psum_tensor(f"{name}_{n}", shape, F32))

        R = STACK + 3
        qs = [sb(f"qs{i}", [R, H, LB], BF16) for i in range(2)]
        ks = [sb(f"ks{i}", [R, H, LB], BF16) for i in range(2)]
        fw = sb("fw", [R, MF], BF16)
        pt, pr = sb("pt", [DH, MF]), sb("pr", [DH, MF])
        pp = sb("pp", [DH, 3, MF], BF16)
        qfT = sb("qfT", [P, 2, PAIRS, P])
        kfT = sb("kfT", [P, 2, PAIRS, P])
        kf = sb("kf", [P, 2, H, MF])
        a = sb("a", [P, H, P])
        mask = sb("mask", [P, P])
        vt = sb("vt", [P, 2, H, 32])
        state = sb("state", [P, 2, H, 32])
        oT, rden, aT = sb("oT", [P, 4 * P]), sb("rden", [P, 4 * P]), sb("aT", [P, 4 * P])
        wo = sb("wo", [P, H // 4, D])
        spread = sb("spread", [P, P])
        ob, xb = sb("ob", [P, D]), sb("xb", [P, 2, D])
        mean, rstd = stats
        psF = ps("psF", [P, 3, 512])
        psA = ps("psA", [P, 2, 4, P])
        psN = ps("psN", [P, 4, P])
        psD = ps("psD", [P, 512])
        psM = ps("psM", [P, 512])

        with stage(nc, name + "_prep", "p_in step moved filled made w_in") as (block, s):
            @block.sync
            def _(sp):
                sp.dma_start(pt[:], projT).then_inc(s.p_in, 16)
                sp.wait_ge(s.step, 5)
                for r, part in enumerate(K_PART):
                    sp.dma_start(fw[r * DH:(r + 1) * DH, :], pp[:, part, :]).then_inc(s.moved, 16)
                sp.dma_start(ob[:], out_b.partition_broadcast(P)).then_inc(s.w_in, 16)
                sp.wait_ge(s.filled, 1)
                for h in range(4):
                    sp.dma_start(wo[32 * h:32 * h + DH],
                                 out_w.rearrange("(g h d) n -> h d g n", g=H // 4, h=4)[h]).then_inc(s.w_in, 16)
                sp.wait_ge(s.moved, 16 * len(K_PART))
                sp.wait_ge(s.w_in, 16 * 5)

            @block.gpsimd
            def _(pool):
                for ap, v in ((wo[:], 0.0), (mask[:], 1.0), (state[:], 0.0), (vt[:], 0.0), (spread[:], 0.0)):
                    pool.memset(ap, v).then_inc(s.filled, 1)
                pool.wait_ge(s.filled, 5)
                pool.memset(vt[:, :, :, DH:DH + 1], 1.0).then_inc(s.made, 1)
                pool.affine_select(out=mask[:], in_=mask[:], compare_op=ALU.is_ge, fill=0.0, base=0,
                                   pattern=[[1, P]], channel_multiplier=-1).then_inc(s.made, 1)
                pool.affine_select(out=spread[:].rearrange("p (h r) -> p h r", h=4),
                                   in_=spread[:].rearrange("p (h r) -> p h r", h=4),
                                   compare_op=ALU.not_equal, fill=1.0, base=-DH,
                                   pattern=[[-32, 4], [0, 32]], channel_multiplier=1).then_inc(s.made, 1)

            @block.vector
            def _(dve):
                link = Steps(dve, s.step)
                dve.wait_ge(s.p_in, 16)
                link(nc.vector.tensor_scalar(pt[:], pt[:], DH ** -0.5, None, ALU.mult))
                link(nc.vector.tensor_copy(pp[:, 0, :], pt[:]))
                link(nc.vector.tensor_tensor(pr[:], pt[:], pp[:, 0, :], ALU.subtract))
                link(nc.vector.tensor_copy(pp[:, 1, :], pr[:]))
                link(nc.vector.tensor_tensor(pp[:, 2, :], pr[:], pp[:, 1, :], ALU.subtract))
                nc.vector.memset(fw[STACK:STACK + 3, :], -1.0).then_inc(s.made, 1)

        with stage(nc, name, "in0 in1 f_ready f_exp a_ready a_masked d_ready d_added num_ready v_moved o_out "
                             "den_ready recip_done mul_done proj_ready normed based added stats") as (block, s):
            stacks_in = (s.in0, s.in1)
            per_load = 2 * (STACK_LOADS + 16)

            @block.sync
            def _(sp):
                def loads(blk, i):
                    cols = bass.ds(blk * LB, LB)
                    for which, dst in ((0, qs), (1, ks)):
                        load_stack(sp, m, which, (0, H), Q_PART, cols, dst[i], stacks_in[i])
                        sp.dma_start(dst[i][STACK:], m.norms[which, :, :, cols]
                                     .rearrange("h r n -> r h n")).then_inc(stacks_in[i], 16)

                loads(0, 0)
                loads(1, 1)
                with sp.Fori(1, NT // BODY) as turn:
                    for i in range(2):
                        sp.wait_ge(s.f_ready, turn * (6 * BODY) - (6 * BODY - 12 * (i + 1)))
                        loads(turn * 2 + i, i)

            @block.tensor
            def _(pe):
                pe.sem_inc(s.f_exp, 3)
                pe.sem_inc(s.a_masked, 2)
                pe.sem_inc(s.num_ready, 2)
                pe.sem_inc(s.d_added, 2)
                pe.sem_inc(s.added, 2)

                def features(t, j, u):
                    pe.wait_ge(s.f_exp, t * 6 + (u + 1))
                    half, kind = u // 3, u % 3
                    cols = slice((j % 2) * P, (j % 2 + 1) * P)
                    for n in range(4 if kind < 2 else 8):
                        if kind < 2:
                            src = (qs, ks)[kind][j // 2]
                            for b in range(2):
                                last = nc.tensor.matmul(psF[64 * b:64 * b + 64, u % 3, n * P:(n + 1) * P], fw[:],
                                                        src[:, 2 * (4 * half + n) + b, cols], start=True, stop=True)
                        else:
                            last = nc.tensor.matmul(psF[:, u % 3, n * MF:(n + 1) * MF],
                                                    ks[j // 2][:, 8 * half + n, cols], fw[:], start=True, stop=True)
                    last.then_inc(s.f_ready, 1)

                def products(t, j, half):
                    pe.wait_ge(s.f_exp, t * 6 + (3 * half + 2 + 3))
                    pe.wait_ge(s.a_masked, t * 4 + (2 * half + 2))
                    for n in range(4):
                        for b in range(2):
                            rows = slice(64 * b, 64 * b + 64)
                            last = nc.tensor.matmul(psA[:, b, n, :], kfT[rows, j % 2, 4 * half + n, :],
                                                    qfT[rows, j % 2, 4 * half + n, :], start=True, stop=True)
                            if n == 3:
                                last.then_inc(s.a_ready, 1)

                def tile_sums(t, j):
                    pe.wait_ge(s.f_exp, t * 6 + (6 + 3))
                    pe.wait_ge(s.d_added, t * 2 + 2)
                    pe.wait_ge(s.v_moved, t + 1)
                    for p in range(PAIRS):
                        last = nc.tensor.matmul(psD[:, p * 2 * VW:(p + 1) * 2 * VW], kf[:, j % 2, 2 * p:2 * p + 2, :],
                                                vt[:, j % 2, 2 * p:2 * p + 2, 0:VW], start=True, stop=True)
                    last.then_inc(s.d_ready, 1)

                def outputs(t, j):
                    pe.wait_ge(s.a_masked, t * 4 + 6)
                    for h in range(H):
                        nc.tensor.matmul(psN[32 * (h % 4):32 * (h % 4) + 32, h // 4, :], vt[:, j % 2, h, :],
                                         a[:, h, :], start=(h < 4), stop=False, skip_group_check=True)
                    for h in range(H):
                        last = nc.tensor.matmul(psN[32 * (h % 4):32 * (h % 4) + 32, h // 4, :],
                                                state[:, j % 2, h, :], qfT[:, j % 2, h // 2, :],
                                                start=False, stop=True, skip_group_check=True)
                    last.then_inc(s.num_ready, 1)

                def divisors(t):
                    pe.wait_ge(s.o_out, t + 1)
                    pe.wait_ge(s.added, t + 2)
                    nc.tensor.matmul(psM[:], spread[:], oT[:], start=True, stop=True).then_inc(s.den_ready, 1)

                def projection(t):
                    pe.wait_ge(s.mul_done, t + 1)
                    for g in range(4):
                        last = nc.tensor.matmul(psM[:, 0:D], aT[:, g * P:(g + 1) * P], wo[:, g, :],
                                                start=(g == 0), stop=(g == 3))
                    last.then_inc(s.proj_ready, 1)

                def tile(turn, j, first, last):
                    t = turn * BODY + j
                    following = (j + 1) % BODY

                    def next_features(u):
                        if not last:
                            features(t + 1, following, u)

                    if not last and following % 2 == 0:
                        pe.wait_ge(stacks_in[following // 2], (turn + (j + 1) // BODY) * per_load + per_load)
                    next_features(0)
                    products(t, j, 0)
                    if not first:
                        divisors(t - 1)
                    next_features(1)
                    next_features(2)
                    products(t, j, 1)
                    next_features(3)
                    tile_sums(t, j)
                    next_features(4)
                    next_features(5)
                    if not first:
                        projection(t - 1)
                    outputs(t, j)

                pe.wait_ge(stacks_in[0], per_load)
                for u in range(6):
                    features(0, 0, u)
                for j in range(BODY):
                    tile(0, j, j == 0, False)
                with pe.Fori(1, NT // BODY - 1) as turn:
                    for j in range(BODY):
                        tile(turn, j, False, False)
                for j in range(BODY):
                    tile(NT // BODY - 1, j, False, j == BODY - 1)
                divisors(NT - 1)
                projection(NT - 1)

            @block.scalar
            def _(act):
                def outputs_out(t):
                    act.wait_ge(s.num_ready, t + 3)
                    nc.scalar.copy(oT[:], psN[:].rearrange("p g n -> p (g n)")).then_inc(s.o_out, 1)

                def tiles(turn, first):
                    for j in range(BODY):
                        t = turn * BODY + j
                        for u in range(6):
                            half, kind = u // 3, u % 3
                            act.wait_ge(s.f_ready, t * 6 + (u + 1))
                            if u == 0:
                                act.wait_ge(s.num_ready, t + 1)
                            dst = (qfT, kfT)[kind][:, j % 2, 4 * half:4 * half + 4, :] if kind < 2 else \
                                kf[:, j % 2, 8 * half:8 * half + 8, :]
                            nc.scalar.activation(dst, psF[:, u % 3, :].rearrange(
                                "p (a b) -> p a b", a=4 if kind < 2 else 8), ACT.Exp).then_inc(s.f_exp, 1)
                        if j or not first:
                            outputs_out(t - 1)

                tiles(0, True)
                with act.Fori(1, NT // BODY) as turn:
                    tiles(turn, False)
                outputs_out(NT - 1)

            @block.gpsimd
            def _(pool):
                def values_in(t, j):
                    pool.wait_ge(s.num_ready, t + 1)
                    nc.gpsimd.tensor_copy(vt[:, j % 2, :, 0:DH], values[:, t, :, :]).then_inc(s.v_moved, 1)

                def divided(t, j):
                    pool.wait_ge(s.recip_done, t + 1)
                    nc.gpsimd.tensor_tensor(aT[:], oT[:], rden[:], ALU.mult).then_inc(s.mul_done, 1)
                    pool.wait_ge(s.normed, t + 1)
                    nc.gpsimd.tensor_tensor(xb[:, j % 2, :], xb[:, j % 2, :], ob[:], ALU.add).then_inc(s.based, 1)

                def tiles(turn, first):
                    for j in range(BODY):
                        t = turn * BODY + j
                        values_in(t, j)
                        if j or not first:
                            divided(t - 1, j - 1)

                tiles(0, True)
                with pool.Fori(1, NT // BODY) as turn:
                    tiles(turn, False)
                divided(NT - 1, NT - 1)

            @block.vector
            def _(dve):
                def divisors(t, j):
                    dve.wait_ge(s.den_ready, t + 1)
                    nc.vector.reciprocal(rden[:], psM[:]).then_inc(s.recip_done, 1)
                    dve.wait_ge(s.added, t + 1)
                    nc.vector.tensor_scalar(xb[:, j % 2, :], m.x[:, t, :], mean[:, bass.ds(t, 1)],
                                            rstd[:, bass.ds(t, 1)], ALU.subtract, ALU.mult).then_inc(s.normed, 1)

                def statistics(t):
                    dve.wait_ge(s.added, t + 3)
                    nc.vector.bn_stats(out_stats[:, t, :], m.xn[:, t, :]).then_inc(s.stats, 1)

                def added(t, j, first=False):
                    if not first:
                        statistics(t - 1)
                    dve.wait_ge(s.proj_ready, t + 1)
                    dve.wait_ge(s.based, t + 1)
                    nc.vector.tensor_tensor(m.xn[:, t, :], psM[:, 0:D], xb[:, j % 2, :], ALU.add)\
                        .then_inc(s.added, 1)

                def turns(turn, first):
                    for j in range(BODY):
                        t = turn * BODY + j
                        dve.wait_ge(s.num_ready, t + 2)
                        for half in range(2):
                            for b in range(2):
                                dve.wait_ge(s.a_ready, t * 4 + (2 * half + b + 1))
                                nc.vector.tensor_tensor(a[:, 8 * half + b:8 * half + 8:2, :], psA[:, b],
                                                        bc(mask[:].unsqueeze(1), [P, 4, P]), ALU.mult)\
                                    .then_inc(s.a_masked, 1)
                            if half == 0 and (j or not first):
                                divisors(t - 1, j - 1)
                        dve.wait_ge(s.d_ready, t + 1)
                        for b in range(2):
                            rows, cols = slice(64 * b, 64 * b + 64), slice(VW * b, VW * b + VW)
                            nc.vector.tensor_tensor(state[rows, (j + 1) % 2, b::2, 0:VW], state[rows, j % 2, b::2, 0:VW],
                                                    psD[rows, 0:PAIRS * 2 * VW].rearrange(
                                                        "p (a b) -> p a b", a=PAIRS)[:, :, cols],
                                                    ALU.add).then_inc(s.d_added, 1)
                        if j or not first:
                            added(t - 1, j - 1, first and j == 1)

                turns(0, True)
                with dve.Fori(1, NT // BODY) as turn:
                    turns(turn, False)
                divisors(NT - 1, NT - 1)
                added(NT - 1, NT - 1)
                statistics(NT - 1)


def favor_norm_stage(nc, m, gamma_dram, beta_dram, out_stats):
    name = "favor_norm"
    YR = 4
    with ExitStack() as ctx:
        def sb(n, shape, dt=F32):
            return ctx.enter_context(nc.sbuf_tensor(f"{name}_{n}", shape, dt))

        b = norm_buffers(nc, ctx, name)._replace(stats=out_stats)
        gamma, beta, y = sb("gamma", [P, D]), sb("beta", [P, D]), sb("y", [P, YR, D])
        with stage(nc, name, "w_in stat_step var_ready root_ready scaled based added") as (block, s):
            @block.sync
            def _(sp):
                sp.dma_start(gamma[:], gamma_dram.partition_broadcast(P)).then_inc(s.w_in, 16)
                sp.dma_start(beta[:], beta_dram.partition_broadcast(P)).then_inc(s.w_in, 16)

            @block.scalar
            def _(act):
                act.wait_ge(s.var_ready, 1)
                nc.scalar.activation(b.rstd[:], b.t1[:], ACT.Sqrt).then_inc(s.root_ready, 1)

            @block.gpsimd
            def _(pool):
                pool.wait_ge(s.w_in, 32)
                with pool.Fori(0, NT // YR) as g:
                    for j in range(YR):
                        t = g * YR + j
                        nc.gpsimd.tensor_tensor(m.x[:, t, :], m.x[:, t, :], beta[:], ALU.add).then_inc(s.based, 1)

            @block.vector
            def _(dve):
                norm_statistics(nc, dve, s, m, b, eps=1e-6, gathered=True)
                dve.wait_ge(s.w_in, 32)
                dve.sem_inc(s.added, YR)
                with dve.Fori(0, NT // YR) as g:
                    for j in range(YR):
                        t = g * YR + j
                        dve.wait_ge(s.added, t + 1)
                        nc.vector.scalar_tensor_tensor(out=y[:, j, :], in0=m.xn[:, t, :],
                                                       scalar=b.mean[:, bass.ds(t, 1)], in1=gamma[:],
                                                       op0=ALU.subtract, op1=ALU.mult).then_inc(s.scaled, 1)
                    for j in range(YR):
                        t = g * YR + j
                        dve.wait_ge(s.scaled, t + 1)
                        dve.wait_ge(s.based, t + 1)
                        nc.vector.scalar_tensor_tensor(out=m.x[:, t, :], in0=y[:, j, :],
                                                       scalar=b.rstd[:, bass.ds(t, 1)], in1=m.x[:, t, :],
                                                       op0=ALU.mult, op1=ALU.add).then_inc(s.added, 1)


def favor(nc, m, i):
    with ExitStack() as ctx:
        mean = ctx.enter_context(nc.sbuf_tensor("favor_mean", [P, NT], F32))
        rstd = ctx.enter_context(nc.sbuf_tensor("favor_rstd", [P, NT], F32))
        out_stats = ctx.enter_context(nc.sbuf_tensor("favor_out_stats", [P, NT, 6], F32))
        with nc.sbuf_tensor("favor_values", [P, NT, H, DH], F32) as values:
            norm_and_values_stage(nc, m, "favor_in", i["L0_attn_v_w"], values, i["L0_attn_v_b"], (mean, rstd))
            split_stage(nc, m, "favor_split", (i["L0_attn_q_w"], i["L0_attn_k_w"]),
                        (i["L0_attn_q_b"], i["L0_attn_k_b"]))
            favor_stage(nc, m, i["L0_attn_proj"], values, i["L0_attn_out_w"], i["L0_attn_out_b"], (mean, rstd),
                        out_stats)
        favor_norm_stage(nc, m, i["L0_attn_gamma"], i["L0_attn_beta"], out_stats)



Ffn = namedtuple("Ffn", "name router router_b up up_b down down_b")
STAGES = (0, 1, 2, 3, 4, 5)


def build(nc, i, out):
    with ExitStack() as ctx:
        m = make_constants(nc, ctx)
        m.tokens = nc.dram_tensor("tokens", [T, D], F32).ap()
        m.outs = nc.dram_tensor("expert_outs", [2 * T, D], F32).ap()
        m.parts = nc.dram_tensor("qk_parts", [2, 3, D, T], BF16).ap()
        m.norms = nc.dram_tensor("qk_norms", [2, H, 3, T], BF16).ap()
        constants_stage(nc, m)

        def switch(name, x_in=None):
            ffn(nc, m, Ffn(name=name, router=i["L0_ffn_w_switch"], router_b=i["L0_ffn_b_switch"],
                                       up=[i["L0_ffn_w1"]], up_b=i["L0_ffn_b1"], down=i["L0_ffn_w2"],
                                       down_b=i["L0_ffn_b2"]), False, x_in=x_in)

        def top2(name, out=None):
            ffn(nc, m, Ffn(name=name, router=i["L1_ffn_router_w"], router_b=None,
                             up=[i["L1_ffn_wg"], i["L1_ffn_wu"]], up_b=None, down=i["L1_ffn_wd"],
                             down_b=None), True, out=out)

        parts = [lambda: switch("switch_a", i["L0_attn_x"]), lambda: favor(nc, m, i), lambda: switch("switch_b"),
                 lambda: top2("top2_a"), lambda: causal(nc, m, i), lambda: top2("top2_b", out)]
        for n in STAGES:
            parts[n]()


_TURNED = ("L1_ffn_router_w", "L1_attn_WQ", "L1_attn_WK", "L1_attn_WV", "L1_attn_WO", "L0_attn_proj")


def kernel(**inputs):
    import numpy as _np
    import concourse.bacc as _bacc
    from concourse import mybir as _mybir
    from concourse.bass_utils import run_bass_kernel_spmd as _run

    nc = _bacc.Bacc("TRN2", target_bir_lowering=False, num_devices=1)
    arrays, aps = {}, {}
    for name, value in inputs.items():
        a = _np.asarray(value)
        a = _np.ascontiguousarray(a.T if name in _TURNED else a)
        arrays[f"in_{name}"] = a
        aps[name] = nc.dram_tensor(f"in_{name}", a.shape, _mybir.dt.from_np(a.dtype), kind="ExternalInput").ap()
    out = nc.dram_tensor("out", (1, T, D), _mybir.dt.float32, kind="ExternalOutput").ap()
    build(nc, aps, out)
    return _run(nc, [arrays], core_ids=[0]).results[0]["out"]
```
